# Optimizing a Trainium2 kernel written in Bass

```python
import numpy as np
import jax
import jax.numpy as jnp

def _softmax(x, axis=-1):
    return jax.nn.softmax(x, axis=axis)

def _gelu(x):
    return jax.nn.gelu(x, approximate=True)

def _silu(x):
    return jax.nn.silu(x)

def _sigmoid(x):
    return jax.nn.sigmoid(x)

def _layernorm(x, axis=-1, eps=1e-05):
    m = jnp.mean(x, axis=axis, keepdims=True)
    v = jnp.var(x, axis=axis, keepdims=True)
    return (x - m) / jnp.sqrt(v + eps)

def _scatter_add(tgt, idx, src, axis=0):
    return tgt.at[idx].add(src)

def _segment_sum(src, seg, n):
    return jax.ops.segment_sum(src, seg, n)
kernel_name = 'mk_adaln_ffn_d2_seqx_r8_6ee376'

def setup_inputs(seed: int=0):
    np.random.seed(seed)
    _w = jnp.asarray

    def _rec_inputs():
        import jax
        import jax.numpy as jnp
        _rk = jax.random.key(seed)
        x = 0.0001212 + 1 * jax.random.normal(jax.random.fold_in(_rk, 1), (32, 128, 128), jnp.float32)
        _lenS = 128 - jax.random.randint(jax.random.fold_in(_rk, 7), (32,), 0, max(1, 128 // 4) + 1, jnp.int32)
        _lenS2 = 128 - jax.random.randint(jax.random.fold_in(_rk, 8), (32,), 0, max(1, 128 // 4) + 1, jnp.int32)
        fside_BxS_0 = -0.00499425 + 1.0058 * jax.random.normal(jax.random.fold_in(_rk, 11), (32, 128), jnp.float32)
        cond_1024 = 0.00513981 + 1.0024 * jax.random.normal(jax.random.fold_in(_rk, 12), (32, 128), jnp.float32)
        return (x, fside_BxS_0, cond_1024)
    x, fside_BxS_0, cond_1024 = _rec_inputs()

    def _L0_cond_setup():
        import jax, jax.numpy as jnp
        import numpy as np
        key = jax.random.key(seed)
        k1, k2, k3, k4 = jax.random.split(key, 4)
        B, N_out, N_in = (32, 128, 128)
        x = jax.random.normal(k1, (B, N_in), dtype=jnp.float32)
        y = jax.random.normal(k2, (B, N_out), dtype=jnp.float32)
        w = jax.random.normal(k3, (B, N_out, N_in), dtype=jnp.float32)
        coeffs = jax.random.normal(k4, (3, 3, 3), dtype=jnp.float32) * 0.01
        return {'x': x, 'y': y, 'w': w, 'coeffs': coeffs}
    _L0_cond_all = _L0_cond_setup()
    _L0_cond_in = {k: v for k, v in _L0_cond_all.items() if k in ('coeffs',)}
    del _L0_cond_all

    def _L0_ffn_setup():
        import jax, jax.numpy as jnp
        import numpy as np
        B, S, D, H, E, K = (4, 256, 128, 256, 8, 2)
        TEMP = 5.0
        EPS = 1e-09
        key = jax.random.key(seed)
        k_x, k_wg, k_w1, k_w2 = jax.random.split(key, 4)
        scale = 0.02
        return {'x': jax.random.normal(k_x, (B, S, D), dtype=jnp.float32), 'Wg': jax.random.normal(k_wg, (D, E), dtype=jnp.float32) * scale, 'bg': jnp.zeros((E,), dtype=jnp.float32), 'W1': jax.random.normal(k_w1, (E, D, H), dtype=jnp.float32) * scale, 'b1': jnp.zeros((E, H), dtype=jnp.float32), 'W2': jax.random.normal(k_w2, (E, H, D), dtype=jnp.float32) * scale, 'b2': jnp.zeros((E, D), dtype=jnp.float32)}
    _L0_ffn_all = _L0_ffn_setup()
    _L0_ffn_in = {k: v for k, v in _L0_ffn_all.items() if k in ('Wg', 'bg', 'W1', 'b1', 'W2', 'b2')}
    del _L0_ffn_all

    def _L1_cond_setup():
        import jax, jax.numpy as jnp
        import numpy as np
        N, T, D, H = (128, 64, 128, 128)
        key = jax.random.key(seed)
        k1, k2, k3, k4 = jax.random.split(key, 4)
        x = jax.random.normal(k1, (N, T, D), dtype=jnp.float32)
        h0 = jax.random.normal(k2, (N, H), dtype=jnp.float32)
        Wx = jax.random.normal(k3, (D, H), dtype=jnp.float32) / np.sqrt(D)
        Wh = jax.random.normal(k4, (H, H), dtype=jnp.float32) / np.sqrt(H)
        b = jnp.zeros((H,), dtype=jnp.float32)
        return {'x': x, 'h0': h0, 'Wx': Wx, 'Wh': Wh, 'b': b}
    _L1_cond_all = _L1_cond_setup()
    _L1_cond_in = {k: v for k, v in _L1_cond_all.items() if k in ('Wx', 'Wh', 'b')}
    del _L1_cond_all

    def _L1_ffn_setup():
        import jax, jax.numpy as jnp
        import numpy as np
        EPS = 1e-05
        LN_EPS = 1e-05
        NUM_EXPERTS = 8
        TOP_K = 2
        HIDDEN = 128
        INTER = 256

        def _swiglu(x, wg, wu, wd):
            return jax.nn.silu(x @ wg) * (x @ wu) @ wd
        key = jax.random.key(seed)
        ks = jax.random.split(key, 10)
        B, S, H, I, E = (8, 512, HIDDEN, INTER, NUM_EXPERTS)
        std_h = 1.0 / np.sqrt(H)
        std_i = 1.0 / np.sqrt(I)
        return {'x': jax.random.normal(ks[0], (B, S, H), dtype=jnp.float32), 'ln_scale': jnp.ones((H,), dtype=jnp.float32), 'ln_bias': jnp.zeros((H,), dtype=jnp.float32), 'gate_w': jax.random.normal(ks[1], (E, H), dtype=jnp.float32) * 0.01, 'Wg': jax.random.normal(ks[2], (E, H, I), dtype=jnp.float32) * std_h, 'Wu': jax.random.normal(ks[3], (E, H, I), dtype=jnp.float32) * std_h, 'Wd': jax.random.normal(ks[4], (E, I, H), dtype=jnp.float32) * std_i, 'sWg': jax.random.normal(ks[5], (H, I), dtype=jnp.float32) * std_h, 'sWu': jax.random.normal(ks[6], (H, I), dtype=jnp.float32) * std_h, 'sWd': jax.random.normal(ks[7], (I, H), dtype=jnp.float32) * std_i}
    _L1_ffn_all = _L1_ffn_setup()
    _L1_ffn_in = {k: v for k, v in _L1_ffn_all.items() if k in ('ln_scale', 'ln_bias', 'gate_w', 'Wg', 'Wu', 'Wd', 'sWg', 'sWu', 'sWd')}
    del _L1_ffn_all
    return {'x': x, 'fside_BxS_0': fside_BxS_0, 'cond_1024': cond_1024, 'L0_cond_coeffs': _L0_cond_in['coeffs'], 'L0_ffn_Wg': _L0_ffn_in['Wg'], 'L0_ffn_bg': _L0_ffn_in['bg'], 'L0_ffn_W1': _L0_ffn_in['W1'], 'L0_ffn_b1': _L0_ffn_in['b1'], 'L0_ffn_W2': _L0_ffn_in['W2'], 'L0_ffn_b2': _L0_ffn_in['b2'], 'L1_cond_Wx': _L1_cond_in['Wx'], 'L1_cond_Wh': _L1_cond_in['Wh'], 'L1_cond_b': _L1_cond_in['b'], 'L1_ffn_ln_scale': _L1_ffn_in['ln_scale'], 'L1_ffn_ln_bias': _L1_ffn_in['ln_bias'], 'L1_ffn_gate_w': _L1_ffn_in['gate_w'], 'L1_ffn_Wg': _L1_ffn_in['Wg'], 'L1_ffn_Wu': _L1_ffn_in['Wu'], 'L1_ffn_Wd': _L1_ffn_in['Wd'], 'L1_ffn_sWg': _L1_ffn_in['sWg'], 'L1_ffn_sWu': _L1_ffn_in['sWu'], 'L1_ffn_sWd': _L1_ffn_in['sWd']}

def reference(x, fside_BxS_0, cond_1024, L0_cond_coeffs, L0_ffn_Wg, L0_ffn_bg, L0_ffn_W1, L0_ffn_b1, L0_ffn_W2, L0_ffn_b2, L1_cond_Wx, L1_cond_Wh, L1_cond_b, L1_ffn_ln_scale, L1_ffn_ln_bias, L1_ffn_gate_w, L1_ffn_Wg, L1_ffn_Wu, L1_ffn_Wd, L1_ffn_sWg, L1_ffn_sWu, L1_ffn_sWd):
    import jax
    import jax.numpy as jnp

    def _L0_cond_ref(x, y, w, coeffs):
        import jax, jax.numpy as jnp
        import numpy as np
        X = jnp.stack([jnp.ones_like(x), x, x * x], axis=1)
        Y = jnp.stack([jnp.ones_like(y), y, y * y], axis=1)
        Wp = jnp.stack([jnp.ones_like(w), w, w * w], axis=1)
        dW = jnp.einsum('abc,kaj,kbi,kcij->kij', coeffs, X, Y, Wp)
        return dW

    def _L0_ffn_ref(x, Wg, bg, W1, b1, W2, b2):
        import jax, jax.numpy as jnp
        import numpy as np
        B, S, D, H, E, K = (4, 256, 128, 256, 8, 2)
        TEMP = 5.0
        EPS = 1e-09
        logits = jnp.einsum('bsd,de->bse', x, Wg) + bg
        probs = jax.nn.softmax(logits / TEMP, axis=-1)
        vals, idx = jax.lax.top_k(probs, K)
        onehot = jax.nn.one_hot(idx, E, dtype=x.dtype)
        mask = jnp.einsum('bske,bsk->bse', onehot, vals)
        gates = mask / (jnp.sum(mask, axis=-1, keepdims=True) + EPS)
        h = jax.nn.gelu(jnp.einsum('bsd,edh->besh', x, W1) + b1[None, :, None, :], approximate=False)
        out = jnp.einsum('besh,ehd->besd', h, W2) + b2[None, :, None, :]
        y = jnp.einsum('bse,besd->bsd', gates, out)
        return y

    def _L1_cond_ref(x, h0, Wx, Wh, b):
        import jax, jax.numpy as jnp
        import numpy as np
        N, T, D, H = (128, 64, 128, 128)
        xp = jnp.einsum('ntd,dh->nth', x, Wx) + b

        def step(prev_h, xp_t):
            next_h = jnp.tanh(xp_t + prev_h @ Wh)
            return (next_h, next_h)
        _, h = jax.lax.scan(step, h0, jnp.swapaxes(xp, 0, 1))
        return jnp.swapaxes(h, 0, 1)

    def _L1_ffn_ref(x, ln_scale, ln_bias, gate_w, Wg, Wu, Wd, sWg, sWu, sWd):
        import jax, jax.numpy as jnp
        import numpy as np
        EPS = 1e-05
        LN_EPS = 1e-05
        NUM_EXPERTS = 8
        TOP_K = 2
        HIDDEN = 128
        INTER = 256

        def _swiglu(x, wg, wu, wd):
            return jax.nn.silu(x @ wg) * (x @ wu) @ wd
        B, S, H = x.shape
        xf = x.reshape(-1, H)
        mu = jnp.mean(xf, axis=-1, keepdims=True)
        var = jnp.var(xf, axis=-1, keepdims=True)
        xn = (xf - mu) * jax.lax.rsqrt(var + LN_EPS) * ln_scale + ln_bias
        logits = xn @ gate_w.T
        probs = jax.nn.softmax(logits, axis=-1)
        tk_probs, tk_idx = jax.lax.top_k(probs, TOP_K)
        tk_probs = tk_probs / (jnp.sum(tk_probs, axis=-1, keepdims=True) + EPS)
        onehot = tk_idx[..., None] == jnp.arange(NUM_EXPERTS)[None, None, :]
        w = jnp.sum(tk_probs[..., None] * onehot.astype(tk_probs.dtype), axis=1)
        out = _swiglu(xf, sWg, sWu, sWd)
        for e in range(NUM_EXPERTS):
            out = out + w[:, e:e + 1] * _swiglu(xf, Wg[e], Wu[e], Wd[e])
        return out.reshape(B, S, H)
    x = x + _L0_ffn_ref(_L0_cond_ref(fside_BxS_0, cond_1024, x, L0_cond_coeffs), L0_ffn_Wg, L0_ffn_bg, L0_ffn_W1, L0_ffn_b1, L0_ffn_W2, L0_ffn_b2)
    x = x + _L1_ffn_ref(_L1_cond_ref(x, cond_1024, L1_cond_Wx, L1_cond_Wh, L1_cond_b), L1_ffn_ln_scale, L1_ffn_ln_bias, L1_ffn_gate_w, L1_ffn_Wg, L1_ffn_Wu, L1_ffn_Wd, L1_ffn_sWg, L1_ffn_sWu, L1_ffn_sWd)
    return x

_drawn_inputs = setup_inputs


def setup_inputs(seed=0):
    import zlib

    import numpy as np

    out = dict(_drawn_inputs(seed))
    spreads = {'L0_ffn_bg': (0.0, 0.1),
     'L0_ffn_b1': (0.0, 0.356),
     'L0_ffn_b2': (0.0, 0.1),
     'L1_cond_b': (0.0, 0.1),
     'L1_ffn_ln_scale': (1.0, 0.2),
     'L1_ffn_ln_bias': (0.0, 0.1)}
    factors = {'L0_ffn_W1': 6.128}
    for name, (base, spread) in spreads.items():
        noise = np.random.default_rng([zlib.crc32(name.encode()), seed]).standard_normal(out[name].shape)
        drawn = base * np.exp(spread * noise) if base else spread * noise
        out[name] = jnp.asarray(drawn.astype(out[name].dtype))
    for name, factor in factors.items():
        out[name] = (out[name] * factor).astype(out[name].dtype)
    return out
```

```python
from contextlib import ExitStack

import concourse.bass as bass
from concourse import mybir

ALU = mybir.AluOpType
ACT = mybir.ActivationFunctionType
F32 = mybir.dt.float32
F32R = mybir.dt.float32r
I32 = mybir.dt.int32
U32 = mybir.dt.uint32
AX_X = mybir.AxisListType.X

P = 128
B, T, D = 32, 128, 128
E, HID, TOPK = 8, 256, 2
NC = HID // P
STEPS = 16
BLK = STEPS * B
TOK = T * B
NB = TOK // BLK
NT = BLK // P
U0 = E * NC
W1 = NB * NC
LAG = 4
RING = 4
TEMP = 5.0
EPS0, EPS1, LN_EPS = 1e-9, 1e-5, 1e-5
NEG = -3.0e38

ROW_GATE, ROW_B1, ROW_LNS, ROW_LNB, ROW_CB, ROW_H0 = 0, 8, 24, 25, 26, 32
G_HI, G_LO, G_HI2 = 0, 32, 64

REGION = TOK + P
ROW = D + 2
SLOTS = TOPK * TOK // P + E
PAD_ROWS = E * REGION
PAD_DEST = 1.0e6
ROWS_RING, OUT_RING = 8, 4
UNROLL = 8
assert UNROLL == ROWS_RING
TABLE_LEAD = 2
ROWS_AT_COL = TABLE_LEAD + SLOTS
PADS_AT_COL = ROWS_AT_COL + SLOTS

CONSTS = {}
for _name, _size in (("ident", P), ("tri", P), ("ones", P), ("center", P), ("ramp", E), ("region", E), ("ids", NT * TOPK),
                     ("dest", SLOTS), ("full", TOK // P), ("upto", E * E), ("slot", SLOTS), ("mean", 1), ("power", NT), ("pad", ROW)):
    CONSTS[_name] = slice(sum(s.stop - s.start for s in CONSTS.values()),
                          sum(s.stop - s.start for s in CONSTS.values()) + _size)
CONST_COLS = CONSTS["pad"].stop

XT_AT, LOGIT_AT, GT_AT = 0, 8, 15
P_AT = {1: 2, 3: 1, 5: 0}
S_AT = {13: 2, 14: 1, 15: 0}
CENTER_AT, LOGIT1_AT, ROWS_AT, RANK_AT = 5, 8, 13, 0
LOGITS_IN, LOGITS_DONE, FIRST_CHOICE, SECOND_CHOICE, EXPS, GATES, META = 8, 9, 10, 11, 12, 13, 14
XP_AT = 5
HEAD = U0 - XP_AT
SCATTER_AT = 3
SPLIT_AT = 6
XP_AT = 5
HEAD = U0 - XP_AT
SCATTER_AT = 3

TAIL6 = {0: ((11,), (12,)), 1: ((13,), (14,)), 2: ((15,), ())}
TAIL7 = {3 + h: ((2 * h,), (2 * h + 1,)) for h in range(STEPS // 2)}
TAIL_XP = 2
LOOP_LINKS = 28
TAIL_CENTER = {3: NB - 2, 11: NB - 1}
TAIL_LOGIT = {5: NB - 2, 13: NB - 1}
TAIL_RANK = {0: NB - 3, 9: NB - 2}
TAIL_ROUTE = {5: NB - 2, 13: NB - 1}


def a_use(n):
    return 1 + 6 * n


def b_use(n):
    return 1 + 4 * n


def step_col(s):
    return (s % 4) * P + (s // 4) * B


def has(i, first):
    return not isinstance(i, int) or i >= first


class Chain:

    def __init__(self, eng, sem):
        self.eng, self.sem, self.base, self.n = eng, sem, 0, 0

    def __call__(self, ins):
        self.n += 1
        ins.then_inc(self.sem, 1)
        self.eng.wait_ge(self.sem, self.base + self.n)

    def at(self, base):
        self.base, self.n = base, 0


def constant_tables():
    import numpy as np
    p, c = np.arange(P)[:, None], np.zeros((P, CONST_COLS), np.float32)
    c[:, CONSTS["ident"]] = np.eye(P)
    c[:, CONSTS["tri"]] = p < np.arange(P)
    c[:, CONSTS["ones"]] = 1.0
    c[:, CONSTS["center"]] = np.eye(P) - 1.0 / D
    c[:, CONSTS["ramp"]] = E - np.arange(E)
    c[:, CONSTS["region"]] = REGION * np.arange(E)
    k = np.arange(NT * TOPK)
    c[:, CONSTS["ids"]] = p * NT + k // TOPK + (k % TOPK) * TOK
    c[:, CONSTS["dest"]] = TOPK * TOK + P * np.arange(SLOTS) + p
    c[:, CONSTS["full"]] = P * np.arange(TOK // P)
    c[:, CONSTS["upto"]] = np.tril(np.ones((E, E))).reshape(-1)
    c[:, CONSTS["slot"]] = np.arange(SLOTS)
    c[:, CONSTS["mean"]] = 1.0 / D
    c[:, CONSTS["power"]] = -0.5
    c[:, CONSTS["pad"].stop - 1] = PAD_DEST
    return c


def build(nc, consts, x, fside_BxS_0, cond_1024, L0_cond_coeffs, L0_ffn_Wg, L0_ffn_bg, L0_ffn_W1, L0_ffn_b1,
          L0_ffn_W2, L0_ffn_b2, L1_cond_Wx, L1_cond_Wh, L1_cond_b, L1_ffn_ln_scale, L1_ffn_ln_bias,
          L1_ffn_gate_w, L1_ffn_Wg, L1_ffn_Wu, L1_ffn_Wd, L1_ffn_sWg, L1_ffn_sWu, L1_ffn_sWd, out):
    regions = nc.dram_tensor("regions", (PAD_ROWS + P, ROW), F32, kind="Internal").ap()
    results = nc.dram_tensor("results", (TOPK * TOK + SLOTS * P, D), F32, kind="Internal").ap()
    with ExitStack() as ctx:
        def sb(name, shape, dt=F32):
            return ctx.enter_context(nc.sbuf_tensor(name, shape, dt))

        def sem(name):
            return ctx.enter_context(nc.semaphore(name))

        banks = ctx.enter_context(nc.psum_tensor("banks", [P, 8, BLK], F32))
        hidden, acc = banks[:, 0:2, :], banks[:, 2:4, :]
        gate_ps, bank_a, rnn_ps, bank_b = (banks[:, n, :] for n in (4, 5, 6, 7))
        pair_ps = ((banks[:, 0, :], banks[:, 1, :]), (gate_ps, bank_a))
        up_ps, result_ps = hidden, acc
        turned_ps, act_turned_ps = (gate_ps, bank_a), (rnn_ps, bank_b)

        w1_hi, w1_lo = sb("w1_hi", [P, U0 * P], F32R), sb("w1_lo", [P, U0 * P], F32R)
        w2_hi, w2_lo = sb("w2_hi", [P, U0 * P], F32R), sb("w2_lo", [P, U0 * P], F32R)
        wgu, wd = sb("wgu", [P, E * 2 * HID]), sb("wd", [P, E * HID])
        sw_raw = sb("sw_raw", [P, 3 * HID])
        sw_hi, sw_lo = sb("sw_hi", [P, 3 * HID], F32R), sb("sw_lo", [P, 3 * HID], F32R)
        wx, wh = sb("wx", [P, P]), sb("wh", [P, P])
        wgate0, gate_b0 = sb("wgate0", [P, E]), sb("gate_b0", [P, E])
        gate_b1, wgate1 = sb("gate_b1", [P, E]), sb("wgate1", [P, E])
        b2_raw, b2_hi, b2s = sb("b2_raw", [P, P]), sb("b2_hi", [P, P]), sb("b2s", [P, P], F32R)
        prow, pcol = sb("prow", [P, P]), sb("pcol", [P, P])
        const_sb = sb("const_sb", [P, CONST_COLS])
        const = {k: const_sb[:, s] for k, s in CONSTS.items()}
        ident = const["ident"]
        lnb_tile, sel = sb("lnb_tile", [P, P]), sb("sel", [P, E, P], F32R)
        coef, xpow = sb("coef", [96, 9]), sb("xpow", [96, D])
        ypow, scond = sb("ypow", [96, 2, T]), sb("scond", [96, 3, T])
        delta, sfac = sb("delta", [96, B]), sb("sfac", [96, 3, BLK])
        prep = sb("prep", [P, 3 * BLK])
        xin, zt, z = (prep[:, k * BLK:(k + 1) * BLK] for k in range(3))
        xT = sb("xT", [P, NB * BLK])
        hT = sb("hT", [P, (NB + 1) * BLK])
        base = sb("base", [P, NB, BLK])
        in_hi, in_lo = sb("in_hi", [P, 2 * BLK], F32R), sb("in_lo", [P, 2 * BLK], F32R)
        gT = sb("gT", [P, 2 * BLK], F32R)
        gates3 = sb("gates3", [P, NT, P])
        gate_sb = sb("gate_sb", [P, 2, BLK])
        actv, gated = sb("actv", [P, RING, BLK]), sb("gated", [P, RING, BLK])
        h_hi, h_lo = sb("h_hi", [P, RING, BLK], F32R), sb("h_lo", [P, RING, BLK], F32R)
        hc, hc2 = sb("hc", [P, BLK]), sb("hc2", [P, BLK])
        rt = {k: sb("rt_" + k, [P, 2 * NT, E]) for k in
              ("logit", "d", "score", "one1", "d2", "two", "mask", "th", "num", "den", "e", "g", "gate")}
        rs = {k: sb("rs_" + k, [P, 2 * NT]) for k in ("m1", "s1", "m2", "s2", "sum", "top", "den", "inv")}
        first, second, both = slice(0, NT), slice(NT, 2 * NT), slice(0, 2 * NT)
        var, rstd = sb("var", [P, NT]), sb("rstd", [P, NT])
        rank, picks = sb("rank", [P, NT, E]), [sb(f"pick{k}", [P, NT, E]) for k in range(TOPK)]
        choices, new_choices = sb("choices", [P, E]), sb("new_choices", [P, E])
        ids, pos_f = sb("ids", [P, NT, TOPK]), sb("pos_f", [P, NT, TOPK])
        hrow_last = prep[:, 0:NT * TOPK * ROW].rearrange("p (t k c) -> p t k c", t=NT, k=TOPK)
        hrows = [sb("hrow", [P, NT, TOPK, ROW]), hrow_last]
        poss = [sb(f"pos{k}", [P, NT, TOPK], U32) for k in range(2)]
        counts, ends, blocks = sb("counts", [P, E]), sb("ends", [P, E]), sb("blocks", [P, E])
        table = sb("table", [P, PADS_AT_COL + E], I32)
        def carve(buf, *shapes):
            at = 0
            for shape in shapes:
                size = shape[0] * shape[1]
                yield buf[:, at:at + size].rearrange("p (a b) -> p a b", a=shape[0])
                at += size

        filled, upto_v, passed, per_slot = carve(xT, (E, TOK // P), (E, E), (SLOTS, E), (3, SLOTS))
        slot_e, slot_row, starts = (per_slot[:, k, :] for k in range(3))
        rows, state, silu_row, act_row, act_col, y_row = carve(hT, (ROWS_RING, ROW), (2, P), (2, HID), (2, HID), (2, HID), (OUT_RING, D))
        y_dest = sb("y_dest", [P, OUT_RING], U32)
        parts = gated.rearrange("p (m k) n -> p m k n", k=TOPK)
        state_tile = sw_raw[:, 0:BLK]
        w1_raw, w2_raw = (base.rearrange("p n t -> p (n t)")[:, k * U0 * P:(k + 1) * U0 * P] for k in range(2))

        (consts_in, params_in, cond_in, w1_in, w2_in, wgu_in, wd_in, shared_in, small_in, rnn_w_in, x_in, pads_done,
         scattered, y_out) = [
            sem(s) for s in ("consts_in", "params_in", "cond_in", "w1_in", "w2_in", "wgu_in", "wd_in", "shared_in",
                             "small_in", "rnn_w_in", "x_in", "pads_done", "scattered", "y_out")]
        (cleared, sel_ready, sfac_ready, pcol_ready, w1_cast, w1_split, w2_cast, w2_split, shared_cast, shared_split) = [
            sem(s) for s in ("cleared", "sel_ready", "sfac_ready", "pcol_ready", "w1_cast", "w1_split", "w2_cast",
                             "w2_split", "shared_cast", "shared_split")]
        (a_ready, a_free, b_ready, b_free, hid_ready, gate_ready, gate_copied, down_done, acc_taken, rnn_ready, h_done) = [
            sem(s) for s in ("a_ready", "a_free", "b_ready", "b_free", "hid_ready", "gate_ready", "gate_copied",
                             "down_done", "acc_taken", "rnn_ready", "h_done")]
        (gelu_done, gated_done, hi_act, hi_dve, lo_done, z_split, d_ready, th_ready, gates_ready) = [
            sem(s) for s in ("gelu_done", "gated_done", "hi_act", "hi_dve", "lo_done", "z_split", "d_ready", "th_ready",
                             "gates_ready")]
        (var_ready, rstd_ready, chosen_ready, pos_ready, table_ready) = [
            sem(s) for s in ("var_ready", "rstd_ready", "chosen_ready", "pos_ready", "table_ready")]
        (q_cast, q_split, pair_ready, silu_done, prod_done, hi1_done, lo1_done, down1_done, base_done) = [
            sem(s) for s in ("q_cast", "q_split", "pair_ready", "silu_done", "prod_done", "hi1_done", "lo1_done",
                             "down1_done", "base_done")]
        (turned, state_ready, up_ready, slot_silu, slot_prod, act_turned, act_copied, result_ready, y_ready, summed) = [
            sem(s) for s in ("turned", "state_ready", "up_ready", "slot_silu", "slot_prod", "act_turned", "act_copied",
                             "result_ready", "y_ready", "summed")]
        rows_in = [sem(f"rows_in{s}") for s in range(ROWS_RING)]
        results_out = [sem(f"results_out{s}") for s in range(OUT_RING)]
        parts_in = [sem(f"parts_in{m}") for m in range(2)]
        dve_chain, scatter_go = sem("dve_chain"), sem("scatter_go")

        def cols(n):
            return bass.ds(n * BLK, BLK)

        def hcols(n, off=0, size=BLK):
            return bass.ds((n + 1) * BLK + off, size)

        def slot(n):
            return bass.ds((n % 2) * BLK, BLK)

        def acc_of(n):
            return acc.rearrange("p a n -> p (a n)")[:, slot(n)]

        def table_values(eng, at, count, most):
            return nc.values_load_multi_w_load_instructions(
                table[0:1, bass.ds(at, count)], engines=[eng.engine], min_val=0, max_val=most,
                skip_runtime_bounds_check_because="the vector engine clamped the table's values")[1]

        def wait_high(eng, i, u):
            eng.wait_ge(hi_dve if u % 2 else hi_act, U0 // 2 * i + u // 2 + 1)

        def layers_of(i, last):
            return not last, has(i, 2)

        def own(n):
            return 1 if isinstance(n, int) and n == NB - 1 else 0

        def shared(w, part, c):
            return w[:, part * HID + c * P:part * HID + (c + 1) * P]

        x_rows = x.rearrange("b (n q r) d -> n q b (r d)", n=NB, q=4)
        y_rows = out.rearrange("b (n q r) d -> n q b (r d)", n=NB, q=4)
        result_rows = results[0:TOPK * TOK, :].rearrange("(k n p r) d -> k n p (r d)", k=TOPK, n=NB, r=NT)
        block = ctx.enter_context(nc.Block())

        @block.sync
        def _(sp):
            def load_x(n):
                for q in range(4):
                    src = x_rows[n, q] if isinstance(n, int) else x_rows[bass.ds(n, 1), q].squeeze(0)
                    sp.dma_start(xin[q * B:(q + 1) * B, :], src).then_inc(x_in, 16)

            def load_rows(it, reused):
                first_rows = table_values(sp, ROWS_AT_COL + it * UNROLL, UNROLL, PAD_ROWS)
                for s, row in enumerate(first_rows):
                    if reused:
                        sp.wait_ge(y_ready, (it - 1) * UNROLL + s + 1)
                    sp.dma_start(rows[:, s, :], regions[bass.ds(row, P), :]).then_inc(rows_in[s], 16)

            def load_parts(n, m):
                for k in range(TOPK):
                    sp.dma_start(parts[:, m, k, :], result_rows[k, n]).then_inc(parts_in[m], 16)

            def store_y(n):
                sp.wait_ge(summed, n + 1)
                for q in range(4):
                    sp.dma_start(y_rows[n, q], base[q * B:(q + 1) * B, n, :]).then_inc(y_out, 16)

            sp.dma_start(const_sb[:, :], consts).then_inc(consts_in, 16)
            load_x(0)
            sp.wait_ge(cleared, 2)
            sp.dma_start(prow[ROW_H0:ROW_H0 + B, :], cond_1024).then_inc(params_in, 16)
            sp.dma_start(prow[ROW_B1:ROW_B1 + U0, :], L0_ffn_b1.rearrange("e (c h) -> (e c) h", c=NC)).then_inc(params_in, 16)
            sp.dma_start(prow[ROW_GATE:ROW_GATE + E, :], L1_ffn_gate_w).then_inc(params_in, 16)
            for row, v in ((ROW_LNS, L1_ffn_ln_scale), (ROW_LNB, L1_ffn_ln_bias), (ROW_CB, L1_cond_b)):
                sp.dma_start(prow[row:row + 1, :], v.rearrange("(o d) -> o d", o=1)).then_inc(params_in, 16)
            sp.dma_start(wgate0[:, :], L0_ffn_Wg).then_inc(small_in, 16)
            sp.dma_start(gate_b0[:, :], L0_ffn_bg.rearrange("(o e) -> o e", o=1).partition_broadcast(P).squeeze(1)).then_inc(small_in, 16)
            for row in (G_HI, G_LO, G_HI2):
                sp.dma_start(b2_raw[row:row + E, :], L0_ffn_b2).then_inc(small_in, 16)
            sp.dma_start(wx[:, :], L1_cond_Wx).then_inc(rnn_w_in, 16)
            sp.dma_start(wh[:, :], L1_cond_Wh).then_inc(rnn_w_in, 16)
            sp.wait_ge(a_ready, a_use(0) + 1)
            load_x(1)
            sp.dma_start(sw_raw[:, 0:HID], L1_ffn_sWg).then_inc(shared_in, 16)
            sp.dma_start(sw_raw[:, HID:2 * HID], L1_ffn_sWu).then_inc(shared_in, 16)
            sp.dma_start(sw_raw[:, 2 * HID:].rearrange("p (c d) -> p c d", c=NC), L1_ffn_sWd.rearrange("(c h) d -> h c d", c=NC)).then_inc(shared_in, 16)
            wgu_v = wgu.rearrange("p (e g h) -> p e g h", e=E, g=2)
            sp.dma_start(wgu_v[:, :, 0, :], L1_ffn_Wg.rearrange("e d h -> d e h")).then_inc(wgu_in, 16)
            sp.dma_start(wgu_v[:, :, 1, :], L1_ffn_Wu.rearrange("e d h -> d e h")).then_inc(wgu_in, 16)
            for c in range(NC):
                sp.dma_start(wd.rearrange("p (e c d) -> p e c d", c=NC, d=D)[:, :, c, :],
                             L1_ffn_Wd[:, c * P:(c + 1) * P, :].rearrange("e h d -> h e d")).then_inc(wd_in, 16)
            sp.wait_ge(consts_in, 16)
            sp.dma_start(regions[PAD_ROWS:PAD_ROWS + P, :], const["pad"]).then_inc(pads_done, 16)
            with sp.Fori(2, NB) as n:
                sp.wait_ge(a_ready, a_use(n - 1) + 1)
                load_x(n)
            sp.wait_ge(table_ready, 1)
            for row in table_values(sp, PADS_AT_COL, E, PAD_ROWS - P):
                sp.dma_start(regions[bass.ds(row, P), :], const["pad"]).then_inc(pads_done, 16)
            sp.wait_ge(scattered, 16 * NB * NT * TOPK)
            sp.wait_ge(pads_done, 16 * (E + 1))
            load_rows(0, False)
            with sp.Fori(1, SLOTS // UNROLL) as it:
                load_rows(it, True)
            for landed in results_out:
                sp.wait_ge(landed, 16 * SLOTS // OUT_RING)
            for n in range(NB):
                if n >= 2:
                    sp.wait_ge(summed, n - 1)
                load_parts(n, n % 2)
                if n >= 1:
                    store_y(n - 1)
            store_y(NB - 1)
            sp.wait_ge(y_out, NB * 4 * 16)

        @block.gpsimd
        def _(pool):
            pool.memset(prow[:, :], 0.0).then_inc(cleared, 1)
            pool.memset(b2_raw[:, :], 0.0).then_inc(cleared, 1)
            pool.memset(gates3[:, :, :], 0.0).then_inc(cleared, 1)
            pool.wait_ge(consts_in, 16)

            def inv_std(n):
                pool.wait_ge(var_ready, n + 1)
                pool.tensor_tensor(rstd[:, :], var[:, :], const["power"], ALU.pow).then_inc(rstd_ready, 1)

            def scatter(n, t, k):
                if t == 0 and k == 0:
                    pool.wait_ge(b_free, b_use(n) + 3)
                    pool.wait_ge(pos_ready, n + 1)
                    pool.sem_inc(scatter_go, 1)
                pool.indirect_dma_start(regions, bass.IndirectOffsetOnAxis(ap=poss[own(n)][:, t, k:k + 1], axis=0),
                                        hrows[own(n)][:, t, k, :], None).then_inc(scattered, 16)

            def low0(i, u):
                k = U0 * i + u
                wait_high(pool, i, u)
                if has(k, RING):
                    pool.wait_ge(down_done, k + 1 - RING)
                pool.tensor_tensor(h_lo[:, u % RING, :], gated[:, u % RING, :],
                                   h_hi[:, u % RING, :].bitcast(F32), ALU.subtract).then_inc(lo_done, 1)

            def body0(i):
                for u in range(U0):
                    low0(i, u)
                    if has(i, 2) and u == LOGITS_IN - 1:
                        inv_std(i - 2)
                    if has(i, 3) and SCATTER_AT <= u < SCATTER_AT + NT * TOPK:
                        scatter(i - 3, *divmod(u - SCATTER_AT, TOPK))

            def scatter_block(n):
                for t in range(NT):
                    for k in range(TOPK):
                        scatter(n, t, k)

            for c in range(NC):
                half = slice(c * E * P, (c + 1) * E * P)
                pool.wait_ge(w2_cast, c + 1)
                pool.tensor_tensor(w2_lo[:, half], w2_raw[:, half], w2_hi[:, half].bitcast(F32),
                                   ALU.subtract).then_inc(w2_split, 1)
            for i in range(3):
                body0(i)
            with pool.Fori(3, NB - 1) as i:
                body0(i)
            body0(NB - 1)
            scatter_block(NB - 3)
            inv_std(NB - 2)
            scatter_block(NB - 2)
            inv_std(NB - 1)
            scatter_block(NB - 1)

            def scatter_result(j, s):
                pool.wait_ge(y_ready, j + 1)
                pool.sem_inc(scatter_go, 1)
                pool.indirect_dma_start(results, bass.IndirectOffsetOnAxis(ap=y_dest[:, s:s + 1], axis=0),
                                        y_row[:, s, :], None).then_inc(results_out[s], 16)

            with pool.Fori(0, SLOTS // UNROLL) as it:
                for s in range(UNROLL):
                    scatter_result(it * UNROLL + s, s % OUT_RING)

        @block.scalar
        def _(act):
            for g in range(3):
                part = slice(32 * g, 32 * g + 32)
                act.dma_start(coef[part, :], L0_cond_coeffs[g].rearrange("b c -> (b c)").partition_broadcast(32)).then_inc(cond_in, 16)
                act.dma_start(ypow[part, 0, :], cond_1024).then_inc(cond_in, 16)
                if g:
                    act.dma_start(xpow[part, :], fside_BxS_0).then_inc(cond_in, 16)
            for e0 in (0, E // 2):
                act.dma_start(w1_raw.rearrange("p (e h) -> p e h", e=E)[:, e0:e0 + E // 2, :],
                              L0_ffn_W1[e0:e0 + E // 2].rearrange("e d h -> d e h")).then_inc(w1_in, 16)
            for c in range(NC):
                act.dma_start(w2_raw.rearrange("p (e c d) -> p e c d", c=NC, d=D)[:, :, c, :],
                              L0_ffn_W2[:, c * P:(c + 1) * P, :].rearrange("e h d -> h e d")).then_inc(w2_in, 16)

            def copy_a(use, dst, size=BLK):
                act.wait_ge(a_ready, use + 1)
                nc.scalar.copy(dst, bank_a[:, 0:size]).then_inc(a_free, 1)

            def gelu(i, u):
                k = U0 * i + u
                act.wait_ge(hid_ready, k + 1)
                if has(k, RING):
                    act.wait_ge(gated_done, k + 1 - RING)
                nc.scalar.activation(actv[:, u % RING, :], hidden[:, u % 2, :], ACT.Gelu,
                                     bias=pcol[:, ROW_B1 + u:ROW_B1 + u + 1]).then_inc(gelu_done, 1)

            def copy_gate(i, e):
                g = E * i + e
                act.wait_ge(gate_ready, g + 1)
                if has(g, 2):
                    act.wait_ge(gated_done, U0 * i + NC * (e - 1))
                nc.scalar.copy(gate_sb[:, e % 2, :], gate_ps[:, :]).then_inc(gate_copied, 1)

            def tanh_step(n, s):
                act.wait_ge(rnn_ready, STEPS * n + s + 1)
                nc.scalar.activation(hT[:, hcols(n, step_col(s), B)], rnn_ps[:, step_col(s):step_col(s) + B],
                                     ACT.Tanh, bias=pcol[:, ROW_CB:ROW_CB + 1]).then_inc(h_done, 1)

            def router_tanh(r, layers):
                act.wait_ge(d_ready, r + 1)
                for layer in layers:
                    part, temp = (first, TEMP) if layer == 0 else (second, 1.0)
                    ins = nc.scalar.activation(rt["th"][:, part, :], rt["d"][:, part, :], ACT.Tanh, scale=0.5 / temp)
                ins.then_inc(th_ready, 1)

            def round0(i, u):
                k = U0 * i + u
                act.wait_ge(gated_done, k + 1)
                if has(k, RING):
                    act.wait_ge(down_done, k + 1 - RING)
                nc.scalar.copy(h_hi[:, u % RING, :], gated[:, u % RING, :]).then_inc(hi_act, 1)

            def centered(n):
                act.wait_ge(b_ready, b_use(n) + 1)
                nc.scalar.copy(state_tile, hT[:, hcols(n)])
                nc.scalar.copy(hc[:, :], bank_b[:, :])
                nc.scalar.activation(hc2[:, :], bank_b[:, :], ACT.Square).then_inc(b_free, 1)

            def copy_rows(n):
                act.wait_ge(b_ready, b_use(n) + 3)
                if own(n) == 0 and has(n, 1):
                    act.wait_ge(scattered, 16 * NT * TOPK * n)
                src = bank_b.rearrange("p (t d) -> p t d", t=NT)
                nc.scalar.copy(hrows[own(n)][:, :, 0, 0:D], src)
                nc.scalar.copy(hrows[own(n)][:, :, 1, 0:D], src).then_inc(b_free, 1)

            def cast_state(n):
                act.wait_ge(h_done, STEPS * (n + 1) + 1)
                if n < 2:
                    act.wait_ge(hid_ready, U0 * (NB - 1 + n))
                else:
                    act.wait_ge(pair_ready, NC * (n - 1))
                nc.scalar.copy(in_hi[:, slot(n)], hT[:, hcols(n)]).then_inc(q_cast, 1)

            def body0(i, last=False):
                for u in range(U0):
                    gelu(i, u)
                    if u % NC == 0:
                        copy_gate(i, u // NC)
                    else:
                        round0(i, u - 1)
                    if not last:
                        if u == XT_AT:
                            copy_a(a_use(i + 1), xT[:, cols(i + 1)])
                        if u == GT_AT:
                            if has(i, 1):
                                act.wait_ge(down_done, U0 * i)
                            copy_a(a_use(i + 1) + 5, gT[:, slot(i + 1)])
                    if u == FIRST_CHOICE:
                        router_tanh(i + 1, [k for k in range(2) if layers_of(i, last)[k]])
                    if has(i, 2):
                        if u < XP_AT:
                            tanh_step(i - 2, HEAD + u)
                        if u == CENTER_AT:
                            centered(i - 2)
                        if u == ROWS_AT + 1:
                            copy_rows(i - 2)
                    if has(i, 1) and u >= XP_AT:
                        tanh_step(i - 1, u - XP_AT)
                    if isinstance(i, int) and i == 0 and u == SPLIT_AT:
                        act.wait_ge(shared_in, 48)
                        nc.scalar.copy(sw_hi[:, :], sw_raw[:, :]).then_inc(shared_cast, 1)
                    if last and u == SPLIT_AT:
                        cast_state(0)

            def silu(w):
                act.wait_ge(pair_ready, w + 1)
                if w < RING:
                    act.wait_ge(gated_done, U0 * (NB - 1) + U0 - RING + w + 1)
                else:
                    act.wait_ge(prod_done, w + 1 - RING)
                nc.scalar.activation(actv[:, w % RING, :], pair_ps[w % 2][0], ACT.Silu).then_inc(silu_done, 1)

            def cast_hidden(w):
                act.wait_ge(prod_done, w + 1)
                if w < RING:
                    act.wait_ge(down_done, U0 * (NB - 1) + U0 - RING + w + 1)
                else:
                    act.wait_ge(down1_done, w + 1 - RING)
                nc.scalar.copy(h_hi[:, w % RING, :], gated[:, w % RING, :]).then_inc(hi1_done, 1)

            def copy_base(n):
                act.wait_ge(down1_done, NC * (n + 1))
                nc.scalar.copy(base[:, n, :], acc_of(n)).then_inc(base_done, 1)

            def tail():
                for w in range(W1):
                    silu(w)
                    for s in TAIL6.get(w, ((), ()))[0]:
                        tanh_step(NB - 2, s)
                    for s in TAIL7.get(w, ((), ()))[0]:
                        tanh_step(NB - 1, s)
                    if w >= 1:
                        cast_hidden(w - 1)
                    for s in TAIL6.get(w, ((), ()))[1]:
                        tanh_step(NB - 2, s)
                    for s in TAIL7.get(w, ((), ()))[1]:
                        tanh_step(NB - 1, s)
                    if w % NC == NC - 1 and w + 1 < W1:
                        cast_state((w + 1) // NC)
                    if w in TAIL_CENTER:
                        centered(TAIL_CENTER[w])
                    if w in TAIL_LOGIT:
                        copy_rows(TAIL_LOGIT[w])
                    if w - 1 in TAIL_ROUTE:
                        router_tanh(TAIL_ROUTE[w - 1] + 3, [1])
                    if w % NC == 0 and w >= 2 * NC:
                        copy_base(w // NC - 2)
                cast_hidden(W1 - 1)
                copy_base(NB - 2)
                copy_base(NB - 1)

            def slot_silu_of(j, s, first):
                act.wait_ge(up_ready, j + 1)
                if not (first and s < 2):
                    act.wait_ge(slot_prod, j - 1)
                nc.scalar.activation(silu_row[:, s % 2, :], up_ps[:, s % 2, 0:HID], ACT.Silu).then_inc(slot_silu, 1)

            def copy_act(j, s, first):
                act.wait_ge(act_turned, j + 1)
                if not (first and s < 2):
                    act.wait_ge(result_ready, j - 1)
                nc.scalar.copy(act_col[:, s % 2, :], act_turned_ps[s % 2][:, 0:HID]).then_inc(act_copied, 1)

            def slots(it, first=False):
                for s in range(UNROLL):
                    j = it * UNROLL + s
                    slot_silu_of(j, s, first)
                    if not (first and s == 0):
                        copy_act(j - 1, s - 1, first)

            copy_a(0, pcol[:, :], P)
            copy_a(a_use(0), xT[:, cols(0)])
            for h in range(2):
                act.wait_ge(w1_in, 32)
                for e in range(E // 2 * h, E // 2 * (h + 1)):
                    nc.scalar.copy(w1_hi[:, e * HID:(e + 1) * HID], w1_raw[:, e * HID:(e + 1) * HID]).then_inc(w1_cast, 1)
            act.wait_ge(w2_in, 32)
            for c in range(NC):
                half = slice(c * E * P, (c + 1) * E * P)
                nc.scalar.copy(w2_hi[:, half], w2_raw[:, half]).then_inc(w2_cast, 1)
            router_tanh(0, [0])
            copy_a(a_use(0) + 5, gT[:, slot(0)])
            for i in range(3):
                body0(i)
            with act.Fori(3, NB - 1) as i:
                body0(i)
            body0(NB - 1, last=True)
            tail()
            slots(0, first=True)
            with act.Fori(1, SLOTS // UNROLL) as it:
                slots(it)
            copy_act(SLOTS - 1, UNROLL - 1, False)

        @block.vector
        def _(dve):
            link = Chain(dve, dve_chain)

            def per_tile(v, part=both):
                return v[:, part].unsqueeze(2).to_broadcast([P, part.stop - part.start, E])

            def per_expert(v, part=first):
                return v[:, :].unsqueeze(1).to_broadcast([P, part.stop - part.start, E])

            def factor(n, c):
                if has(n, 1):
                    dve.wait_ge(a_ready, a_use(n - 1) + 4 - c)
                src = scond[:, c, bass.ds(n * STEPS, STEPS)].rearrange("p (q r) -> p r q", q=4)
                dve.tensor_tensor(
                    sfac[:, c, :].rearrange("p (r q b) -> p r q b", r=4, q=4),
                    src.unsqueeze(3).to_broadcast([96, 4, 4, B]),
                    delta[:, :].unsqueeze(1).unsqueeze(1).to_broadcast([96, 4, 4, B]),
                    ALU.mult).then_inc(sfac_ready, 1)

            def condition(n, c):
                use = a_use(n) + 3 - c
                xb = xT[:, cols(n)]
                dve.wait_ge(a_ready, use + 1)
                if c == 2:
                    dve.tensor_tensor(zt[:, :], bank_a, xb, ALU.mult).then_inc(a_free, 1)
                elif c == 1:
                    dve.tensor_tensor(zt[:, :], bank_a, zt[:, :], ALU.add).then_inc(a_free, 1)
                    dve.wait_ge(a_free, use + 1)
                    link(dve.tensor_tensor(zt[:, :], zt[:, :], xb, ALU.mult))
                else:
                    dve.tensor_tensor(z[:, :], bank_a, zt[:, :], ALU.add).then_inc(a_free, 1)
                    dve.wait_ge(a_free, use + 1)
                    if has(n, 2):
                        dve.wait_ge(hid_ready, U0 * (n - 1))
                    link(dve.tensor_copy(in_hi[:, slot(n)], z[:, :]))
                    dve.tensor_tensor(in_lo[:, slot(n)], z[:, :], in_hi[:, slot(n)].bitcast(F32),
                                      ALU.subtract).then_inc(z_split, 1)

            def logits0(n):
                use = a_use(n) + 4
                dve.wait_ge(a_ready, use + 1)
                dve.tensor_tensor(rt["logit"][:, first, :], bank_a[:, 0:NT * E].rearrange("p (t e) -> p t e", e=E),
                                  per_expert(gate_b0), ALU.add).then_inc(a_free, 1)

            def variance1(n):
                dve.wait_ge(b_ready, b_use(n) + 2)
                dve.tensor_scalar(var[:, :], bank_b[:, NT * E:NT * E + NT], LN_EPS, None, ALU.add).then_inc(var_ready, 1)

            def logits1(n):
                use = b_use(n) + 1
                dve.wait_ge(rstd_ready, n + 1)
                dve.tensor_tensor(rt["logit"][:, second, :], bank_b[:, 0:NT * E].rearrange("p (t e) -> p t e", e=E),
                                  per_tile(rstd, first), ALU.mult).then_inc(b_free, 1)
                dve.wait_ge(b_free, use + 1)
                link(dve.tensor_tensor(rt["logit"][:, second, :], rt["logit"][:, second, :], per_expert(gate_b1), ALU.add))

            def less_maximum(r, part):
                link(dve.tensor_reduce(rs["m1"][:, part], rt["logit"][:, part, :], AX_X, ALU.max))
                dve.tensor_tensor(rt["d"][:, part, :], rt["logit"][:, part, :], per_tile(rs["m1"], part), ALU.subtract).then_inc(d_ready, 1)

            def first_choice(r, part):
                d, score, one1, d2 = (rt[k][:, part, :] for k in ("d", "score", "one1", "d2"))
                ramp = per_expert(const["ramp"], part)
                dve.wait_ge(d_ready, r + 1)
                link(dve.scalar_tensor_tensor(out=score, in0=d, scalar=0.0, in1=ramp, op0=ALU.is_ge, op1=ALU.mult))
                link(dve.tensor_reduce(rs["s1"][:, part], score, AX_X, ALU.max))
                link(dve.tensor_tensor(one1, score, per_tile(rs["s1"], part), ALU.is_equal))
                link(dve.scalar_tensor_tensor(out=d2, in0=one1, scalar=NEG, in1=d, op0=ALU.mult, op1=ALU.add))
                link(dve.tensor_reduce(rs["m2"][:, part], d2, AX_X, ALU.max))

            def second_choice(part):
                score, d2, two = (rt[k][:, part, :] for k in ("score", "d2", "two"))
                ramp = per_expert(const["ramp"], part)
                link(dve.tensor_tensor(score, d2, per_tile(rs["m2"], part), ALU.is_equal))
                link(dve.tensor_tensor(score, score, ramp, ALU.mult))
                link(dve.tensor_reduce(rs["s2"][:, part], score, AX_X, ALU.max))
                link(dve.tensor_tensor(two, score, per_tile(rs["s2"], part), ALU.is_equal))
                link(dve.tensor_tensor(rt["mask"][:, part, :], rt["one1"][:, part, :], two, ALU.add))

            def exps(r, part):
                th, num, den, e, g = (rt[k][:, part, :] for k in ("th", "num", "den", "e", "g"))
                dve.wait_ge(th_ready, r + 1)
                link(dve.tensor_scalar(den, th, -1.0, 1.0, ALU.mult, ALU.add))
                dve.reciprocal(den, den)
                link(dve.tensor_scalar(num, th, 1.0, None, ALU.add))
                link(dve.tensor_tensor(e, num, den, ALU.mult))
                link(dve.tensor_tensor(g, e, rt["mask"][:, part, :], ALU.mult))

            def gates(part):
                e, g = rt["e"][:, part, :], rt["g"][:, part, :]
                dve.tensor_reduce(rs["sum"][:, part], e, AX_X, ALU.add)
                link(dve.tensor_reduce(rs["top"][:, part], g, AX_X, ALU.add))
                for layer, eps in ((first, EPS0), (second, EPS1)):
                    if part.start <= layer.start and layer.stop <= part.stop:
                        ins = dve.scalar_tensor_tensor(out=rs["den"][:, layer], in0=rs["sum"][:, layer], scalar=eps,
                                                       in1=rs["top"][:, layer], op0=ALU.mult, op1=ALU.add)
                link(ins)
                link(dve.reciprocal(rs["inv"][:, part], rs["den"][:, part]))
                link(dve.tensor_tensor(rt["gate"][:, part, :], g, per_tile(rs["inv"], part), ALU.mult))

            def gates0(n):
                gate, hi = rt["gate"][:, first, :], gates3[:, :, G_HI:G_HI + E]
                dve.tensor_copy(gates3[:, :, G_HI2:G_HI2 + E].bitcast(F32R), gate)
                link(dve.tensor_copy(hi.bitcast(F32R), gate))
                dve.tensor_tensor(gates3[:, :, G_LO:G_LO + E], gate, hi, ALU.subtract).then_inc(gates_ready, 1)

            def gates1(n):
                if has(n, 1):
                    dve.wait_ge(chosen_ready, n)
                    if own(n) == 0:
                        dve.wait_ge(scattered, 16 * NT * TOPK * n)
                hrow = hrows[own(n)]
                for k, chosen in enumerate(("one1", "two")):
                    ins = dve.tensor_tensor(picks[k][:, :, :], rt["gate"][:, second, :], rt[chosen][:, second, :], ALU.mult)
                link(ins)
                for k in range(TOPK):
                    dve.tensor_reduce(hrow[:, :, k, D:D + 1].squeeze(2), picks[k][:, :, :], AX_X, ALU.add)
                link(dve.tensor_copy(hrow[:, :, :, D + 1:D + 2].squeeze(3), ids[:, :, :]))
                dve.tensor_scalar(ids[:, :, :], ids[:, :, :], float(BLK), None, ALU.add).then_inc(chosen_ready, 1)

            def positions(n):
                use = b_use(n) + 3
                dve.wait_ge(b_ready, use + 1)
                dve.tensor_tensor(rank[:, :, :], bank_b[:, 0:NT * E].rearrange("p (t e) -> p t e", e=E),
                                  per_expert(const["region"]), ALU.add).then_inc(b_free, 1)
                link(dve.tensor_reduce(new_choices[:, :], rt["mask"][:, second, :].rearrange("p t e -> p e t"), AX_X, ALU.add))
                dve.wait_ge(b_free, use + 1)
                for k, chosen in enumerate(("one1", "two")):
                    ins = dve.tensor_tensor(picks[k][:, :, :], rank[:, :, :], rt[chosen][:, second, :], ALU.mult)
                link(ins)
                dve.tensor_tensor(choices[:, :], choices[:, :], new_choices[:, :], ALU.add)
                for k in range(TOPK):
                    ins = dve.tensor_reduce(pos_f[:, :, k:k + 1].squeeze(2), picks[k][:, :, :], AX_X, ALU.add)
                link(ins)
                dve.tensor_copy(poss[own(n)][:, :, :], pos_f[:, :, :]).then_inc(pos_ready, 1)

            def gate0(i, u):
                k = U0 * i + u
                dve.wait_ge(gelu_done, k + 1)
                dve.wait_ge(gate_copied, E * i + u // NC + 1)
                if has(k, RING):
                    dve.wait_ge(lo_done, k + 1 - RING)
                dve.tensor_tensor(gated[:, u % RING, :], actv[:, u % RING, :], gate_sb[:, (u // NC) % 2, :],
                                  ALU.mult).then_inc(gated_done, 1)

            def round0(i, u):
                k = U0 * i + u
                dve.wait_ge(gated_done, k + 1)
                if has(k, RING):
                    dve.wait_ge(down_done, k + 1 - RING)
                dve.tensor_copy(h_hi[:, u % RING, :], gated[:, u % RING, :]).then_inc(hi_dve, 1)

            def residual0(n):
                dve.wait_ge(down_done, U0 * (n + 1))
                dve.tensor_tensor(xT[:, cols(n)], acc_of(n), xT[:, cols(n)], ALU.add).then_inc(acc_taken, 1)

            def split_state(n):
                dve.wait_ge(q_cast, n + 1)
                dve.tensor_tensor(in_lo[:, slot(n)], hT[:, hcols(n)], in_hi[:, slot(n)].bitcast(F32),
                                  ALU.subtract).then_inc(q_split, 1)

            def body0(i, last=False):
                layer0, layer1 = layers_of(i, last)
                part = slice(0 if layer0 else NT, 2 * NT if layer1 else NT)
                for u in range(U0):
                    gate0(i, u)
                    if has(i, 3) and u == RANK_AT + 1:
                        positions(i - 3)
                    if has(i, 1) and u == LAG - 1:
                        residual0(i - 1)
                    if layer0 and u in P_AT:
                        condition(i + 1, P_AT[u])
                    if u == LOGITS_IN:
                        if layer0:
                            logits0(i + 1)
                        if layer1:
                            variance1(i - 2)
                    if layer0 or layer1:
                        if u == LOGITS_DONE:
                            if layer1:
                                logits1(i - 2)
                            if layer0:
                                dve.wait_ge(a_free, a_use(i + 1) + 5)
                            less_maximum(i + 1, part)
                        if u == FIRST_CHOICE:
                            first_choice(i + 1, part)
                        if u == SECOND_CHOICE:
                            second_choice(part)
                        if u == EXPS:
                            exps(i + 1, part)
                        if u == GATES:
                            gates(part)
                            if layer0:
                                gates0(i + 1)
                        if u == META and layer1:
                            gates1(i - 2)
                    if not (isinstance(i, int) and i + 2 >= NB) and u in S_AT:
                        factor(i + 2, S_AT[u])
                    if isinstance(i, int) and i == 0 and u == SPLIT_AT:
                        dve.wait_ge(shared_cast, 1)
                        dve.tensor_tensor(sw_lo[:, :], sw_raw[:, :], sw_hi[:, :].bitcast(F32), ALU.subtract).then_inc(shared_split, 1)
                    if last and u == SPLIT_AT:
                        split_state(0)
                    if u % 2:
                        round0(i, u)

            def multiply(w):
                dve.wait_ge(silu_done, w + 1)
                if w < RING:
                    dve.wait_ge(lo_done, U0 * (NB - 1) + U0 - RING + w + 1)
                else:
                    dve.wait_ge(lo1_done, w + 1 - RING)
                dve.tensor_tensor(gated[:, w % RING, :], actv[:, w % RING, :], pair_ps[w % 2][1], ALU.mult).then_inc(prod_done, 1)

            def split_hidden(w):
                dve.wait_ge(hi1_done, w + 1)
                if w < RING:
                    dve.wait_ge(down_done, U0 * (NB - 1) + U0 - RING + w + 1)
                else:
                    dve.wait_ge(down1_done, w + 1 - RING)
                dve.tensor_tensor(h_lo[:, w % RING, :], gated[:, w % RING, :], h_hi[:, w % RING, :].bitcast(F32),
                                  ALU.subtract).then_inc(lo1_done, 1)

            def tail():
                for w in range(W1):
                    multiply(w)
                    if w == 1:
                        residual0(NB - 1)
                    if w >= 1:
                        split_hidden(w - 1)
                    if w % NC == NC - 1 and w + 1 < W1:
                        split_state((w + 1) // NC)
                    if w in TAIL_RANK:
                        positions(TAIL_RANK[w])
                    if w in TAIL_ROUTE:
                        n = TAIL_ROUTE[w]
                        variance1(n)
                        logits1(n)
                        less_maximum(n + 3, second)
                    if w - 1 in TAIL_ROUTE:
                        first_choice(TAIL_ROUTE[w - 1] + 3, second)
                        second_choice(second)
                    if w - 2 in TAIL_ROUTE:
                        n = TAIL_ROUTE[w - 2]
                        exps(n + 3, second)
                        gates(second)
                        gates1(n)
                split_hidden(W1 - 1)
                positions(NB - 1)

            def make_table():
                use = b_use(NB)
                dve.wait_ge(b_ready, use + 1)
                dve.tensor_copy(counts[:, :], bank_b[:, 0:E]).then_inc(b_free, 1)
                dve.wait_ge(b_free, use + 1)
                by_full, by_slot = [P, E, TOK // P], [P, SLOTS, E]
                link(dve.tensor_tensor(filled[:, :, :], counts[:, :].unsqueeze(2).to_broadcast(by_full),
                                       const["full"].unsqueeze(1).to_broadcast(by_full), ALU.is_gt))
                link(dve.tensor_reduce(blocks[:, :], filled[:, :, :], AX_X, ALU.add))
                link(dve.tensor_tensor(upto_v[:, :, :], blocks[:, :].unsqueeze(1).to_broadcast([P, E, E]),
                                       const["upto"].rearrange("p (a b) -> p a b", a=E), ALU.mult))
                link(dve.tensor_reduce(ends[:, :], upto_v[:, :, :], AX_X, ALU.add))
                link(dve.tensor_tensor(passed[:, :, :], const["slot"].unsqueeze(2).to_broadcast(by_slot),
                                       ends[:, :].unsqueeze(1).to_broadcast(by_slot), ALU.is_ge))
                link(dve.tensor_reduce(slot_e[:, :], passed[:, :, :], AX_X, ALU.add))
                link(dve.tensor_tensor(passed[:, :, :], passed[:, :, :], blocks[:, :].unsqueeze(1).to_broadcast(by_slot), ALU.mult))
                link(dve.tensor_reduce(starts[:, :], passed[:, :, :], AX_X, ALU.add))
                link(dve.tensor_tensor(starts[:, :], const["slot"], starts[:, :], ALU.subtract))
                link(dve.tensor_scalar(slot_row[:, :], slot_e[:, :], float(REGION), None, ALU.mult))
                link(dve.scalar_tensor_tensor(out=slot_row[:, :], in0=starts[:, :], scalar=float(P), in1=slot_row[:, :],
                                              op0=ALU.mult, op1=ALU.add))
                link(dve.tensor_scalar(slot_row[:, :], slot_row[:, :], float(PAD_ROWS), None, ALU.min))
                link(dve.tensor_scalar(slot_e[:, :], slot_e[:, :], float(E - 1), None, ALU.min))
                link(dve.tensor_tensor(counts[:, :], counts[:, :], const["region"], ALU.add))
                dve.tensor_copy(table[:, TABLE_LEAD:ROWS_AT_COL], slot_e)
                dve.tensor_copy(table[:, ROWS_AT_COL:PADS_AT_COL], slot_row)
                dve.tensor_copy(table[:, PADS_AT_COL:], counts[:, :]).then_inc(table_ready, 1)

            def take_state(j, s, first):
                dve.wait_ge(turned, j + 1)
                if not (first and s < 2):
                    dve.wait_ge(up_ready, j - 1)
                dve.tensor_copy(state[:, s % 2, :], turned_ps[s % 2][:, 0:P]).then_inc(state_ready, 1)

            def multiply_slot(j, s, first):
                dve.wait_ge(slot_silu, j + 1)
                if not (first and s < 2):
                    dve.wait_ge(act_turned, j - 1)
                dve.tensor_tensor(act_row[:, s % 2, :], silu_row[:, s % 2, :], up_ps[:, s % 2, HID:2 * HID],
                                  ALU.mult).then_inc(slot_prod, 1)

            def gate_result(it, s):
                j = it * UNROLL + s
                dve.wait_ge(result_ready, j + 1)
                if has(it, 1) or s >= OUT_RING:
                    dve.wait_ge(results_out[s % OUT_RING], 16 * (it * (UNROLL // OUT_RING) + s // OUT_RING))
                row = rows[:, s % ROWS_RING, :]
                dve.tensor_tensor(y_dest[:, s % OUT_RING:s % OUT_RING + 1], row[:, D + 1:D + 2],
                                  const["dest"][:, bass.ds(j, 1)], ALU.min)
                dve.tensor_scalar(y_row[:, s % OUT_RING, :], result_ps[:, s % 2, 0:D], row[:, D:D + 1], None,
                                  ALU.mult).then_inc(y_ready, 1)

            def slots(it, first=False, last=False):
                for s in range(UNROLL):
                    j = it * UNROLL + s
                    multiply_slot(j, s, first)
                    if not (last and s >= UNROLL - 2):
                        take_state(j + 2, s + 2, first)
                    if s >= 2:
                        gate_result(it, s - 2)
                    elif not first:
                        gate_result(it - 1, UNROLL - 2 + s)

            def add_parts(n):
                m = n % 2
                dve.wait_ge(parts_in[m], 16 * TOPK * (n // 2 + 1))
                link(dve.tensor_tensor(base[:, n, :], base[:, n, :], parts[:, m, 0, :], ALU.add))
                dve.tensor_tensor(base[:, n, :], base[:, n, :], parts[:, m, 1, :], ALU.add).then_inc(summed, 1)

            dve.memset(xpow[0:32, :], 1.0)
            dve.memset(choices[:, :], 0.0)
            dve.memset(table[:, 0:TABLE_LEAD], 0)
            dve.wait_ge(cond_in, 8 * 16)
            link(dve.tensor_tensor(ypow[:, 1, :], ypow[:, 0, :], ypow[:, 0, :], ALU.mult))
            dve.tensor_tensor(xpow[64:96, :], xpow[64:96, :], xpow[64:96, :], ALU.mult)
            for c in range(3):
                link(dve.tensor_scalar(scond[:, c, :], ypow[:, 0, :], coef[:, 3 + c:4 + c], coef[:, c:c + 1], ALU.mult, ALU.add))
            for c in range(3):
                link(dve.scalar_tensor_tensor(out=scond[:, c, :], in0=ypow[:, 1, :], scalar=coef[:, 6 + c:7 + c],
                                              in1=scond[:, c, :], op0=ALU.mult, op1=ALU.add))
            dve.wait_ge(consts_in, 16)
            for g in range(3):
                link(dve.tensor_copy(delta[32 * g:32 * g + 32, :], const_sb[32 * g:32 * g + 32, 32 * g:32 * g + 32]))
            for c in (2, 1, 0):
                factor(0, c)
            dve.tensor_copy(ids[:, :, :].rearrange("p t k -> p (t k)"), const["ids"])
            dve.tensor_tensor(sel[:, :, :], ident[:, G_HI:G_HI + E].unsqueeze(2).to_broadcast([P, E, P]),
                              ident[:, G_LO:G_LO + E].unsqueeze(2).to_broadcast([P, E, P]), ALU.add).then_inc(sel_ready, 1)
            dve.wait_ge(small_in, 5 * 16)
            dve.tensor_copy(b2s[0:64, :], b2_raw[0:64, :])
            link(dve.tensor_copy(b2_hi[64:128, :].bitcast(F32R), b2_raw[64:128, :]))
            dve.tensor_tensor(b2s[64:128, :], b2_raw[64:128, :], b2_hi[64:128, :], ALU.subtract).then_inc(sel_ready, 1)
            dve.wait_ge(a_free, 1)
            dve.tensor_copy(hT[:, step_col(STEPS - 1):step_col(STEPS - 1) + B], pcol[:, ROW_H0:ROW_H0 + B]).then_inc(h_done, 1)
            dve.tensor_scalar(wgate1[:, :], pcol[:, ROW_GATE:ROW_GATE + E], pcol[:, ROW_LNS:ROW_LNS + 1], None, ALU.mult)
            dve.tensor_scalar(lnb_tile[:, :], const["ones"], pcol[:, ROW_LNB:ROW_LNB + 1], None, ALU.mult).then_inc(pcol_ready, 1)
            for c in (2, 1, 0):
                condition(0, c)
            for e in range(E):
                cols_e = slice(e * HID, (e + 1) * HID)
                dve.wait_ge(w1_cast, e + 1)
                dve.tensor_tensor(w1_lo[:, cols_e], w1_raw[:, cols_e], w1_hi[:, cols_e].bitcast(F32),
                                  ALU.subtract).then_inc(w1_split, 1)
            dve.wait_ge(cleared, 3)
            logits0(0)
            dve.wait_ge(a_free, a_use(0) + 5)
            less_maximum(0, first)
            first_choice(0, first)
            second_choice(first)
            exps(0, first)
            gates(first)
            gates0(0)
            for c in (2, 1, 0):
                factor(1, c)
            dve.wait_ge(b_ready, 1)
            dve.tensor_copy(gate_b1[:, :], bank_b[:, 0:E]).then_inc(b_free, 1)

            link.at(link.base + link.n)
            for i in range(3):
                body0(i)
                link.at(link.base + link.n)
            start, per = link.base, LOOP_LINKS
            with dve.Fori(3, NB - 2) as i:
                link.at(start + per * (i - 3))
                body0(i)
                assert link.n == per, link.n
            link.at(start + per * (NB - 5))
            body0(NB - 2)
            body0(NB - 1, last=True)
            tail()
            make_table()
            take_state(0, 0, True)
            take_state(1, 1, True)
            slots(0, first=True)
            with dve.Fori(1, SLOTS // UNROLL - 1) as it:
                slots(it)
            slots(SLOTS // UNROLL - 1, last=True)
            gate_result(SLOTS // UNROLL - 1, UNROLL - 2)
            gate_result(SLOTS // UNROLL - 1, UNROLL - 1)
            for n in range(NB):
                add_parts(n)

        @block.tensor
        def _(pe):
            def mm(dst, w, v, start=True, stop=True, **kw):
                return nc.tensor.matmul(dst, w, v, start=start, stop=stop, **kw)

            def turn(bank, tiles, ready):
                for t, tile in enumerate(tiles):
                    ins = nc.tensor.transpose(bank[:, t * P:(t + 1) * P], tile, ident)
                ins.then_inc(ready, 1)

            def input_block(n):
                pe.wait_ge(x_in, 64 * (n + 1))
                pe.wait_ge(a_free, a_use(n))
                turn(bank_a, [xin[:, t * P:(t + 1) * P] for t in range(NT)], a_ready)

            def factor_product(n, c):
                pe.wait_ge(sfac_ready, 3 * n + 3 - c)
                pe.wait_ge(a_free, a_use(n) + 3 - c)
                mm(bank_a, xpow[:, :], sfac[:, c, :]).then_inc(a_ready, 1)

            def logits0(n):
                pe.wait_ge(z_split, n + 1)
                pe.wait_ge(a_free, a_use(n) + 4)
                for t in range(NT):
                    ins = mm(bank_a[:, t * E:(t + 1) * E], z[:, t * P:(t + 1) * P], wgate0[:, :])
                ins.then_inc(a_ready, 1)

            def turn_gates(n):
                pe.wait_ge(gates_ready, n + 1)
                pe.wait_ge(a_free, a_use(n) + 5)
                turn(bank_a, [gates3[:, t, :] for t in range(NT)], a_ready)

            def spread_gate(i, e):
                g = E * i + e
                if e == 0:
                    pe.wait_ge(a_free, a_use(i) + 6)
                if has(g, 1):
                    pe.wait_ge(gate_copied, g)
                mm(gate_ps, sel[:, e, :], gT[:, slot(i)]).then_inc(gate_ready, 1)

            def hidden0(i, u):
                k = U0 * i + u
                if u == 0:
                    pe.wait_ge(z_split, i + 1)
                if isinstance(i, int) and i == 0 and u % NC == 0:
                    pe.wait_ge(w1_split, u // NC + 1)
                if has(k, 2):
                    pe.wait_ge(gelu_done, k + 1 - 2)
                w = slice(u * P, (u + 1) * P)
                dst = hidden[:, u % 2, :]
                mm(dst, w1_hi[:, w], in_hi[:, slot(i)], stop=False)
                mm(dst, w1_hi[:, w], in_lo[:, slot(i)], start=False, stop=False)
                mm(dst, w1_lo[:, w], in_hi[:, slot(i)], start=False).then_inc(hid_ready, 1)

            def down0(i, u):
                k = U0 * i + u
                if u == 0:
                    if isinstance(i, int) and i == 0:
                        pe.wait_ge(w2_split, NC)
                    if has(i, 2):
                        pe.wait_ge(acc_taken, i - 1)
                    mm(acc_of(i), b2s[:, :], gT[:, slot(i)], stop=False)
                w = slice(u * P, (u + 1) * P)
                wait_high(pe, i, u)
                mm(acc_of(i), w2_hi[:, w], h_hi[:, u % RING, :], start=False, stop=False)
                mm(acc_of(i), w2_lo[:, w], h_hi[:, u % RING, :], start=False, stop=False)
                pe.wait_ge(lo_done, k + 1)
                mm(acc_of(i), w2_hi[:, w], h_lo[:, u % RING, :], start=False, stop=(u == U0 - 1)).then_inc(down_done, 1)

            def rnn_input(n):
                pe.wait_ge(acc_taken, n + 1)
                pe.wait_ge(h_done, STEPS * n + 1)
                mm(rnn_ps, wx[:, :], xT[:, cols(n)], stop=False, skip_group_check=True)

            def rnn_step(n, s):
                pe.wait_ge(h_done, STEPS * n + s + 1)
                prev = hT[:, hcols(n, step_col(s - 1), B)] if s else hT[:, hcols(n - 1, step_col(STEPS - 1), B)]
                mm(rnn_ps[:, step_col(s):step_col(s) + B], wh[:, :], prev, start=False, stop=True,
                   skip_group_check=True).then_inc(rnn_ready, 1)

            def center_state(n):
                pe.wait_ge(h_done, STEPS * (n + 1) + 1)
                pe.wait_ge(b_free, b_use(n))
                mm(bank_b, const["center"], hT[:, hcols(n)]).then_inc(b_ready, 1)

            def logits1(n):
                pe.wait_ge(b_free, b_use(n) + 1)
                for t in range(NT):
                    mm(bank_b[:, t * E:(t + 1) * E], hc[:, t * P:(t + 1) * P], wgate1[:, :])
                    ins = mm(bank_b[:, NT * E + t:NT * E + t + 1], hc2[:, t * P:(t + 1) * P], const["mean"])
                ins.then_inc(b_ready, 1)

            def state_rows(n):
                pe.wait_ge(b_free, b_use(n) + 2)
                turn(bank_b, [state_tile[:, t * P:(t + 1) * P] for t in range(NT)], b_ready)

            def ranks(n):
                pe.wait_ge(chosen_ready, n + 1)
                pe.wait_ge(b_free, b_use(n) + 3)
                dst = bank_b[:, 0:NT * E]
                mask = rt["mask"][:, second, :].rearrange("p t e -> p (t e)")
                mm(dst, const["tri"], mask, stop=False, skip_group_check=True)
                for t in range(1, NT):
                    mm(dst[:, t * E:], const["ones"], mask[:, 0:(NT - t) * E], start=False, stop=False, skip_group_check=True)
                mm(dst.rearrange("p (t e) -> p t e", e=E), const["ones"], choices[:, :].unsqueeze(1).to_broadcast([P, NT, E]),
                   start=False, skip_group_check=True).then_inc(b_ready, 1)

            def body0(i, last=False):
                for u in range(U0):
                    hidden0(i, u)
                    if u % NC == 0:
                        spread_gate(i, u // NC)
                    if not last:
                        if u == XT_AT:
                            input_block(i + 1)
                        if u in P_AT:
                            factor_product(i + 1, P_AT[u])
                        if u == LOGIT_AT:
                            logits0(i + 1)
                        if u == GT_AT:
                            turn_gates(i + 1)
                    if has(i, 2):
                        if u == CENTER_AT:
                            center_state(i - 2)
                        if u == LOGIT1_AT:
                            logits1(i - 2)
                        if u == ROWS_AT:
                            state_rows(i - 2)
                    if has(i, 3) and u == RANK_AT:
                        ranks(i - 3)
                    if has(i, 1) and u == XP_AT:
                        rnn_input(i - 1)
                    if u >= LAG:
                        down0(i, u - LAG)
                    elif has(i, 1):
                        down0(i - 1, U0 - LAG + u)
                    if has(i, 2) and u < XP_AT:
                        rnn_step(i - 2, HEAD + u)
                    if has(i, 1) and u >= XP_AT:
                        rnn_step(i - 1, u - XP_AT)

            def pair(w):
                n, c = divmod(w, NC)
                pe.wait_ge(q_split, n + 1)
                if w == 0:
                    pe.wait_ge(gelu_done, U0 * NB)
                    pe.wait_ge(shared_split, 1)
                elif w == 1:
                    pe.wait_ge(gate_copied, E * NB)
                    pe.wait_ge(a_free, a_use(NB))
                else:
                    pe.wait_ge(prod_done, w + 1 - 2)
                for part, dst in enumerate(pair_ps[w % 2]):
                    mm(dst, shared(sw_hi, part, c), in_hi[:, slot(n)], stop=False)
                    mm(dst, shared(sw_hi, part, c), in_lo[:, slot(n)], start=False, stop=False)
                    ins = mm(dst, shared(sw_lo, part, c), in_hi[:, slot(n)], start=False)
                ins.then_inc(pair_ready, 1)

            def down1(w):
                n, c = divmod(w, NC)
                if c == 0:
                    pe.wait_ge(acc_taken, n + 1)
                    if n < 2:
                        pe.wait_ge(acc_taken, NB - 1 + n)
                    else:
                        pe.wait_ge(base_done, n - 1)
                pe.wait_ge(hi1_done, w + 1)
                pe.wait_ge(lo1_done, w + 1)
                for t in range(NT):
                    dst = acc[:, n % 2, t * P:(t + 1) * P]
                    tile = slice(t * P, (t + 1) * P)
                    if c == 0:
                        mm(dst, xT[:, n * BLK + t * P:n * BLK + (t + 1) * P], ident, start=(t == 0), stop=False, skip_group_check=True)
                    mm(dst, h_hi[:, w % RING, tile], shared(sw_hi, 2, c), start=False, stop=False, skip_group_check=True)
                    mm(dst, h_hi[:, w % RING, tile], shared(sw_lo, 2, c), start=False, stop=False, skip_group_check=True)
                    ins = mm(dst, h_lo[:, w % RING, tile], shared(sw_hi, 2, c), start=False, stop=(c == NC - 1), skip_group_check=True)
                ins.then_inc(down1_done, 1)

            def tail():
                for w in range(W1):
                    pair(w)
                    before6, after6 = TAIL6.get(w, ((), ()))
                    before7, after7 = TAIL7.get(w, ((), ()))
                    for s in before6:
                        rnn_step(NB - 2, s)
                    for s in before7:
                        rnn_step(NB - 1, s)
                    if w < 2:
                        for u in (2 * w, 2 * w + 1):
                            down0(NB - 1, U0 - LAG + u)
                    if w >= 2:
                        down1(w - 2)
                    for s in after6:
                        rnn_step(NB - 2, s)
                    for s in after7:
                        rnn_step(NB - 1, s)
                    if w == TAIL_XP:
                        rnn_input(NB - 1)
                    if w in TAIL_CENTER:
                        center_state(TAIL_CENTER[w])
                    if w in TAIL_LOGIT:
                        logits1(TAIL_LOGIT[w])
                        state_rows(TAIL_LOGIT[w])
                    if w in TAIL_RANK:
                        ranks(TAIL_RANK[w])
                down1(W1 - 2)
                down1(W1 - 1)
                ranks(NB - 1)
                pe.wait_ge(pos_ready, NB)
                pe.wait_ge(b_free, b_use(NB))
                mm(bank_b[:, 0:E], const["ones"], choices[:, :]).then_inc(b_ready, 1)

            def turn_rows(it, s):
                it, s = (it, s) if s < UNROLL else (it + 1, s - UNROLL)
                j = it * UNROLL + s
                pe.wait_ge(rows_in[s], 16 * (it + 1))
                if has(it, 1) or s >= 2:
                    pe.wait_ge(state_ready, j - 1)
                nc.tensor.transpose(turned_ps[s % 2][:, 0:P], rows[:, s, 0:D], ident).then_inc(turned, 1)

            def gate_and_up(j, s, e, first):
                pe.wait_ge(state_ready, j + 1)
                if not (first and s < 2):
                    pe.wait_ge(slot_prod, j - 1)
                mm(up_ps[:, s % 2, :], state[:, s % 2, :], wgu[:, bass.ds(e * 2 * HID, 2 * HID)]).then_inc(up_ready, 1)

            def turn_act(j, s, first):
                pe.wait_ge(slot_prod, j + 1)
                if not (first and s < 2):
                    pe.wait_ge(act_copied, j - 1)
                turn(act_turned_ps[s % 2], [act_row[:, s % 2, c * P:(c + 1) * P] for c in range(NC)], act_turned)

            def slot_down(j, s, e, first):
                pe.wait_ge(act_copied, j + 1)
                if not (first and s < 2):
                    pe.wait_ge(y_ready, j - 1)
                for c in range(NC):
                    ins = mm(result_ps[:, s % 2, 0:D], act_col[:, s % 2, c * P:(c + 1) * P],
                             wd[:, bass.ds(e * HID + c * P, P)], start=(c == 0), stop=(c == NC - 1))
                ins.then_inc(result_ready, 1)

            def slots(it, first=False, last=False):
                experts = table_values(pe, it * UNROLL, UNROLL + 2, E - 1)
                for s in range(UNROLL):
                    j = it * UNROLL + s
                    if not (last and s >= UNROLL - 2):
                        turn_rows(it, s + 2)
                    gate_and_up(j, s, experts[s + 2], first)
                    if not (first and s < 1):
                        turn_act(j - 1, (s - 1) % UNROLL, first)
                    if not (first and s < 2):
                        slot_down(j - 2, (s - 2) % UNROLL, experts[s], first)
                return experts

            pe.wait_ge(consts_in, 16)
            pe.wait_ge(params_in, 6 * 16)
            nc.tensor.transpose(bank_a[:, 0:P], prow[:, :], ident).then_inc(a_ready, 1)
            input_block(0)
            for c in (2, 1, 0):
                factor_product(0, c)
            pe.wait_ge(small_in, 5 * 16)
            logits0(0)
            turn_gates(0)
            pe.wait_ge(pcol_ready, 1)
            mm(bank_b[:, 0:E], lnb_tile[:, :], pcol[:, ROW_GATE:ROW_GATE + E]).then_inc(b_ready, 1)
            pe.wait_ge(sel_ready, 2)
            pe.wait_ge(rnn_w_in, 32)
            for i in range(3):
                body0(i)
            with pe.Fori(3, NB - 1) as i:
                body0(i)
            body0(NB - 1, last=True)
            tail()
            pe.wait_ge(base_done, NB)
            pe.wait_ge(prod_done, W1)
            pe.wait_ge(h_done, STEPS * NB + 1)
            pe.wait_ge(b_free, b_use(NB) + 1)
            pe.wait_ge(table_ready, 1)
            pe.wait_ge(wgu_in, 32)
            pe.wait_ge(wd_in, 32)
            turn_rows(0, 0)
            turn_rows(0, 1)
            slots(0, first=True)
            with pe.Fori(1, SLOTS // UNROLL - 1) as it:
                slots(it)
            experts = slots(SLOTS // UNROLL - 1, last=True)
            turn_act(SLOTS - 1, UNROLL - 1, False)
            slot_down(SLOTS - 2, UNROLL - 2, experts[UNROLL], False)
            slot_down(SLOTS - 1, UNROLL - 1, experts[UNROLL + 1], False)


INPUTS = ("x", "fside_BxS_0", "cond_1024", "L0_cond_coeffs", "L0_ffn_Wg", "L0_ffn_bg", "L0_ffn_W1", "L0_ffn_b1",
          "L0_ffn_W2", "L0_ffn_b2", "L1_cond_Wx", "L1_cond_Wh", "L1_cond_b", "L1_ffn_ln_scale", "L1_ffn_ln_bias",
          "L1_ffn_gate_w", "L1_ffn_Wg", "L1_ffn_Wu", "L1_ffn_Wd", "L1_ffn_sWg", "L1_ffn_sWu", "L1_ffn_sWd")


def kernel(**inputs):
    import numpy as np
    import concourse.bacc as bacc
    from concourse.bass_utils import run_bass_kernel_spmd

    nc = bacc.Bacc("TRN2", target_bir_lowering=False, num_devices=1)
    arrays, args = {}, []
    for name, a in [("consts", constant_tables())] + [(n, np.ascontiguousarray(inputs[n])) for n in INPUTS]:
        arrays[f"in_{name}"] = a
        args.append(nc.dram_tensor(f"in_{name}", a.shape, mybir.dt.from_np(a.dtype), kind="ExternalInput").ap())
    out = nc.dram_tensor("out", (B, T, D), F32, kind="ExternalOutput").ap()
    build(nc, *args, out)
    result = run_bass_kernel_spmd(nc, [arrays], core_ids=[0])
    return result.results[0]["out"]
```

```python
from contextlib import ExitStack

import concourse.bass as bass
from concourse import mybir

ALU = mybir.AluOpType
ACT = mybir.ActivationFunctionType
F32 = mybir.dt.float32
F32R = mybir.dt.float32r
I32 = mybir.dt.int32
U32 = mybir.dt.uint32
AX_X = mybir.AxisListType.X

P = 128
B, T, D = 32, 128, 128
E, HID, TOPK = 8, 256, 2
NC = HID // P
STEPS = 16
BLK = STEPS * B
TOK = T * B
NB = TOK // BLK
NT = BLK // P
U0 = E * NC
W1 = NB * NC
LAG = 4
RING = 4
TEMP = 5.0
EPS0, EPS1, LN_EPS = 1e-9, 1e-5, 1e-5
NEG = -3.0e38

ROW_GATE, ROW_B1, ROW_LNS, ROW_LNB, ROW_CB, ROW_H0 = 0, 8, 24, 25, 26, 32
G_HI, G_LO, G_HI2 = 0, 32, 64

REGION = TOK + P
ROW = D + 2
SLOTS = TOPK * TOK // P + E
PAD_ROWS = E * REGION
PAD_DEST = 1.0e6
ROWS_RING, OUT_RING = 8, 4
UNROLL = 8
assert UNROLL == ROWS_RING
TABLE_LEAD = 2
ROWS_AT_COL = TABLE_LEAD + SLOTS
PADS_AT_COL = ROWS_AT_COL + SLOTS

CONSTS = {}
for _name, _size in (("ident", P), ("tri", P), ("ones", P), ("center", P), ("ramp", E), ("region", E), ("ids", NT * TOPK),
                     ("dest", SLOTS), ("full", TOK // P), ("upto", E * E), ("slot", SLOTS), ("mean", 1), ("power", NT), ("pad", ROW)):
    CONSTS[_name] = slice(sum(s.stop - s.start for s in CONSTS.values()),
                          sum(s.stop - s.start for s in CONSTS.values()) + _size)
CONST_COLS = CONSTS["pad"].stop

XT_AT, LOGIT_AT, GT_AT = 0, 8, 15
P_AT = {1: 2, 3: 1, 5: 0}
S_AT = {13: 2, 14: 1, 15: 0}
CENTER_AT, LOGIT1_AT, ROWS_AT, RANK_AT = 5, 8, 13, 0
LOGITS_IN, LOGITS_DONE, FIRST_CHOICE, SECOND_CHOICE, EXPS, GATES, META = 8, 9, 10, 10, 11, 12, 13
SPLIT_AT = 6
XP_AT = 5
HEAD = U0 - XP_AT
SCATTER_AT = (3, 4, 5, 6, 7, 8, 9, 10)

TAIL_STEPS = {0: tuple((NB - 2, s) for s in (11, 12, 13, 14)), 1: ((NB - 2, 15), None, None, None), 2: (None, None, (NB - 1, 0), (NB - 1, 1)),
              6: ((NB - 1, 14), (NB - 1, 15), None, None)}
for _w in range(3, 6):
    TAIL_STEPS[_w] = tuple((NB - 1, 4 * (_w - 3) + _k) for _k in (2, 3, 4, 5))
NO_STEPS = (None,) * 4
TAIL_XP = 2
TAIL_CENTER = {2: NB - 2, 7: NB - 1}
TAIL_LOGIT = {3: NB - 2, 8: NB - 1}
TAIL_ROWS = {4: NB - 2, 9: NB - 1}
TAIL_RANK = {1: NB - 3, 6: NB - 2, 11: NB - 1}
TAIL_COUNTS = 14
LOOP_LINKS = 28


def a_use(n):
    return 1 + 6 * n


def b_use(n):
    return 1 + 4 * n


def step_col(s):
    return (s % 4) * P + (s // 4) * B


def has(i, first):
    return not isinstance(i, int) or i >= first


class Chain:

    def __init__(self, eng, sem):
        self.eng, self.sem, self.base, self.n = eng, sem, 0, 0

    def __call__(self, ins):
        self.n += 1
        ins.then_inc(self.sem, 1)
        self.eng.wait_ge(self.sem, self.base + self.n)

    def at(self, base):
        self.base, self.n = base, 0


def constant_tables():
    import numpy as np
    p, c = np.arange(P)[:, None], np.zeros((P, CONST_COLS), np.float32)
    c[:, CONSTS["ident"]] = np.eye(P)
    c[:, CONSTS["tri"]] = p < np.arange(P)
    c[:, CONSTS["ones"]] = 1.0
    c[:, CONSTS["center"]] = np.eye(P) - 1.0 / D
    c[:, CONSTS["ramp"]] = E - np.arange(E)
    c[:, CONSTS["region"]] = REGION * np.arange(E)
    k = np.arange(NT * TOPK)
    c[:, CONSTS["ids"]] = p * NT + k // TOPK + (k % TOPK) * TOK
    c[:, CONSTS["dest"]] = TOPK * TOK + P * np.arange(SLOTS) + p
    c[:, CONSTS["full"]] = P * np.arange(TOK // P)
    c[:, CONSTS["upto"]] = np.tril(np.ones((E, E))).reshape(-1)
    c[:, CONSTS["slot"]] = np.arange(SLOTS)
    c[:, CONSTS["mean"]] = 1.0 / D
    c[:, CONSTS["power"]] = -0.5
    c[:, CONSTS["pad"].stop - 1] = PAD_DEST
    return c


def build(nc, consts, x, fside_BxS_0, cond_1024, L0_cond_coeffs, L0_ffn_Wg, L0_ffn_bg, L0_ffn_W1, L0_ffn_b1,
          L0_ffn_W2, L0_ffn_b2, L1_cond_Wx, L1_cond_Wh, L1_cond_b, L1_ffn_ln_scale, L1_ffn_ln_bias,
          L1_ffn_gate_w, L1_ffn_Wg, L1_ffn_Wu, L1_ffn_Wd, L1_ffn_sWg, L1_ffn_sWu, L1_ffn_sWd, out):
    regions = nc.dram_tensor("regions", (PAD_ROWS + P, ROW), F32, kind="Internal").ap()
    results = nc.dram_tensor("results", (TOPK * TOK + SLOTS * P, D), F32, kind="Internal").ap()
    with ExitStack() as ctx:
        def sb(name, shape, dt=F32):
            return ctx.enter_context(nc.sbuf_tensor(name, shape, dt))

        def sem(name):
            return ctx.enter_context(nc.semaphore(name))

        banks = ctx.enter_context(nc.psum_tensor("banks", [P, 8, BLK], F32))
        hidden, acc = banks[:, 0:2, :], banks[:, 2:4, :]
        gate_ps, bank_a, rnn_ps, bank_b = (banks[:, n, :] for n in (4, 5, 6, 7))
        pair_ps = ((banks[:, 0, :], banks[:, 1, :]), (gate_ps, bank_a))
        up_ps, result_ps = hidden, acc
        turned_ps, act_turned_ps = (gate_ps, bank_a), (rnn_ps, bank_b)

        split_w = sb("split_w", [P, 4 * U0 * P], F32R)
        w1_hi, w1_lo, w2_hi, w2_lo = (split_w[:, k * U0 * P:(k + 1) * U0 * P] for k in range(4))
        wgu_hi, wgu_lo = split_w[:, 0:2 * U0 * P], split_w[:, 2 * U0 * P:4 * U0 * P]
        wgu, wd = sb("wgu", [P, E * 2 * HID]), sb("wd", [P, E * HID])
        sw_raw = sb("sw_raw", [P, 3 * HID])
        sw_hi, sw_lo = sb("sw_hi", [P, 2 * HID], F32R), sb("sw_lo", [P, 2 * HID], F32R)
        wx, wh = sb("wx", [P, P]), sb("wh", [P, P])
        wgate0, gate_b0 = sb("wgate0", [P, E]), sb("gate_b0", [P, E])
        gate_b1, wgate1 = sb("gate_b1", [P, E]), sb("wgate1", [P, E])
        b2_raw, b2_hi, b2s = sb("b2_raw", [P, P]), sb("b2_hi", [P, P]), sb("b2s", [P, P], F32R)
        prow, pcol = sb("prow", [P, P]), sb("pcol", [P, P])
        const_sb = sb("const_sb", [P, CONST_COLS])
        const = {k: const_sb[:, s] for k, s in CONSTS.items()}
        ident = const["ident"]
        lnb_tile, sel = sb("lnb_tile", [P, P]), sb("sel", [P, E, P], F32R)
        coef, xpow = sb("coef", [96, 9]), sb("xpow", [96, D])
        ypow, scond = sb("ypow", [96, 2, T]), sb("scond", [96, 3, T])
        delta, sfac = sb("delta", [96, B]), sb("sfac", [96, 3, BLK])
        prep = sb("prep", [P, 3 * BLK])
        xin, zt, z = (prep[:, k * BLK:(k + 1) * BLK] for k in range(3))
        xT = sb("xT", [P, NB * BLK])
        hT = sb("hT", [P, (NB + 1) * BLK])
        base = sb("base", [P, NB, BLK])
        in_hi, in_lo = sb("in_hi", [P, 2 * BLK], F32R), sb("in_lo", [P, 2 * BLK], F32R)
        gT = sb("gT", [P, 2 * BLK], F32R)
        gates3 = sb("gates3", [P, NT, P])
        gate_sb = sb("gate_sb", [P, 2, BLK])
        actv, gated = sb("actv", [P, RING, BLK]), sb("gated", [P, RING, BLK])
        h_hi, h_lo = sb("h_hi", [P, RING, BLK], F32R), sb("h_lo", [P, RING, BLK], F32R)
        hc, hc2 = sb("hc", [P, BLK]), sb("hc2", [P, BLK])
        rt = {k: sb("rt_" + k, [P, 2 * NT, E]) for k in
              ("logit", "d", "score", "one1", "d2", "two", "mask", "th", "num", "den", "e", "g", "gate")}
        rs = {k: sb("rs_" + k, [P, 2 * NT]) for k in ("m1", "s1", "m2", "s2", "sum", "top", "den", "inv")}
        first, second, both = slice(0, NT), slice(NT, 2 * NT), slice(0, 2 * NT)
        var, rstd = sb("var", [P, NT]), sb("rstd", [P, NT])
        rank, picks = sb("rank", [P, NT, E]), [sb(f"pick{k}", [P, NT, E]) for k in range(TOPK)]
        choices, new_choices = sb("choices", [P, E]), sb("new_choices", [P, E])
        ids, pos_f = sb("ids", [P, NT, TOPK]), sb("pos_f", [P, NT, TOPK])
        hrow_last = prep[:, 0:NT * TOPK * ROW].rearrange("p (t k c) -> p t k c", t=NT, k=TOPK)
        hrows = [sb("hrow", [P, NT, TOPK, ROW]), hrow_last]
        poss = [sb(f"pos{k}", [P, NT, TOPK], U32) for k in range(2)]
        counts, ends, blocks = sb("counts", [P, E]), sb("ends", [P, E]), sb("blocks", [P, E])
        table = sb("table", [P, PADS_AT_COL + E], I32)
        def carve(buf, *shapes):
            at = 0
            for shape in shapes:
                size = shape[0] * shape[1]
                yield buf[:, at:at + size].rearrange("p (a b) -> p a b", a=shape[0])
                at += size

        filled, upto_v, passed, per_slot = carve(xT, (E, TOK // P), (E, E), (SLOTS, E), (3, SLOTS))
        slot_e, slot_row, starts = (per_slot[:, k, :] for k in range(3))
        rows, silu_row, act_row, act_col, y_row = carve(hT, (ROWS_RING, ROW), (2, HID), (2, HID), (2, HID), (OUT_RING, D))
        state_hi, state_lo = (w.rearrange("p (a b) -> p a b", a=2) for w in (in_hi[:, 0:2 * P], in_lo[:, 0:2 * P]))
        y_dest = sb("y_dest", [P, OUT_RING], U32)
        parts = split_w.bitcast(F32).rearrange("p (n k t) -> p n k t", n=NB, k=TOPK)
        state_tile = sw_raw[:, 0:BLK]
        w1_raw, w2_raw = (base.rearrange("p n t -> p (n t)")[:, k * U0 * P:(k + 1) * U0 * P] for k in range(2))

        (consts_in, params_in, cond_in, w1_in, w2_in, wgu_in, wd_in, shared_in, small_in, rnn_w_in, x_in, pads_done,
         scattered, y_out) = [
            sem(s) for s in ("consts_in", "params_in", "cond_in", "w1_in", "w2_in", "wgu_in", "wd_in", "shared_in",
                             "small_in", "rnn_w_in", "x_in", "pads_done", "scattered", "y_out")]
        (cleared, sel_ready, sfac_ready, pcol_ready, w1_cast, w1_split, w2_cast, w2_split, shared_cast, shared_split) = [
            sem(s) for s in ("cleared", "sel_ready", "sfac_ready", "pcol_ready", "w1_cast", "w1_split", "w2_cast",
                             "w2_split", "shared_cast", "shared_split")]
        (a_ready, a_free, b_ready, b_free, hid_ready, gate_ready, gate_copied, down_done, acc_taken, rnn_ready, h_done) = [
            sem(s) for s in ("a_ready", "a_free", "b_ready", "b_free", "hid_ready", "gate_ready", "gate_copied",
                             "down_done", "acc_taken", "rnn_ready", "h_done")]
        (gelu_done, gated_done, hi_act, hi_dve, lo_done, z_split, d_ready, th_ready, gates_ready) = [
            sem(s) for s in ("gelu_done", "gated_done", "hi_act", "hi_dve", "lo_done", "z_split", "d_ready", "th_ready",
                             "gates_ready")]
        (var_ready, rstd_ready, chosen_ready, pos_ready, table_ready) = [
            sem(s) for s in ("var_ready", "rstd_ready", "chosen_ready", "pos_ready", "table_ready")]
        (q_cast, q_split, pair_ready, silu_done, prod_done, down1_done, base_done, wgu_cast, wgu_split, high_ready) = [
            sem(s) for s in ("q_cast", "q_split", "pair_ready", "silu_done", "prod_done", "down1_done", "base_done",
                             "wgu_cast", "wgu_split", "high_ready")]
        (turned, state_ready, up_ready, slot_silu, slot_prod, act_turned, act_copied, result_ready, y_ready, summed) = [
            sem(s) for s in ("turned", "state_ready", "up_ready", "slot_silu", "slot_prod", "act_turned", "act_copied",
                             "result_ready", "y_ready", "summed")]
        rows_in = [sem(f"rows_in{s}") for s in range(ROWS_RING)]
        results_out = [sem(f"results_out{s}") for s in range(OUT_RING)]
        parts_in = [sem(f"parts_in{n}") for n in range(NB)]
        dve_chain, scatter_go = sem("dve_chain"), sem("scatter_go")

        def cols(n):
            return bass.ds(n * BLK, BLK)

        def hcols(n, off=0, size=BLK):
            return bass.ds((n + 1) * BLK + off, size)

        def slot(n):
            return bass.ds((n % 2) * BLK, BLK)

        def acc_of(n):
            return acc.rearrange("p a n -> p (a n)")[:, slot(n)]

        def table_values(eng, at, count, most):
            return nc.values_load_multi_w_load_instructions(
                table[0:1, bass.ds(at, count)], engines=[eng.engine], min_val=0, max_val=most,
                skip_runtime_bounds_check_because="the vector engine clamped the table's values")[1]

        def wait_high(eng, i, u):
            eng.wait_ge(hi_dve if u % 2 else hi_act, U0 // 2 * i + u // 2 + 1)

        def layers_of(i, last):
            return not last, has(i, 2)

        def own(n):
            return 1 if isinstance(n, int) and n == NB - 1 else 0

        def shared(w, part, c):
            return w[:, part * HID + c * P:part * HID + (c + 1) * P]

        x_rows = x.rearrange("b (n q r) d -> n q b (r d)", n=NB, q=4)
        y_rows = out.rearrange("b (n q r) d -> n q b (r d)", n=NB, q=4)
        result_rows = results[0:TOPK * TOK, :].rearrange("(k n p r) d -> k n p (r d)", k=TOPK, n=NB, r=NT)
        block = ctx.enter_context(nc.Block())

        @block.sync
        def _(sp):
            def load_x(n):
                for q in range(4):
                    src = x_rows[n, q] if isinstance(n, int) else x_rows[bass.ds(n, 1), q].squeeze(0)
                    sp.dma_start(xin[q * B:(q + 1) * B, :], src).then_inc(x_in, 16)

            def load_rows(it, reused):
                first_rows = table_values(sp, ROWS_AT_COL + it * UNROLL, UNROLL, PAD_ROWS)
                for s, row in enumerate(first_rows):
                    if reused:
                        sp.wait_ge(y_ready, (it - 1) * UNROLL + s + 1)
                    sp.dma_start(rows[:, s, :], regions[bass.ds(row, P), :]).then_inc(rows_in[s], 16)

            sp.dma_start(const_sb[:, :], consts).then_inc(consts_in, 16)
            load_x(0)
            sp.wait_ge(cleared, 2)
            sp.dma_start(prow[ROW_H0:ROW_H0 + B, :], cond_1024).then_inc(params_in, 16)
            sp.dma_start(prow[ROW_B1:ROW_B1 + U0, :], L0_ffn_b1.rearrange("e (c h) -> (e c) h", c=NC)).then_inc(params_in, 16)
            sp.dma_start(prow[ROW_GATE:ROW_GATE + E, :], L1_ffn_gate_w).then_inc(params_in, 16)
            for row, v in ((ROW_LNS, L1_ffn_ln_scale), (ROW_LNB, L1_ffn_ln_bias), (ROW_CB, L1_cond_b)):
                sp.dma_start(prow[row:row + 1, :], v.rearrange("(o d) -> o d", o=1)).then_inc(params_in, 16)
            sp.dma_start(wgate0[:, :], L0_ffn_Wg).then_inc(small_in, 16)
            sp.dma_start(gate_b0[:, :], L0_ffn_bg.rearrange("(o e) -> o e", o=1).partition_broadcast(P).squeeze(1)).then_inc(small_in, 16)
            for row in (G_HI, G_LO, G_HI2):
                sp.dma_start(b2_raw[row:row + E, :], L0_ffn_b2).then_inc(small_in, 16)
            sp.dma_start(wx[:, :], L1_cond_Wx).then_inc(rnn_w_in, 16)
            sp.dma_start(wh[:, :], L1_cond_Wh).then_inc(rnn_w_in, 16)
            sp.wait_ge(a_ready, a_use(0) + 1)
            load_x(1)
            sp.dma_start(sw_raw[:, 0:HID], L1_ffn_sWg).then_inc(shared_in, 16)
            sp.dma_start(sw_raw[:, HID:2 * HID], L1_ffn_sWu).then_inc(shared_in, 16)
            sp.dma_start(sw_raw[:, 2 * HID:].rearrange("p (c d) -> p c d", c=NC), L1_ffn_sWd.rearrange("(c h) d -> h c d", c=NC)).then_inc(shared_in, 16)
            wgu_v = wgu.rearrange("p (e g h) -> p e g h", e=E, g=2)
            sp.dma_start(wgu_v[:, :, 0, :], L1_ffn_Wg.rearrange("e d h -> d e h")).then_inc(wgu_in, 16)
            sp.dma_start(wgu_v[:, :, 1, :], L1_ffn_Wu.rearrange("e d h -> d e h")).then_inc(wgu_in, 16)
            for c in range(NC):
                sp.dma_start(wd.rearrange("p (e c d) -> p e c d", c=NC, d=D)[:, :, c, :],
                             L1_ffn_Wd[:, c * P:(c + 1) * P, :].rearrange("e h d -> h e d")).then_inc(wd_in, 16)
            sp.wait_ge(consts_in, 16)
            sp.dma_start(regions[PAD_ROWS:PAD_ROWS + P, :], const["pad"]).then_inc(pads_done, 16)
            with sp.Fori(2, NB) as n:
                sp.wait_ge(a_ready, a_use(n - 1) + 1)
                load_x(n)
            sp.wait_ge(table_ready, 1)
            for row in table_values(sp, PADS_AT_COL, E, PAD_ROWS - P):
                sp.dma_start(regions[bass.ds(row, P), :], const["pad"]).then_inc(pads_done, 16)
            sp.wait_ge(scattered, 16 * NB * NT * TOPK)
            sp.wait_ge(pads_done, 16 * (E + 1))
            load_rows(0, False)
            with sp.Fori(1, SLOTS // UNROLL) as it:
                load_rows(it, True)
            for landed in results_out:
                sp.wait_ge(landed, 16 * SLOTS // OUT_RING)
            for n in range(NB):
                sp.dma_start(parts[:, n, :, :], result_rows[:, n].rearrange("k p c -> p k c")).then_inc(parts_in[n], 16)
            sp.wait_ge(y_out, NB * 4 * 16)

        @block.gpsimd
        def _(pool):
            pool.memset(prow[:, :], 0.0).then_inc(cleared, 1)
            pool.memset(b2_raw[:, :], 0.0).then_inc(cleared, 1)
            pool.memset(gates3[:, :, :], 0.0).then_inc(cleared, 1)
            pool.wait_ge(consts_in, 16)

            def inv_std(n):
                pool.wait_ge(var_ready, n + 1)
                pool.tensor_tensor(rstd[:, :], var[:, :], const["power"], ALU.pow).then_inc(rstd_ready, 1)

            def scatter(n, t, k):
                if t == 0 and k == 0:
                    pool.wait_ge(b_free, b_use(n) + 3)
                    pool.wait_ge(pos_ready, n + 1)
                    pool.sem_inc(scatter_go, 1)
                pool.indirect_dma_start(regions, bass.IndirectOffsetOnAxis(ap=poss[own(n)][:, t, k:k + 1], axis=0),
                                        hrows[own(n)][:, t, k, :], None).then_inc(scattered, 16)

            def low0(i, u):
                k = U0 * i + u
                wait_high(pool, i, u)
                if has(k, RING):
                    pool.wait_ge(down_done, k + 1 - RING)
                pool.tensor_tensor(h_lo[:, u % RING, :], gated[:, u % RING, :],
                                   h_hi[:, u % RING, :].bitcast(F32), ALU.subtract).then_inc(lo_done, 1)

            def body0(i):
                for u in range(U0):
                    low0(i, u)
                    if has(i, 2) and u == LOGITS_IN - 1:
                        inv_std(i - 2)
                    if has(i, 3) and u in SCATTER_AT:
                        scatter(i - 3, *divmod(SCATTER_AT.index(u), TOPK))

            def scatter_block(n):
                for t in range(NT):
                    if t == NT // 2 and n + 1 < NB:
                        inv_std(n + 1)
                    for k in range(TOPK):
                        scatter(n, t, k)

            for c in range(NC):
                half = slice(c * E * P, (c + 1) * E * P)
                pool.wait_ge(w2_cast, c + 1)
                pool.tensor_tensor(w2_lo[:, half], w2_raw[:, half], w2_hi[:, half].bitcast(F32),
                                   ALU.subtract).then_inc(w2_split, 1)
            for i in range(3):
                body0(i)
            with pool.Fori(3, NB - 1) as i:
                body0(i)
            body0(NB - 1)
            for n in range(NB - 3, NB):
                scatter_block(n)

            def scatter_result(j, s):
                pool.wait_ge(y_ready, j + 1)
                pool.sem_inc(scatter_go, 1)
                pool.indirect_dma_start(results, bass.IndirectOffsetOnAxis(ap=y_dest[:, s:s + 1], axis=0),
                                        y_row[:, s, :], None).then_inc(results_out[s], 16)

            with pool.Fori(0, SLOTS // UNROLL) as it:
                for s in range(UNROLL):
                    scatter_result(it * UNROLL + s, s % OUT_RING)

        @block.scalar
        def _(act):
            for g in range(3):
                part = slice(32 * g, 32 * g + 32)
                act.dma_start(coef[part, :], L0_cond_coeffs[g].rearrange("b c -> (b c)").partition_broadcast(32)).then_inc(cond_in, 16)
                act.dma_start(ypow[part, 0, :], cond_1024).then_inc(cond_in, 16)
                if g:
                    act.dma_start(xpow[part, :], fside_BxS_0).then_inc(cond_in, 16)
            for e0 in (0, E // 2):
                act.dma_start(w1_raw.rearrange("p (e h) -> p e h", e=E)[:, e0:e0 + E // 2, :],
                              L0_ffn_W1[e0:e0 + E // 2].rearrange("e d h -> d e h")).then_inc(w1_in, 16)
            for c in range(NC):
                act.dma_start(w2_raw.rearrange("p (e c d) -> p e c d", c=NC, d=D)[:, :, c, :],
                              L0_ffn_W2[:, c * P:(c + 1) * P, :].rearrange("e h d -> h e d")).then_inc(w2_in, 16)

            def copy_a(use, dst, size=BLK):
                act.wait_ge(a_ready, use + 1)
                nc.scalar.copy(dst, bank_a[:, 0:size]).then_inc(a_free, 1)

            def gelu(i, u):
                k = U0 * i + u
                act.wait_ge(hid_ready, k + 1)
                if has(k, RING):
                    act.wait_ge(gated_done, k + 1 - RING)
                nc.scalar.activation(actv[:, u % RING, :], hidden[:, u % 2, :], ACT.Gelu,
                                     bias=pcol[:, ROW_B1 + u:ROW_B1 + u + 1]).then_inc(gelu_done, 1)

            def copy_gate(i, e):
                g = E * i + e
                act.wait_ge(gate_ready, g + 1)
                if has(g, 2):
                    act.wait_ge(gated_done, U0 * i + NC * (e - 1))
                nc.scalar.copy(gate_sb[:, e % 2, :], gate_ps[:, :]).then_inc(gate_copied, 1)

            def tanh_step(n, s):
                act.wait_ge(rnn_ready, STEPS * n + s + 1)
                nc.scalar.activation(hT[:, hcols(n, step_col(s), B)], rnn_ps[:, step_col(s):step_col(s) + B],
                                     ACT.Tanh, bias=pcol[:, ROW_CB:ROW_CB + 1]).then_inc(h_done, 1)

            def router_tanh(r, layers):
                act.wait_ge(d_ready, r + 1)
                for layer in layers:
                    part, temp = (first, TEMP) if layer == 0 else (second, 1.0)
                    ins = nc.scalar.activation(rt["th"][:, part, :], rt["d"][:, part, :], ACT.Tanh, scale=0.5 / temp)
                ins.then_inc(th_ready, 1)

            def round0(i, u):
                k = U0 * i + u
                act.wait_ge(gated_done, k + 1)
                if has(k, RING):
                    act.wait_ge(down_done, k + 1 - RING)
                nc.scalar.copy(h_hi[:, u % RING, :], gated[:, u % RING, :]).then_inc(hi_act, 1)

            def centered(n):
                act.wait_ge(b_ready, b_use(n) + 1)
                nc.scalar.copy(state_tile, hT[:, hcols(n)])
                nc.scalar.copy(hc[:, :], bank_b[:, :])
                nc.scalar.activation(hc2[:, :], bank_b[:, :], ACT.Square).then_inc(b_free, 1)

            def copy_rows(n):
                act.wait_ge(b_ready, b_use(n) + 3)
                if own(n) == 0 and has(n, 1):
                    act.wait_ge(scattered, 16 * NT * TOPK * n)
                src = bank_b.rearrange("p (t d) -> p t d", t=NT)
                nc.scalar.copy(hrows[own(n)][:, :, 0, 0:D], src)
                nc.scalar.copy(hrows[own(n)][:, :, 1, 0:D], src).then_inc(b_free, 1)

            def cast_state(n):
                act.wait_ge(h_done, STEPS * (n + 1) + 1)
                if n < 2:
                    act.wait_ge(hid_ready, U0 * (NB - 1 + n))
                else:
                    act.wait_ge(pair_ready, NC * (n - 1))
                nc.scalar.copy(in_hi[:, slot(n)], hT[:, hcols(n)]).then_inc(q_cast, 1)

            def body0(i, last=False):
                for u in range(U0):
                    gelu(i, u)
                    if not last and u == U0 - 1:
                        if has(i, 1):
                            act.wait_ge(down_done, U0 * i)
                        copy_a(a_use(i + 1) + 5, gT[:, slot(i + 1)])
                    if u % NC == 0:
                        copy_gate(i, u // NC)
                    else:
                        round0(i, u - 1)
                    if not last and u == XT_AT:
                        copy_a(a_use(i + 1), xT[:, cols(i + 1)])
                    if u == FIRST_CHOICE:
                        router_tanh(i + 1, [k for k in range(2) if layers_of(i, last)[k]])
                    if has(i, 2):
                        if u < XP_AT:
                            tanh_step(i - 2, HEAD + u)
                        if u == CENTER_AT:
                            centered(i - 2)
                    if has(i, 1) and u >= XP_AT:
                        tanh_step(i - 1, u - XP_AT)
                    if has(i, 2) and u == ROWS_AT + 1:
                        copy_rows(i - 2)
                    if isinstance(i, int) and i == 0 and u == SPLIT_AT:
                        act.wait_ge(shared_in, 48)
                        nc.scalar.copy(sw_hi[:, :], sw_raw[:, 0:2 * HID]).then_inc(shared_cast, 1)
                    if last and u == SPLIT_AT:
                        cast_state(0)

            def cast_wgu(e):
                act.wait_ge(wgu_in, 32)
                act.wait_ge(hid_ready, U0 * NB)
                cols_e = slice(e * 2 * HID, (e + 1) * 2 * HID)
                nc.scalar.copy(wgu_hi[:, cols_e], wgu[:, cols_e]).then_inc(wgu_cast, 1)

            def silu(w):
                act.wait_ge(pair_ready, w + 1)
                if w < RING:
                    act.wait_ge(gated_done, U0 * (NB - 1) + U0 - RING + w + 1)
                else:
                    act.wait_ge(prod_done, w + 1 - RING)
                nc.scalar.activation(actv[:, w % RING, :], pair_ps[w % 2][0], ACT.Silu).then_inc(silu_done, 1)

            def copy_base(n):
                act.wait_ge(down1_done, NC * (n + 1))
                nc.scalar.copy(base[:, n, :], acc_of(n)).then_inc(base_done, 1)

            def tail():
                for w in range(W1):
                    steps = [step for step in TAIL_STEPS.get(w, NO_STEPS) if step]
                    for step in steps[0:1]:
                        tanh_step(*step)
                    silu(w)
                    for step in steps[1:]:
                        tanh_step(*step)
                    if w % NC == 0 and w // NC + 1 < NB:
                        cast_state(w // NC + 1)
                    if w in TAIL_CENTER:
                        centered(TAIL_CENTER[w])
                    if w - 1 in TAIL_ROWS:
                        copy_rows(TAIL_ROWS[w - 1])
                    if w - 1 in TAIL_LOGIT:
                        router_tanh(TAIL_LOGIT[w - 1] + 3, [1])
                    if w % NC == 0 and w >= 2 * NC:
                        copy_base(w // NC - 2)
                    if w >= W1 - E:
                        cast_wgu(w - (W1 - E))
                copy_base(NB - 2)
                copy_base(NB - 1)

            def round_turned(j, s, first):
                act.wait_ge(turned, j + 1)
                if not (first and s < 2):
                    act.wait_ge(up_ready, j - 1)
                nc.scalar.copy(state_hi[:, s % 2, :], turned_ps[s % 2][:, 0:P]).then_inc(high_ready, 1)

            def slot_silu_of(j, s, first):
                act.wait_ge(up_ready, j + 1)
                if not (first and s < 2):
                    act.wait_ge(slot_prod, j - 1)
                nc.scalar.activation(silu_row[:, s % 2, :], up_ps[:, s % 2, 0:HID], ACT.Silu).then_inc(slot_silu, 1)

            def copy_act(j, s, first):
                act.wait_ge(act_turned, j + 1)
                if not (first and s < 2):
                    act.wait_ge(result_ready, j - 1)
                nc.scalar.copy(act_col[:, s % 2, :], act_turned_ps[s % 2][:, 0:HID]).then_inc(act_copied, 1)

            def slots(it, first=False, last=False):
                for s in range(UNROLL):
                    j = it * UNROLL + s
                    slot_silu_of(j, s, first)
                    if not (last and s >= UNROLL - 2):
                        round_turned(j + 2, s + 2, first)
                    if not (first and s == 0):
                        copy_act(j - 1, s - 1, first)

            copy_a(0, pcol[:, :], P)
            copy_a(a_use(0), xT[:, cols(0)])
            for h in range(2):
                act.wait_ge(w1_in, 32)
                for e in range(E // 2 * h, E // 2 * (h + 1)):
                    nc.scalar.copy(w1_hi[:, e * HID:(e + 1) * HID], w1_raw[:, e * HID:(e + 1) * HID]).then_inc(w1_cast, 1)
            act.wait_ge(w2_in, 32)
            for c in range(NC):
                half = slice(c * E * P, (c + 1) * E * P)
                nc.scalar.copy(w2_hi[:, half], w2_raw[:, half]).then_inc(w2_cast, 1)
            router_tanh(0, [0])
            copy_a(a_use(0) + 5, gT[:, slot(0)])
            for i in range(3):
                body0(i)
            with act.Fori(3, NB - 1) as i:
                body0(i)
            body0(NB - 1, last=True)
            tail()
            round_turned(0, 0, True)
            round_turned(1, 1, True)
            slots(0, first=True)
            with act.Fori(1, SLOTS // UNROLL - 1) as it:
                slots(it)
            slots(SLOTS // UNROLL - 1, last=True)
            copy_act(SLOTS - 1, UNROLL - 1, False)
            for n in range(NB):
                act.wait_ge(summed, n + 1)
                for q in range(4):
                    act.dma_start(y_rows[n, q], base[q * B:(q + 1) * B, n, :]).then_inc(y_out, 16)

        @block.vector
        def _(dve):
            link = Chain(dve, dve_chain)

            def per_tile(v, part=both):
                return v[:, part].unsqueeze(2).to_broadcast([P, part.stop - part.start, E])

            def per_expert(v, part=first):
                return v[:, :].unsqueeze(1).to_broadcast([P, part.stop - part.start, E])

            def factor(n, c):
                if has(n, 1):
                    dve.wait_ge(a_ready, a_use(n - 1) + 4 - c)
                src = scond[:, c, bass.ds(n * STEPS, STEPS)].rearrange("p (q r) -> p r q", q=4)
                dve.tensor_tensor(
                    sfac[:, c, :].rearrange("p (r q b) -> p r q b", r=4, q=4),
                    src.unsqueeze(3).to_broadcast([96, 4, 4, B]),
                    delta[:, :].unsqueeze(1).unsqueeze(1).to_broadcast([96, 4, 4, B]),
                    ALU.mult).then_inc(sfac_ready, 1)

            def condition(n, c):
                use = a_use(n) + 3 - c
                xb = xT[:, cols(n)]
                dve.wait_ge(a_ready, use + 1)
                if c == 2:
                    dve.tensor_tensor(zt[:, :], bank_a, xb, ALU.mult).then_inc(a_free, 1)
                elif c == 1:
                    dve.tensor_tensor(zt[:, :], bank_a, zt[:, :], ALU.add).then_inc(a_free, 1)
                    dve.wait_ge(a_free, use + 1)
                    link(dve.tensor_tensor(zt[:, :], zt[:, :], xb, ALU.mult))
                else:
                    dve.tensor_tensor(z[:, :], bank_a, zt[:, :], ALU.add).then_inc(a_free, 1)
                    dve.wait_ge(a_free, use + 1)
                    if has(n, 2):
                        dve.wait_ge(hid_ready, U0 * (n - 1))
                    link(dve.tensor_copy(in_hi[:, slot(n)], z[:, :]))
                    dve.tensor_tensor(in_lo[:, slot(n)], z[:, :], in_hi[:, slot(n)].bitcast(F32),
                                      ALU.subtract).then_inc(z_split, 1)

            def logits0(n):
                use = a_use(n) + 4
                dve.wait_ge(a_ready, use + 1)
                dve.tensor_tensor(rt["logit"][:, first, :], bank_a[:, 0:NT * E].rearrange("p (t e) -> p t e", e=E),
                                  per_expert(gate_b0), ALU.add).then_inc(a_free, 1)

            def variance1(n):
                dve.wait_ge(b_ready, b_use(n) + 2)
                dve.tensor_scalar(var[:, :], bank_b[:, NT * E:NT * E + NT], LN_EPS, None, ALU.add).then_inc(var_ready, 1)

            def logits1(n):
                use = b_use(n) + 1
                dve.wait_ge(rstd_ready, n + 1)
                dve.tensor_tensor(rt["logit"][:, second, :], bank_b[:, 0:NT * E].rearrange("p (t e) -> p t e", e=E),
                                  per_tile(rstd, first), ALU.mult).then_inc(b_free, 1)
                dve.wait_ge(b_free, use + 1)
                link(dve.tensor_tensor(rt["logit"][:, second, :], rt["logit"][:, second, :], per_expert(gate_b1), ALU.add))

            def less_maximum(r, part):
                link(dve.tensor_reduce(rs["m1"][:, part], rt["logit"][:, part, :], AX_X, ALU.max))
                dve.tensor_tensor(rt["d"][:, part, :], rt["logit"][:, part, :], per_tile(rs["m1"], part), ALU.subtract).then_inc(d_ready, 1)

            def first_choice(r, part):
                d, score, one1, d2 = (rt[k][:, part, :] for k in ("d", "score", "one1", "d2"))
                ramp = per_expert(const["ramp"], part)
                dve.wait_ge(d_ready, r + 1)
                link(dve.scalar_tensor_tensor(out=score, in0=d, scalar=0.0, in1=ramp, op0=ALU.is_ge, op1=ALU.mult))
                link(dve.tensor_reduce(rs["s1"][:, part], score, AX_X, ALU.max))
                link(dve.tensor_tensor(one1, score, per_tile(rs["s1"], part), ALU.is_equal))
                link(dve.scalar_tensor_tensor(out=d2, in0=one1, scalar=NEG, in1=d, op0=ALU.mult, op1=ALU.add))
                link(dve.tensor_reduce(rs["m2"][:, part], d2, AX_X, ALU.max))

            def second_choice(part):
                score, d2, two = (rt[k][:, part, :] for k in ("score", "d2", "two"))
                ramp = per_expert(const["ramp"], part)
                link(dve.tensor_tensor(score, d2, per_tile(rs["m2"], part), ALU.is_equal))
                link(dve.tensor_tensor(score, score, ramp, ALU.mult))
                link(dve.tensor_reduce(rs["s2"][:, part], score, AX_X, ALU.max))
                link(dve.tensor_tensor(two, score, per_tile(rs["s2"], part), ALU.is_equal))
                link(dve.tensor_tensor(rt["mask"][:, part, :], rt["one1"][:, part, :], two, ALU.add))

            def exps(r, part):
                th, num, den, e, g = (rt[k][:, part, :] for k in ("th", "num", "den", "e", "g"))
                dve.wait_ge(th_ready, r + 1)
                link(dve.tensor_scalar(den, th, -1.0, 1.0, ALU.mult, ALU.add))
                dve.reciprocal(den, den)
                link(dve.tensor_scalar(num, th, 1.0, None, ALU.add))
                link(dve.tensor_tensor(e, num, den, ALU.mult))
                link(dve.tensor_tensor(g, e, rt["mask"][:, part, :], ALU.mult))

            def gates(part):
                e, g = rt["e"][:, part, :], rt["g"][:, part, :]
                dve.tensor_reduce(rs["sum"][:, part], e, AX_X, ALU.add)
                link(dve.tensor_reduce(rs["top"][:, part], g, AX_X, ALU.add))
                for layer, eps in ((first, EPS0), (second, EPS1)):
                    if part.start <= layer.start and layer.stop <= part.stop:
                        ins = dve.scalar_tensor_tensor(out=rs["den"][:, layer], in0=rs["sum"][:, layer], scalar=eps,
                                                       in1=rs["top"][:, layer], op0=ALU.mult, op1=ALU.add)
                link(ins)
                link(dve.reciprocal(rs["inv"][:, part], rs["den"][:, part]))
                link(dve.tensor_tensor(rt["gate"][:, part, :], g, per_tile(rs["inv"], part), ALU.mult))

            def gates0(n):
                gate, hi = rt["gate"][:, first, :], gates3[:, :, G_HI:G_HI + E]
                dve.tensor_copy(gates3[:, :, G_HI2:G_HI2 + E].bitcast(F32R), gate)
                link(dve.tensor_copy(hi.bitcast(F32R), gate))
                dve.tensor_tensor(gates3[:, :, G_LO:G_LO + E], gate, hi, ALU.subtract).then_inc(gates_ready, 1)

            def gates1(n):
                if has(n, 1):
                    dve.wait_ge(chosen_ready, n)
                    if own(n) == 0:
                        dve.wait_ge(scattered, 16 * NT * TOPK * n)
                hrow = hrows[own(n)]
                for k, chosen in enumerate(("one1", "two")):
                    ins = dve.tensor_tensor(picks[k][:, :, :], rt["gate"][:, second, :], rt[chosen][:, second, :], ALU.mult)
                link(ins)
                for k in range(TOPK):
                    dve.tensor_reduce(hrow[:, :, k, D:D + 1].squeeze(2), picks[k][:, :, :], AX_X, ALU.add)
                link(dve.tensor_copy(hrow[:, :, :, D + 1:D + 2].squeeze(3), ids[:, :, :]))
                dve.tensor_scalar(ids[:, :, :], ids[:, :, :], float(BLK), None, ALU.add).then_inc(chosen_ready, 1)

            def positions(n):
                use = b_use(n) + 3
                dve.wait_ge(b_ready, use + 1)
                dve.tensor_tensor(rank[:, :, :], bank_b[:, 0:NT * E].rearrange("p (t e) -> p t e", e=E),
                                  per_expert(const["region"]), ALU.add).then_inc(b_free, 1)
                link(dve.tensor_reduce(new_choices[:, :], rt["mask"][:, second, :].rearrange("p t e -> p e t"), AX_X, ALU.add))
                dve.wait_ge(b_free, use + 1)
                for k, chosen in enumerate(("one1", "two")):
                    ins = dve.tensor_tensor(picks[k][:, :, :], rank[:, :, :], rt[chosen][:, second, :], ALU.mult)
                link(ins)
                dve.tensor_tensor(choices[:, :], choices[:, :], new_choices[:, :], ALU.add)
                for k in range(TOPK):
                    ins = dve.tensor_reduce(pos_f[:, :, k:k + 1].squeeze(2), picks[k][:, :, :], AX_X, ALU.add)
                link(ins)
                dve.tensor_copy(poss[own(n)][:, :, :], pos_f[:, :, :]).then_inc(pos_ready, 1)

            def gate0(i, u):
                k = U0 * i + u
                dve.wait_ge(gelu_done, k + 1)
                dve.wait_ge(gate_copied, E * i + u // NC + 1)
                if has(k, RING):
                    dve.wait_ge(lo_done, k + 1 - RING)
                dve.tensor_tensor(gated[:, u % RING, :], actv[:, u % RING, :], gate_sb[:, (u // NC) % 2, :],
                                  ALU.mult).then_inc(gated_done, 1)

            def round0(i, u):
                k = U0 * i + u
                dve.wait_ge(gated_done, k + 1)
                if has(k, RING):
                    dve.wait_ge(down_done, k + 1 - RING)
                dve.tensor_copy(h_hi[:, u % RING, :], gated[:, u % RING, :]).then_inc(hi_dve, 1)

            def residual0(n):
                dve.wait_ge(down_done, U0 * (n + 1))
                dve.tensor_tensor(xT[:, cols(n)], acc_of(n), xT[:, cols(n)], ALU.add).then_inc(acc_taken, 1)

            def split_state(n):
                dve.wait_ge(q_cast, n + 1)
                dve.tensor_tensor(in_lo[:, slot(n)], hT[:, hcols(n)], in_hi[:, slot(n)].bitcast(F32),
                                  ALU.subtract).then_inc(q_split, 1)

            def body0(i, last=False):
                layer0, layer1 = layers_of(i, last)
                part = slice(0 if layer0 else NT, 2 * NT if layer1 else NT)
                for u in range(U0):
                    gate0(i, u)
                    if has(i, 3) and u == RANK_AT + 1:
                        positions(i - 3)
                    if has(i, 1) and u == LAG - 1:
                        residual0(i - 1)
                    if layer0 and u in P_AT:
                        condition(i + 1, P_AT[u])
                    if u == LOGITS_IN:
                        if layer0:
                            logits0(i + 1)
                        if layer1:
                            variance1(i - 2)
                    if layer0 or layer1:
                        if u == LOGITS_DONE:
                            if layer1:
                                logits1(i - 2)
                            if layer0:
                                dve.wait_ge(a_free, a_use(i + 1) + 5)
                            less_maximum(i + 1, part)
                        if u == FIRST_CHOICE:
                            first_choice(i + 1, part)
                        if u == SECOND_CHOICE:
                            second_choice(part)
                        if u == EXPS:
                            exps(i + 1, part)
                        if u == GATES:
                            gates(part)
                            if layer0:
                                gates0(i + 1)
                        if u == META and layer1:
                            gates1(i - 2)
                    if not (isinstance(i, int) and i + 2 >= NB) and u in S_AT:
                        factor(i + 2, S_AT[u])
                    if isinstance(i, int) and i == 0 and u == SPLIT_AT:
                        dve.wait_ge(shared_cast, 1)
                        dve.tensor_tensor(sw_lo[:, :], sw_raw[:, 0:2 * HID], sw_hi[:, :].bitcast(F32), ALU.subtract).then_inc(shared_split, 1)
                    if last and u == SPLIT_AT:
                        split_state(0)
                    if u % 2:
                        round0(i, u)

            def multiply(w):
                dve.wait_ge(silu_done, w + 1)
                if w < RING:
                    dve.wait_ge(lo_done, U0 * (NB - 1) + U0 - RING + w + 1)
                else:
                    dve.wait_ge(down1_done, w + 1 - RING)
                dve.tensor_tensor(gated[:, w % RING, :], actv[:, w % RING, :], pair_ps[w % 2][1], ALU.mult).then_inc(prod_done, 1)

            def split_wgu(e):
                dve.wait_ge(wgu_cast, e + 1)
                dve.wait_ge(down_done, U0 * NB)
                cols_e = slice(e * 2 * HID, (e + 1) * 2 * HID)
                dve.tensor_tensor(wgu_lo[:, cols_e], wgu[:, cols_e], wgu_hi[:, cols_e].bitcast(F32), ALU.subtract).then_inc(wgu_split, 1)

            def tail():
                for w in range(W1):
                    multiply(w)
                    if w > W1 - E:
                        split_wgu(w - 1 - (W1 - E))
                    if w == 1:
                        residual0(NB - 1)
                    if w % NC == 0 and w // NC + 1 < NB:
                        split_state(w // NC + 1)
                    if w in TAIL_RANK:
                        positions(TAIL_RANK[w])
                    if w in TAIL_LOGIT:
                        variance1(TAIL_LOGIT[w])
                        logits1(TAIL_LOGIT[w])
                        less_maximum(TAIL_LOGIT[w] + 3, second)
                    if w - 1 in TAIL_LOGIT:
                        first_choice(TAIL_LOGIT[w - 1] + 3, second)
                        second_choice(second)
                    if w - 2 in TAIL_LOGIT:
                        n = TAIL_LOGIT[w - 2]
                        exps(n + 3, second)
                        gates(second)
                        gates1(n)
                split_wgu(E - 1)

            def make_table():
                use = b_use(NB)
                dve.wait_ge(b_ready, use + 1)
                dve.tensor_copy(counts[:, :], bank_b[:, 0:E]).then_inc(b_free, 1)
                dve.wait_ge(b_free, use + 1)
                by_full, by_slot = [P, E, TOK // P], [P, SLOTS, E]
                link(dve.tensor_tensor(filled[:, :, :], counts[:, :].unsqueeze(2).to_broadcast(by_full),
                                       const["full"].unsqueeze(1).to_broadcast(by_full), ALU.is_gt))
                link(dve.tensor_reduce(blocks[:, :], filled[:, :, :], AX_X, ALU.add))
                link(dve.tensor_tensor(upto_v[:, :, :], blocks[:, :].unsqueeze(1).to_broadcast([P, E, E]),
                                       const["upto"].rearrange("p (a b) -> p a b", a=E), ALU.mult))
                link(dve.tensor_reduce(ends[:, :], upto_v[:, :, :], AX_X, ALU.add))
                link(dve.tensor_tensor(passed[:, :, :], const["slot"].unsqueeze(2).to_broadcast(by_slot),
                                       ends[:, :].unsqueeze(1).to_broadcast(by_slot), ALU.is_ge))
                link(dve.tensor_reduce(slot_e[:, :], passed[:, :, :], AX_X, ALU.add))
                link(dve.tensor_tensor(passed[:, :, :], passed[:, :, :], blocks[:, :].unsqueeze(1).to_broadcast(by_slot), ALU.mult))
                link(dve.tensor_reduce(starts[:, :], passed[:, :, :], AX_X, ALU.add))
                link(dve.tensor_tensor(starts[:, :], const["slot"], starts[:, :], ALU.subtract))
                link(dve.tensor_scalar(slot_row[:, :], slot_e[:, :], float(REGION), None, ALU.mult))
                link(dve.scalar_tensor_tensor(out=slot_row[:, :], in0=starts[:, :], scalar=float(P), in1=slot_row[:, :],
                                              op0=ALU.mult, op1=ALU.add))
                link(dve.tensor_scalar(slot_row[:, :], slot_row[:, :], float(PAD_ROWS), None, ALU.min))
                link(dve.tensor_scalar(slot_e[:, :], slot_e[:, :], float(E - 1), None, ALU.min))
                link(dve.tensor_tensor(counts[:, :], counts[:, :], const["region"], ALU.add))
                dve.tensor_copy(table[:, TABLE_LEAD:ROWS_AT_COL], slot_e)
                dve.tensor_copy(table[:, ROWS_AT_COL:PADS_AT_COL], slot_row)
                dve.tensor_copy(table[:, PADS_AT_COL:], counts[:, :]).then_inc(table_ready, 1)

            def split_turned(j, s, first):
                dve.wait_ge(high_ready, j + 1)
                if not (first and s < 2):
                    dve.wait_ge(up_ready, j - 1)
                dve.tensor_tensor(state_lo[:, s % 2, :], turned_ps[s % 2][:, 0:P], state_hi[:, s % 2, :].bitcast(F32),
                                  ALU.subtract).then_inc(state_ready, 1)

            def multiply_slot(j, s, first):
                dve.wait_ge(slot_silu, j + 1)
                if not (first and s < 2):
                    dve.wait_ge(act_turned, j - 1)
                dve.tensor_tensor(act_row[:, s % 2, :], silu_row[:, s % 2, :], up_ps[:, s % 2, HID:2 * HID],
                                  ALU.mult).then_inc(slot_prod, 1)

            def gate_result(it, s):
                j = it * UNROLL + s
                dve.wait_ge(result_ready, j + 1)
                if has(it, 1) or s >= OUT_RING:
                    dve.wait_ge(results_out[s % OUT_RING], 16 * (it * (UNROLL // OUT_RING) + s // OUT_RING))
                row = rows[:, s % ROWS_RING, :]
                dve.tensor_tensor(y_dest[:, s % OUT_RING:s % OUT_RING + 1], row[:, D + 1:D + 2],
                                  const["dest"][:, bass.ds(j, 1)], ALU.min)
                dve.tensor_scalar(y_row[:, s % OUT_RING, :], result_ps[:, s % 2, 0:D], row[:, D:D + 1], None,
                                  ALU.mult).then_inc(y_ready, 1)

            def slots(it, first=False, last=False):
                for s in range(UNROLL):
                    j = it * UNROLL + s
                    multiply_slot(j, s, first)
                    if not (last and s >= UNROLL - 2):
                        split_turned(j + 2, s + 2, first)
                    if s >= 2:
                        gate_result(it, s - 2)
                    elif not first:
                        gate_result(it - 1, UNROLL - 2 + s)

            def add_parts(n):
                dve.wait_ge(parts_in[n], 16)
                link(dve.tensor_tensor(base[:, n, :], base[:, n, :], parts[:, n, 0, :], ALU.add))
                dve.tensor_tensor(base[:, n, :], base[:, n, :], parts[:, n, 1, :], ALU.add).then_inc(summed, 1)

            dve.memset(xpow[0:32, :], 1.0)
            dve.memset(choices[:, :], 0.0)
            dve.memset(table[:, 0:TABLE_LEAD], 0)
            dve.wait_ge(cond_in, 8 * 16)
            link(dve.tensor_tensor(ypow[:, 1, :], ypow[:, 0, :], ypow[:, 0, :], ALU.mult))
            dve.tensor_tensor(xpow[64:96, :], xpow[64:96, :], xpow[64:96, :], ALU.mult)
            for c in range(3):
                link(dve.tensor_scalar(scond[:, c, :], ypow[:, 0, :], coef[:, 3 + c:4 + c], coef[:, c:c + 1], ALU.mult, ALU.add))
            for c in range(3):
                link(dve.scalar_tensor_tensor(out=scond[:, c, :], in0=ypow[:, 1, :], scalar=coef[:, 6 + c:7 + c],
                                              in1=scond[:, c, :], op0=ALU.mult, op1=ALU.add))
            dve.wait_ge(consts_in, 16)
            for g in range(3):
                link(dve.tensor_copy(delta[32 * g:32 * g + 32, :], const_sb[32 * g:32 * g + 32, 32 * g:32 * g + 32]))
            for c in (2, 1, 0):
                factor(0, c)
            dve.tensor_copy(ids[:, :, :].rearrange("p t k -> p (t k)"), const["ids"])
            dve.tensor_tensor(sel[:, :, :], ident[:, G_HI:G_HI + E].unsqueeze(2).to_broadcast([P, E, P]),
                              ident[:, G_LO:G_LO + E].unsqueeze(2).to_broadcast([P, E, P]), ALU.add).then_inc(sel_ready, 1)
            dve.wait_ge(small_in, 5 * 16)
            dve.tensor_copy(b2s[0:64, :], b2_raw[0:64, :])
            link(dve.tensor_copy(b2_hi[64:128, :].bitcast(F32R), b2_raw[64:128, :]))
            dve.tensor_tensor(b2s[64:128, :], b2_raw[64:128, :], b2_hi[64:128, :], ALU.subtract).then_inc(sel_ready, 1)
            dve.wait_ge(a_free, 1)
            dve.tensor_copy(hT[:, step_col(STEPS - 1):step_col(STEPS - 1) + B], pcol[:, ROW_H0:ROW_H0 + B]).then_inc(h_done, 1)
            dve.tensor_scalar(wgate1[:, :], pcol[:, ROW_GATE:ROW_GATE + E], pcol[:, ROW_LNS:ROW_LNS + 1], None, ALU.mult)
            dve.tensor_scalar(lnb_tile[:, :], const["ones"], pcol[:, ROW_LNB:ROW_LNB + 1], None, ALU.mult).then_inc(pcol_ready, 1)
            for c in (2, 1, 0):
                condition(0, c)
            for e in range(E):
                cols_e = slice(e * HID, (e + 1) * HID)
                dve.wait_ge(w1_cast, e + 1)
                dve.tensor_tensor(w1_lo[:, cols_e], w1_raw[:, cols_e], w1_hi[:, cols_e].bitcast(F32),
                                  ALU.subtract).then_inc(w1_split, 1)
            dve.wait_ge(cleared, 3)
            logits0(0)
            dve.wait_ge(a_free, a_use(0) + 5)
            less_maximum(0, first)
            first_choice(0, first)
            second_choice(first)
            exps(0, first)
            gates(first)
            gates0(0)
            for c in (2, 1, 0):
                factor(1, c)
            dve.wait_ge(b_ready, 1)
            dve.tensor_copy(gate_b1[:, :], bank_b[:, 0:E]).then_inc(b_free, 1)

            link.at(link.base + link.n)
            for i in range(3):
                body0(i)
                link.at(link.base + link.n)
            start, per = link.base, LOOP_LINKS
            with dve.Fori(3, NB - 2) as i:
                link.at(start + per * (i - 3))
                body0(i)
                assert link.n == per, link.n
            link.at(start + per * (NB - 5))
            body0(NB - 2)
            body0(NB - 1, last=True)
            tail()
            make_table()
            split_turned(0, 0, True)
            split_turned(1, 1, True)
            slots(0, first=True)
            with dve.Fori(1, SLOTS // UNROLL - 1) as it:
                slots(it)
            slots(SLOTS // UNROLL - 1, last=True)
            gate_result(SLOTS // UNROLL - 1, UNROLL - 2)
            gate_result(SLOTS // UNROLL - 1, UNROLL - 1)
            for n in range(NB):
                add_parts(n)

        @block.tensor
        def _(pe):
            def mm(dst, w, v, start=True, stop=True, **kw):
                return nc.tensor.matmul(dst, w, v, start=start, stop=stop, **kw)

            def turn(bank, tiles, ready):
                for t, tile in enumerate(tiles):
                    ins = nc.tensor.transpose(bank[:, t * P:(t + 1) * P], tile, ident)
                ins.then_inc(ready, 1)

            def input_block(n):
                pe.wait_ge(x_in, 64 * (n + 1))
                pe.wait_ge(a_free, a_use(n))
                turn(bank_a, [xin[:, t * P:(t + 1) * P] for t in range(NT)], a_ready)

            def factor_product(n, c):
                pe.wait_ge(sfac_ready, 3 * n + 3 - c)
                pe.wait_ge(a_free, a_use(n) + 3 - c)
                mm(bank_a, xpow[:, :], sfac[:, c, :]).then_inc(a_ready, 1)

            def logits0(n):
                pe.wait_ge(z_split, n + 1)
                pe.wait_ge(a_free, a_use(n) + 4)
                for t in range(NT):
                    ins = mm(bank_a[:, t * E:(t + 1) * E], z[:, t * P:(t + 1) * P], wgate0[:, :])
                ins.then_inc(a_ready, 1)

            def turn_gates(n):
                pe.wait_ge(gates_ready, n + 1)
                pe.wait_ge(a_free, a_use(n) + 5)
                turn(bank_a, [gates3[:, t, :] for t in range(NT)], a_ready)

            def spread_gate(i, e):
                g = E * i + e
                if e == 0:
                    pe.wait_ge(a_free, a_use(i) + 6)
                if has(g, 1):
                    pe.wait_ge(gate_copied, g)
                mm(gate_ps, sel[:, e, :], gT[:, slot(i)]).then_inc(gate_ready, 1)

            def hidden0(i, u):
                k = U0 * i + u
                if u == 0:
                    pe.wait_ge(z_split, i + 1)
                if isinstance(i, int) and i == 0 and u % NC == 0:
                    pe.wait_ge(w1_split, u // NC + 1)
                if has(k, 2):
                    pe.wait_ge(gelu_done, k + 1 - 2)
                w = slice(u * P, (u + 1) * P)
                dst = hidden[:, u % 2, :]
                mm(dst, w1_hi[:, w], in_hi[:, slot(i)], stop=False)
                mm(dst, w1_hi[:, w], in_lo[:, slot(i)], start=False, stop=False)
                mm(dst, w1_lo[:, w], in_hi[:, slot(i)], start=False).then_inc(hid_ready, 1)

            def down0(i, u):
                k = U0 * i + u
                if u == 0:
                    if isinstance(i, int) and i == 0:
                        pe.wait_ge(w2_split, NC)
                    if has(i, 2):
                        pe.wait_ge(acc_taken, i - 1)
                    mm(acc_of(i), b2s[:, :], gT[:, slot(i)], stop=False)
                w = slice(u * P, (u + 1) * P)
                wait_high(pe, i, u)
                mm(acc_of(i), w2_hi[:, w], h_hi[:, u % RING, :], start=False, stop=False)
                mm(acc_of(i), w2_lo[:, w], h_hi[:, u % RING, :], start=False, stop=False)
                pe.wait_ge(lo_done, k + 1)
                mm(acc_of(i), w2_hi[:, w], h_lo[:, u % RING, :], start=False, stop=(u == U0 - 1)).then_inc(down_done, 1)

            def rnn_input(n):
                pe.wait_ge(acc_taken, n + 1)
                pe.wait_ge(h_done, STEPS * n + 1)
                mm(rnn_ps, wx[:, :], xT[:, cols(n)], stop=False, skip_group_check=True)

            def rnn_step(n, s):
                pe.wait_ge(h_done, STEPS * n + s + 1)
                prev = hT[:, hcols(n, step_col(s - 1), B)] if s else hT[:, hcols(n - 1, step_col(STEPS - 1), B)]
                mm(rnn_ps[:, step_col(s):step_col(s) + B], wh[:, :], prev, start=False, stop=True,
                   skip_group_check=True).then_inc(rnn_ready, 1)

            def center_state(n):
                pe.wait_ge(h_done, STEPS * (n + 1) + 1)
                pe.wait_ge(b_free, b_use(n))
                mm(bank_b, const["center"], hT[:, hcols(n)]).then_inc(b_ready, 1)

            def logits1(n):
                pe.wait_ge(b_free, b_use(n) + 1)
                for t in range(NT):
                    mm(bank_b[:, t * E:(t + 1) * E], hc[:, t * P:(t + 1) * P], wgate1[:, :])
                    ins = mm(bank_b[:, NT * E + t:NT * E + t + 1], hc2[:, t * P:(t + 1) * P], const["mean"])
                ins.then_inc(b_ready, 1)

            def state_rows(n):
                pe.wait_ge(b_free, b_use(n) + 2)
                turn(bank_b, [state_tile[:, t * P:(t + 1) * P] for t in range(NT)], b_ready)

            def ranks(n):
                pe.wait_ge(chosen_ready, n + 1)
                pe.wait_ge(b_free, b_use(n) + 3)
                dst = bank_b[:, 0:NT * E]
                mask = rt["mask"][:, second, :].rearrange("p t e -> p (t e)")
                mm(dst, const["tri"], mask, stop=False, skip_group_check=True)
                for t in range(1, NT):
                    mm(dst[:, t * E:], const["ones"], mask[:, 0:(NT - t) * E], start=False, stop=False, skip_group_check=True)
                mm(dst.rearrange("p (t e) -> p t e", e=E), const["ones"], choices[:, :].unsqueeze(1).to_broadcast([P, NT, E]),
                   start=False, skip_group_check=True).then_inc(b_ready, 1)

            def body0(i, last=False):
                for u in range(U0):
                    hidden0(i, u)
                    if u % NC == 0:
                        spread_gate(i, u // NC)
                    if not last:
                        if u == XT_AT:
                            input_block(i + 1)
                        if u in P_AT:
                            factor_product(i + 1, P_AT[u])
                        if u == LOGIT_AT:
                            logits0(i + 1)
                        if u == GT_AT:
                            turn_gates(i + 1)
                    if has(i, 2):
                        if u == CENTER_AT:
                            center_state(i - 2)
                        if u == LOGIT1_AT:
                            logits1(i - 2)
                        if u == ROWS_AT:
                            state_rows(i - 2)
                    if has(i, 3) and u == RANK_AT:
                        ranks(i - 3)
                    if has(i, 1) and u == XP_AT:
                        rnn_input(i - 1)
                    if u >= LAG:
                        down0(i, u - LAG)
                    elif has(i, 1):
                        down0(i - 1, U0 - LAG + u)
                    if has(i, 2) and u < XP_AT:
                        rnn_step(i - 2, HEAD + u)
                    if has(i, 1) and u >= XP_AT:
                        rnn_step(i - 1, u - XP_AT)

            def pair(w, within):
                n, c = divmod(w, NC)
                pe.wait_ge(q_split, n + 1)
                if w == 0:
                    pe.wait_ge(gelu_done, U0 * NB)
                    pe.wait_ge(shared_split, 1)
                elif w == 1:
                    pe.wait_ge(gate_copied, E * NB)
                    pe.wait_ge(a_free, a_use(NB))
                else:
                    pe.wait_ge(prod_done, w + 1 - 2)
                for part, dst in enumerate(pair_ps[w % 2]):
                    if part and within:
                        rnn_step(*within)
                    mm(dst, shared(sw_hi, part, c), in_hi[:, slot(n)], stop=False)
                    mm(dst, shared(sw_hi, part, c), in_lo[:, slot(n)], start=False, stop=False)
                    ins = mm(dst, shared(sw_lo, part, c), in_hi[:, slot(n)], start=False)
                ins.then_inc(pair_ready, 1)

            def down1(w, step=None):
                n, c = divmod(w, NC)
                if c == 0:
                    pe.wait_ge(acc_taken, n + 1)
                    if n < 2:
                        pe.wait_ge(acc_taken, NB - 1 + n)
                    else:
                        pe.wait_ge(base_done, n - 1)
                pe.wait_ge(prod_done, w + 1)
                for t in range(NT):
                    if t == NT // 2 and step:
                        rnn_step(*step)
                    dst = acc[:, n % 2, t * P:(t + 1) * P]
                    tile = slice(t * P, (t + 1) * P)
                    if c == 0:
                        mm(dst, xT[:, n * BLK + t * P:n * BLK + (t + 1) * P], ident, start=(t == 0), stop=False, skip_group_check=True)
                    ins = mm(dst, gated[:, w % RING, tile], shared(sw_raw, 2, c), start=False, stop=(c == NC - 1), skip_group_check=True)
                ins.then_inc(down1_done, 1)

            def tail():
                for w in range(W1):
                    within, between, inside, behind = TAIL_STEPS.get(w, NO_STEPS)
                    pair(w, within)
                    if between:
                        rnn_step(*between)
                    if w == TAIL_XP:
                        rnn_input(NB - 1)
                    if w < 2:
                        down0(NB - 1, U0 - LAG + 2 * w)
                        if inside:
                            rnn_step(*inside)
                        down0(NB - 1, U0 - LAG + 2 * w + 1)
                    else:
                        down1(w - 2, inside)
                    if behind:
                        rnn_step(*behind)
                    if w in TAIL_RANK:
                        ranks(TAIL_RANK[w])
                    if w in TAIL_CENTER:
                        center_state(TAIL_CENTER[w])
                    if w in TAIL_LOGIT:
                        logits1(TAIL_LOGIT[w])
                    if w in TAIL_ROWS:
                        state_rows(TAIL_ROWS[w])
                    if w == TAIL_COUNTS:
                        pe.wait_ge(pos_ready, NB)
                        pe.wait_ge(b_free, b_use(NB))
                        mm(bank_b[:, 0:E], const["ones"], choices[:, :]).then_inc(b_ready, 1)
                down1(W1 - 2)
                down1(W1 - 1)

            def turn_rows(it, s):
                it, s = (it, s) if s < UNROLL else (it + 1, s - UNROLL)
                j = it * UNROLL + s
                pe.wait_ge(rows_in[s], 16 * (it + 1))
                if has(it, 1) or s >= 2:
                    pe.wait_ge(state_ready, j - 1)
                nc.tensor.transpose(turned_ps[s % 2][:, 0:P], rows[:, s, 0:D], ident).then_inc(turned, 1)

            def gate_and_up(j, s, e, first):
                pe.wait_ge(state_ready, j + 1)
                if not (first and s < 2):
                    pe.wait_ge(slot_prod, j - 1)
                expert = bass.ds(e * 2 * HID, 2 * HID)
                mm(up_ps[:, s % 2, :], state_hi[:, s % 2, :], wgu_hi[:, expert], stop=False)
                mm(up_ps[:, s % 2, :], state_hi[:, s % 2, :], wgu_lo[:, expert], start=False, stop=False)
                mm(up_ps[:, s % 2, :], state_lo[:, s % 2, :], wgu_hi[:, expert], start=False).then_inc(up_ready, 1)

            def turn_act(j, s, first):
                pe.wait_ge(slot_prod, j + 1)
                if not (first and s < 2):
                    pe.wait_ge(act_copied, j - 1)
                turn(act_turned_ps[s % 2], [act_row[:, s % 2, c * P:(c + 1) * P] for c in range(NC)], act_turned)

            def slot_down(j, s, e, first):
                pe.wait_ge(act_copied, j + 1)
                if not (first and s < 2):
                    pe.wait_ge(y_ready, j - 1)
                for c in range(NC):
                    ins = mm(result_ps[:, s % 2, 0:D], act_col[:, s % 2, c * P:(c + 1) * P],
                             wd[:, bass.ds(e * HID + c * P, P)], start=(c == 0), stop=(c == NC - 1))
                ins.then_inc(result_ready, 1)

            def slots(it, first=False, last=False):
                experts = table_values(pe, it * UNROLL, UNROLL + 2, E - 1)
                for s in range(UNROLL):
                    j = it * UNROLL + s
                    if not (last and s >= UNROLL - 2):
                        turn_rows(it, s + 2)
                    gate_and_up(j, s, experts[s + 2], first)
                    if not (first and s < 1):
                        turn_act(j - 1, (s - 1) % UNROLL, first)
                    if not (first and s < 2):
                        slot_down(j - 2, (s - 2) % UNROLL, experts[s], first)
                return experts

            pe.wait_ge(consts_in, 16)
            pe.wait_ge(params_in, 6 * 16)
            nc.tensor.transpose(bank_a[:, 0:P], prow[:, :], ident).then_inc(a_ready, 1)
            input_block(0)
            for c in (2, 1, 0):
                factor_product(0, c)
            pe.wait_ge(small_in, 5 * 16)
            logits0(0)
            turn_gates(0)
            pe.wait_ge(pcol_ready, 1)
            mm(bank_b[:, 0:E], lnb_tile[:, :], pcol[:, ROW_GATE:ROW_GATE + E]).then_inc(b_ready, 1)
            pe.wait_ge(sel_ready, 2)
            pe.wait_ge(rnn_w_in, 32)
            for i in range(3):
                body0(i)
            with pe.Fori(3, NB - 1) as i:
                body0(i)
            body0(NB - 1, last=True)
            tail()
            pe.wait_ge(base_done, NB)
            pe.wait_ge(prod_done, W1)
            pe.wait_ge(h_done, STEPS * NB + 1)
            pe.wait_ge(b_free, b_use(NB) + 1)
            pe.wait_ge(table_ready, 1)
            pe.wait_ge(wgu_split, E)
            pe.wait_ge(wd_in, 32)
            turn_rows(0, 0)
            turn_rows(0, 1)
            slots(0, first=True)
            with pe.Fori(1, SLOTS // UNROLL - 1) as it:
                slots(it)
            experts = slots(SLOTS // UNROLL - 1, last=True)
            turn_act(SLOTS - 1, UNROLL - 1, False)
            slot_down(SLOTS - 2, UNROLL - 2, experts[UNROLL], False)
            slot_down(SLOTS - 1, UNROLL - 1, experts[UNROLL + 1], False)


INPUTS = ("x", "fside_BxS_0", "cond_1024", "L0_cond_coeffs", "L0_ffn_Wg", "L0_ffn_bg", "L0_ffn_W1", "L0_ffn_b1",
          "L0_ffn_W2", "L0_ffn_b2", "L1_cond_Wx", "L1_cond_Wh", "L1_cond_b", "L1_ffn_ln_scale", "L1_ffn_ln_bias",
          "L1_ffn_gate_w", "L1_ffn_Wg", "L1_ffn_Wu", "L1_ffn_Wd", "L1_ffn_sWg", "L1_ffn_sWu", "L1_ffn_sWd")


def kernel(**inputs):
    import numpy as np
    import concourse.bacc as bacc
    from concourse.bass_utils import run_bass_kernel_spmd

    nc = bacc.Bacc("TRN2", target_bir_lowering=False, num_devices=1)
    arrays, args = {}, []
    for name, a in [("consts", constant_tables())] + [(n, np.ascontiguousarray(inputs[n])) for n in INPUTS]:
        arrays[f"in_{name}"] = a
        args.append(nc.dram_tensor(f"in_{name}", a.shape, mybir.dt.from_np(a.dtype), kind="ExternalInput").ap())
    out = nc.dram_tensor("out", (B, T, D), F32, kind="ExternalOutput").ap()
    build(nc, *args, out)
    result = run_bass_kernel_spmd(nc, [arrays], core_ids=[0])
    return result.results[0]["out"]
```

```python
from contextlib import ExitStack

import concourse.bass as bass
from concourse import mybir

ALU = mybir.AluOpType
ACT = mybir.ActivationFunctionType
F32 = mybir.dt.float32
F32R = mybir.dt.float32r
I32 = mybir.dt.int32
U32 = mybir.dt.uint32
AX_X = mybir.AxisListType.X

P = 128
B, T, D = 32, 128, 128
E, HID, TOPK = 8, 256, 2
NC = HID // P
STEPS = 16
BLK = STEPS * B
TOK = T * B
NB = TOK // BLK
NT = BLK // P
GROUP = 2
NG, GT = NB // GROUP, GROUP * NT
TEMP = 5.0
EPS0, EPS1, LN_EPS = 1e-9, 1e-5, 1e-5
NEG = -3.0e38

ROW_GATE, ROW_LNS, ROW_LNB, ROW_CB, ROW_H0 = 0, 8, 9, 10, 32

REGION = TOK + P
ROW = D + 2
SLOTS = TOPK * TOK // P + E
PAD_ROWS = E * REGION
PAD_DEST = 1.0e6
ROWS_RING, OUT_RING = 18, 6
UNROLL = 18
assert UNROLL == ROWS_RING and UNROLL % OUT_RING == 0 and SLOTS % UNROLL == 0
TABLE_LEAD = 3
ROWS_AT_COL = TABLE_LEAD + SLOTS
PADS_AT_COL = ROWS_AT_COL + SLOTS
DOWN_LAG = (3, 2)

CONSTS = {}
for _name, _size in (("ident", P), ("tri", P), ("ones", P), ("center", P), ("ramp", E), ("region", E), ("ids", GT * TOPK),
                     ("dest", SLOTS), ("full", TOK // P), ("upto", E * E), ("slot", SLOTS), ("power", NT), ("pad", ROW)):
    CONSTS[_name] = slice(sum(s.stop - s.start for s in CONSTS.values()),
                          sum(s.stop - s.start for s in CONSTS.values()) + _size)
CONST_COLS = CONSTS["pad"].stop

RANKS_AT, LAST_RANKS_AT = (0, 1), (14, 15)
STATE_AT, CAST_AT, ROWS_AT, COPY_ROWS_AT, LOGIT1_AT, ROUTER_TANH_AT = 0, 1, 2, (3, 4), (6, 7), 11
PAIR_AT, SILU_AT, DOWN_AT = ((4, 5), (8, 9)), (6, 10), ((10, 11), (14, 15))
TURN_X1_AT, COPY_X1_AT, KEEP_AT, XP_AT = 3, 5, 7, (12, 13)
FILL = [{s: 2 for s in range(STEPS) if s not in (TURN_X1_AT, *XP_AT)}, {0: 2, 1: 2}] + (NB - 3) * [{}] + [{3: 2, 12: 2, 13: 2}]
GAP_FILL, ROUTER_FILL = (14, 12, 10), 16


def b_use(n):
    return 2 * n


def step_col(s):
    return (s % 4) * P + (s // 4) * B


def has(i, first):
    return not isinstance(i, int) or i >= first


def stream_loop(body):
    for i in range(NB):
        body(i, i % 2)


class Chain:

    def __init__(self, eng, sem):
        self.eng, self.sem, self.base, self.n = eng, sem, 0, 0

    def __call__(self, ins):
        self.n += 1
        ins.then_inc(self.sem, 1)
        self.eng.wait_ge(self.sem, self.base + self.n)

    def at(self, base):
        self.base, self.n = base, 0


def constant_tables():
    import numpy as np
    p, c = np.arange(P)[:, None], np.zeros((P, CONST_COLS), np.float32)
    c[:, CONSTS["ident"]] = np.eye(P)
    c[:, CONSTS["tri"]] = p < np.arange(P)
    c[:, CONSTS["ones"]] = 1.0
    c[:, CONSTS["center"]] = np.eye(P) - 1.0 / D
    c[:, CONSTS["ramp"]] = E - np.arange(E)
    c[:, CONSTS["region"]] = REGION * np.arange(E)
    t, k = np.divmod(np.arange(GT * TOPK), TOPK)
    c[:, CONSTS["ids"]] = t // NT * BLK + p * NT + t % NT + k * TOK
    c[:, CONSTS["dest"]] = TOPK * TOK + P * np.arange(SLOTS) + p
    c[:, CONSTS["full"]] = P * np.arange(TOK // P)
    c[:, CONSTS["upto"]] = np.tril(np.ones((E, E))).reshape(-1)
    c[:, CONSTS["slot"]] = np.arange(SLOTS)
    c[:, CONSTS["power"]] = -0.5
    c[:, CONSTS["pad"].stop - 1] = PAD_DEST
    return c


def build(nc, consts, x, fside_BxS_0, cond_1024, L0_cond_coeffs, L0_ffn_Wg, L0_ffn_bg, L0_ffn_W1, L0_ffn_b1,
          L0_ffn_W2, L0_ffn_b2, L1_cond_Wx, L1_cond_Wh, L1_cond_b, L1_ffn_ln_scale, L1_ffn_ln_bias,
          L1_ffn_gate_w, L1_ffn_Wg, L1_ffn_Wu, L1_ffn_Wd, L1_ffn_sWg, L1_ffn_sWu, L1_ffn_sWd, out):
    regions = [nc.dram_tensor(f"regions{k}", (PAD_ROWS + P, ROW), F32, kind="Internal").ap() for k in range(2)]
    results = [nc.dram_tensor(f"results{k}", (TOPK * TOK + SLOTS * P, D), F32, kind="Internal").ap() for k in range(2)]
    with ExitStack() as ctx:
        def sb(name, shape, dt=F32):
            return ctx.enter_context(nc.sbuf_tensor(name, shape, dt))

        def sem(name):
            return ctx.enter_context(nc.semaphore(name))

        def by_layer(name):
            return [sem(f"{name}{k}") for k in range(2)]

        def carve(buf, *shapes):
            at = 0
            for shape in shapes:
                size = 1
                for s in shape:
                    size *= s
                part, at = buf[:, at:at + size], at + size
                if len(shape) == 2:
                    part = part.rearrange("p (a b) -> p a b", a=shape[0])
                elif len(shape) == 4:
                    part = part.rearrange("p (a b c d) -> p a b c d", a=shape[0], b=shape[1], c=shape[2])
                yield part

        banks = ctx.enter_context(nc.psum_tensor("banks", [P, 8, BLK], F32))
        poly_ps = [banks[:, k, :] for k in (0, 1, 2, 3, 5)]
        turn_x_ps, bank_c, bank_b = banks[:, 6, :], banks[:, 4, :], banks[:, 7, :]
        param_ps, logit_ps = bank_b[:, 2 * P:3 * P], bank_b[:, P:2 * P]
        gate1_ps = banks[:, 3, 0:2 * E]
        pair_ps, acc, rnn_ps = banks[:, 0:2, :], banks[:, 2:4, :], banks[:, 5:7, :]
        up_ps, result_ps = banks[:, 0:2, :], banks[:, 2:4, :]
        turned_ps, act_turned_ps = banks[:, 4:6, :], banks[:, 6:8, :]
        rank_ps = bank_b, bank_c
        count_ps = banks[:, 0, 0:E], bank_b[:, 0:E]

        first_w = sb("first_w", [P, E * (3 * HID + D)])
        w1, w2, b1, b2 = (first_w[:, k * E * HID:min(k + 1, 3) * E * HID + k // 3 * E * D] for k in range(4))
        wgu, wd = sb("wgu", [P, E * 2 * HID]), sb("wd", [P, E * HID])
        wgu_hi, wgu_lo = sb("wgu_hi", [P, E * 2 * HID], F32R), sb("wgu_lo", [P, E * 2 * HID], F32R)
        sw_raw = sb("sw_raw", [P, 3 * HID])
        sw_hi, sw_lo = sb("sw_hi", [P, 2 * HID], F32R), sb("sw_lo", [P, 2 * HID], F32R)
        wx, wh = sb("wx", [P, P]), sb("wh", [P, P])
        wgate0, gate_b0 = sb("wgate0", [P, E]), sb("gate_b0", [P, E])
        gate_b1, wgate1, wgate1c = sb("gate_b1", [P, E]), sb("wgate1", [P, E]), sb("wgate1c", [P, E])
        prow, pcol, lnb_tile = sb("prow", [P, P]), sb("pcol", [P, P]), sb("lnb_tile", [P, P])
        const_sb = sb("const_sb", [P, CONST_COLS])
        const = {k: const_sb[:, s] for k, s in CONSTS.items()}
        ident = const["ident"]
        coef, xpow = sb("coef", [96, 9]), sb("xpow", [96, D])
        ypow, scond, delta = sb("ypow", [96, 2, T]), sb("scond", [96, 3, T]), sb("delta", [96, B])
        hT, base = sb("hT", [P, (NB + 1) * BLK]), sb("base", [P, NB, BLK])
        parts_buf = sb("parts", [P, NB * TOPK * BLK])
        parts = parts_buf.rearrange("p (n k t) -> p n k t", n=NB, k=TOPK)
        sfac_buf, xin, xT, hrow0 = carve(parts_buf, (3, BLK), (2, BLK), (2, BLK), (2, GT, TOPK, ROW))
        sfac = sfac_buf[0:96, :, :]
        stream = sb("stream", [P, 3 * BLK])
        xr, x1r, x1T = (stream[:, k * BLK:(k + 1) * BLK] for k in range(3))
        zt, z = xr, x1r
        filled, upto_v, passed, per_slot = carve(stream, (E, TOK // P), (E, E), (SLOTS, E), (3, SLOTS))
        slot_e, slot_row, starts = (per_slot[:, k, :] for k in range(3))
        hrow1, silu_out, gated, state_at = carve(first_w, (2, NT, TOPK, ROW), (2, BLK), (2, BLK), (1, BLK))
        in_hi, in_lo = sb("in_hi", [P, 2 * BLK], F32R), sb("in_lo", [P, 2 * BLK], F32R)
        state_tile = state_at[:, 0, :]
        rt = {k: sb("rt_" + k, [P, GT, E]) for k in ("logit", "score", "one1", "d2", "two", "mask", "rank", "pick0", "pick1")}
        rt.update({k: sb("rt_" + k, [P, GT, E + 1]) for k in ("d", "th", "num", "den", "e")})
        rs = {k: sb("rs_" + k, [P, GT]) for k in ("m1", "s1", "s2", "sum", "top", "den", "inv")}
        picks = rt["pick0"], rt["pick1"]
        unused = sb("unused", [P, 1])
        stats, moments = sb("stats", [P, NT, 6]), sb("moments", [P, NT, 2])
        var, rstd = sb("var", [P, NT]), sb("rstd", [P, NT])
        hrows = [hrow0, hrow1]
        tiles_of = GT, NT
        ids = [sb(f"ids{k}", [P, tiles_of[k], TOPK]) for k in range(2)]
        poss = [[sb(f"pos{k}{q}", [P, tiles_of[k], TOPK], U32) for q in range(2)] for k in range(2)]
        pos_f = sb("pos_f", [P, GT, TOPK])
        choices, new_choices = [sb(f"choices{k}", [P, E]) for k in range(2)], sb("new_choices", [P, E])
        counts, ends, blocks = sb("counts", [P, E]), sb("ends", [P, E]), sb("blocks", [P, E])
        tables = [sb(f"table{k}", [P, PADS_AT_COL + E], I32) for k in range(2)]
        rows, silu_row, act_row, act_col = carve(hT[:, BLK:], (ROWS_RING, ROW), (2, HID), (2, HID), (2, HID))
        y_row, = carve(stream, (OUT_RING, D))
        y_dest = sb("y_dest", [P, OUT_RING], U32)
        state0 = sb("state0", [P, 2, P])
        state_hi, state_lo = (w.rearrange("p (a b) -> p a b", a=2) for w in (in_hi[:, 0:2 * P], in_lo[:, 0:2 * P]))

        (consts_in, params_in, cond_in, w1_in, w2_in, bias_in, wgu_in, wd_in, shared_in, small_in, rnn_w_in, base_in,
         parts0_in, y_out) = [
            sem(s) for s in ("consts_in", "params_in", "cond_in", "w1_in", "w2_in", "bias_in", "wgu_in", "wd_in", "shared_in",
                             "small_in", "rnn_w_in", "base_in", "parts0_in", "y_out")]
        x_in = [sem(f"x_in{k}") for k in range(2)]
        (cleared, scond_ready, sfac_ready, params_turned, pcol_copied, pcol_ready, shared_cast, shared_split, gate1_ready, gate1_taken) = [
            sem(s) for s in ("cleared", "scond_ready", "sfac_ready", "params_turned", "pcol_copied", "pcol_ready", "shared_cast",
                             "shared_split", "gate1_ready", "gate1_taken")]
        (x_turned, x_copied, poly_ready, poly_taken, z_ready, z_turned, z_copied, logits_ready) = [
            sem(s) for s in ("x_turned", "x_copied", "poly_ready", "poly_taken", "z_ready", "z_turned", "z_copied", "logits_ready")]
        rank_ready, rank_taken = by_layer("rank_ready"), by_layer("rank_taken")
        d_ready, th_ready, chosen_ready, gates_ready, pos_ready, counted, ends_ready, table_ready, pads_done = [
            by_layer(s) for s in ("d_ready", "th_ready", "chosen_ready", "gates_ready", "pos_ready", "counted", "ends_ready",
                                  "table_ready", "pads_done")]
        nearly_sent = by_layer("nearly_sent")
        scattered = [[sem(f"scattered{k}{q}") for q in range(2)] for k in range(2)]
        (x1_ready, x1_turned, x1_copied, base_kept, rnn_ready, h_done, state_copied, b_ready, b_free, var_ready, rstd_ready) = [
            sem(s) for s in ("x1_ready", "x1_turned", "x1_copied", "base_kept", "rnn_ready", "h_done", "state_copied", "b_ready",
                             "b_free", "var_ready", "rstd_ready")]
        (q_cast, q_split, pair_ready, silu_done, prod_done, down1_done, base_done, wgu_cast, wgu_split, high_ready, slot_silu) = [
            sem(s) for s in ("q_cast", "q_split", "pair_ready", "silu_done", "prod_done", "down1_done", "base_done",
                             "wgu_cast", "wgu_split", "high_ready", "slot_silu")]
        biased = sem("biased")
        turned, state_ready, up_ready, slot_act, act_turned, act_copied, result_ready, y_ready = [
            by_layer(s) for s in ("turned", "state_ready", "up_ready", "slot_act", "act_turned", "act_copied", "result_ready", "y_ready")]
        one_added, summed = sem("one_added"), sem("summed")
        rows_in = [sem(f"rows_in{s}") for s in range(ROWS_RING)]
        results_out = [[sem(f"results_out{k}{s}") for s in range(OUT_RING)] for k in range(2)]
        parts1_in = [sem(f"parts1_in{n}") for n in range(NB)]
        dve_chain, scatter_go = sem("dve_chain"), sem("scatter_go")

        def hcols(n, off=0, size=BLK):
            return bass.ds((n + 1) * BLK + off, size)

        def half(p):
            return slice(p * BLK, (p + 1) * BLK)

        def table_values(eng, layer, at, count, most):
            return nc.values_load_multi_w_load_instructions(
                tables[layer][0:1, bass.ds(at, count)], engines=[eng.engine], min_val=0, max_val=most,
                skip_runtime_bounds_check_because="the vector engine clamped the table's values")[1]

        def shared(w, part, c):
            return w[:, part * HID + c * P:part * HID + (c + 1) * P]

        x_rows = x.rearrange("b (n q r) d -> n q b (r d)", n=NB, q=4)
        y_rows = out.rearrange("b (n q r) d -> n q b (r d)", n=NB, q=4)
        result_rows = [r[0:TOPK * TOK, :].rearrange("(k n p r) d -> n p k (r d)", k=TOPK, n=NB, r=NT) for r in results]
        block = ctx.enter_context(nc.Block())

        @block.sync
        def _(sp):
            def load_x(n):
                sp.dma_start(xin[:, n % 2, :], x_rows[n]).then_inc(x_in[n % 2], 16)

            def finish_regions(layer):
                sp.wait_ge(ends_ready[layer], 1)
                for row in table_values(sp, layer, PADS_AT_COL, E, PAD_ROWS - P):
                    sp.dma_start(regions[layer][bass.ds(row, P), :], const["pad"]).then_inc(pads_done[layer], 16)

            def load_rows(layer, it, reused):
                first_rows = table_values(sp, layer, ROWS_AT_COL + it * UNROLL, UNROLL, PAD_ROWS)
                if not reused:
                    for sent in scattered[layer]:
                        sp.wait_ge(sent, 16 * TOK // P * TOPK // 2)
                    sp.wait_ge(pads_done[layer], 16 * (E + 1))
                for s, row in enumerate(first_rows):
                    if reused:
                        sp.wait_ge(y_ready[layer], (it - 1) * UNROLL + s + 1)
                    sp.dma_start(rows[:, s, :], regions[layer][bass.ds(row, P), :]).then_inc(rows_in[s], 16)

            def slot_rows(layer):
                sp.wait_ge(table_ready[layer], 1)
                load_rows(layer, 0, False)
                with sp.Fori(1, SLOTS // UNROLL) as it:
                    load_rows(layer, it, True)
                for landed in results_out[layer]:
                    sp.wait_ge(landed, 16 * SLOTS // OUT_RING)

            def load_weights():
                sp.dma_start(w1.rearrange("p (e h) -> p e h", e=E), L0_ffn_W1.rearrange("e d h -> d e h")).then_inc(w1_in, 16)
                for c in range(NC):
                    sp.dma_start(w2.rearrange("p (e c d) -> p e c d", c=NC, d=D)[:, :, c, :],
                                  L0_ffn_W2[:, c * P:(c + 1) * P, :].rearrange("e h d -> h e d")).then_inc(w2_in, 16)
                sp.dma_start(b1, L0_ffn_b1.rearrange("e h -> (e h)").partition_broadcast(P)).then_inc(bias_in, 16)
                sp.dma_start(b2, L0_ffn_b2.rearrange("e d -> (e d)").partition_broadcast(P)).then_inc(bias_in, 16)
                sp.dma_start(sw_raw[:, 0:HID], L1_ffn_sWg).then_inc(shared_in, 16)
                sp.dma_start(sw_raw[:, HID:2 * HID], L1_ffn_sWu).then_inc(shared_in, 16)
                sp.dma_start(sw_raw[:, 2 * HID:].rearrange("p (c d) -> p c d", c=NC), L1_ffn_sWd.rearrange("(c h) d -> h c d", c=NC)).then_inc(shared_in, 16)
                wgu_v = wgu.rearrange("p (e g h) -> p e g h", e=E, g=2)
                sp.dma_start(wgu_v[:, :, 0, :], L1_ffn_Wg.rearrange("e d h -> d e h")).then_inc(wgu_in, 16)
                sp.dma_start(wgu_v[:, :, 1, :], L1_ffn_Wu.rearrange("e d h -> d e h")).then_inc(wgu_in, 16)
                for c in range(NC):
                    sp.dma_start(wd.rearrange("p (e c d) -> p e c d", c=NC, d=D)[:, :, c, :],
                                  L1_ffn_Wd[:, c * P:(c + 1) * P, :].rearrange("e h d -> h e d")).then_inc(wd_in, 16)
                sp.dma_start(wx[:, :], L1_cond_Wx).then_inc(rnn_w_in, 16)
                sp.dma_start(wh[:, :], L1_cond_Wh).then_inc(rnn_w_in, 16)
                for q in range(4):
                    sp.dma_start(base[q * B:(q + 1) * B, :, :], x.rearrange("b (n q r) d -> q b n (r d)", n=NB, q=4)[q]).then_inc(base_in, 16)

            sp.dma_start(const_sb[:, :], consts).then_inc(consts_in, 16)
            load_x(0)
            sp.wait_ge(cleared, 1)
            sp.dma_start(prow[ROW_H0:ROW_H0 + B, :], cond_1024).then_inc(params_in, 16)
            sp.dma_start(prow[ROW_GATE:ROW_GATE + E, :], L1_ffn_gate_w).then_inc(params_in, 16)
            for row, v in ((ROW_LNS, L1_ffn_ln_scale), (ROW_LNB, L1_ffn_ln_bias), (ROW_CB, L1_cond_b)):
                sp.dma_start(prow[row:row + 1, :], v.rearrange("(o d) -> o d", o=1)).then_inc(params_in, 16)
            sp.dma_start(wgate0[:, :], L0_ffn_Wg).then_inc(small_in, 16)
            sp.dma_start(gate_b0[:, :], L0_ffn_bg.rearrange("(o e) -> o e", o=1).partition_broadcast(P).squeeze(1)).then_inc(small_in, 16)
            load_x(1)
            sp.wait_ge(consts_in, 16)
            for layer in range(2):
                sp.dma_start(regions[layer][PAD_ROWS:PAD_ROWS + P, :], const["pad"]).then_inc(pads_done[layer], 16)
            for n in range(2, NB):
                sp.wait_ge(x_turned, n - 1)
                load_x(n)
                if n == 3:
                    load_weights()
            finish_regions(0)
            slot_rows(0)
            sp.dma_start(parts[:, 0, :, :], result_rows[0][0]).then_inc(parts0_in, 16)
            with sp.Fori(1, NB) as n:
                sp.wait_ge(parts0_in, 16 * n)
                sp.dma_start(parts[:, bass.ds(n, 1), :, :].squeeze(1), result_rows[0][bass.ds(n, 1)].squeeze(0)).then_inc(parts0_in, 16)
            finish_regions(1)
            sp.wait_ge(q_split, NB)
            slot_rows(1)
            for n in range(NB):
                sp.dma_start(parts[:, n, :, :], result_rows[1][n]).then_inc(parts1_in[n], 16)
            sp.wait_ge(y_out, NB * 16)

        @block.gpsimd
        def _(pool):
            pool.memset(prow[:, :], 0.0).then_inc(cleared, 1)

            def factor(n, c):
                if n:
                    pool.wait_ge(poly_ready, 3 * n - c)
                src = scond[:, c, n * STEPS:(n + 1) * STEPS].rearrange("p (q r) -> p r q", q=4)
                pool.tensor_tensor(
                    sfac[:, c, :].rearrange("p (r q b) -> p r q b", r=4, q=4),
                    src.unsqueeze(3).to_broadcast([96, 4, 4, B]),
                    delta[:, :].unsqueeze(1).unsqueeze(1).to_broadcast([96, 4, 4, B]),
                    ALU.mult).then_inc(sfac_ready, 1)

            def scatter(layer, n, q, rows_written, at_least, middle=lambda: None):
                pool.wait_ge(rows_written, at_least)
                pool.wait_ge(pos_ready[layer], n + 1)
                pool.sem_inc(scatter_go, 1)
                for t in range(tiles_of[layer]):
                    if t == 1:
                        middle()
                    if t == tiles_of[layer] - 1 and n == (NG, NB)[layer] - 1:
                        pool.sem_inc(nearly_sent[layer], 1)
                    for k in range(TOPK):
                        pool.indirect_dma_start(regions[layer], bass.IndirectOffsetOnAxis(ap=poss[layer][q][:, t, k:k + 1], axis=0),
                                                hrows[layer][:, q, t, k, :], None).then_inc(scattered[layer][q], 16)

            def inv_std(n):
                pool.wait_ge(var_ready, n + 1)
                pool.tensor_tensor(rstd[:, :], var[:, :], const["power"], ALU.pow).then_inc(rstd_ready, 1)

            def add_one(n):
                pool.wait_ge(parts0_in, 16 * (n + 1))
                pool.tensor_tensor(parts[:, n, 0, :], base[:, n, :], parts[:, n, 0, :], ALU.add).then_inc(one_added, 1)

            def scatter_results(layer):
                with pool.Fori(0, SLOTS // UNROLL) as it:
                    for s in range(UNROLL):
                        pool.wait_ge(y_ready[layer], it * UNROLL + s + 1)
                        pool.sem_inc(scatter_go, 1)
                        out_slot = s % OUT_RING
                        pool.indirect_dma_start(results[layer], bass.IndirectOffsetOnAxis(ap=y_dest[:, out_slot:out_slot + 1], axis=0),
                                                y_row[:, out_slot, :], None).then_inc(results_out[layer][out_slot], 16)

            pool.wait_ge(scond_ready, 1)
            for n in range(GROUP):
                for c in (2, 1, 0):
                    factor(n, c)
            for g in range(NG):
                scatter(0, g, g % 2, z_copied, GROUP * (g + 1))
            scatter_results(0)
            pool.wait_ge(base_in, 4 * 16)
            for n in range(1, 4):
                add_one(n)
            inv_std(0)
            for n in range(NB):
                if n + 4 < NB:
                    add_one(n + 4)
                scatter(1, n, n % 2, b_free, b_use(n) + 1, lambda: inv_std(n + 1) if n + 1 < NB else None)
            scatter_results(1)

        @block.scalar
        def _(act):
            act.dma_start(coef[:, :], L0_cond_coeffs.rearrange("a b c -> a (b c)").unsqueeze(1).to_broadcast([3, B, 9])).then_inc(cond_in, 16)
            act.dma_start(ypow[:, 0, :], cond_1024.unsqueeze(0).to_broadcast([3, B, T])).then_inc(cond_in, 16)
            act.dma_start(xpow[B:3 * B, :], fside_BxS_0.unsqueeze(0).to_broadcast([2, B, D])).then_inc(cond_in, 16)

            def load_tables(function):
                nc.scalar.activation(unused[:, :], pcol[:, 0:1], function)

            def copy_x(n):
                act.wait_ge(x_turned, n + 1)
                if n >= 2:
                    act.wait_ge(z_ready, n - 1)
                nc.scalar.copy(xT[:, n % 2, :], turn_x_ps).then_inc(x_copied, 1)

            def copy_z(n):
                g, half = divmod(n, GROUP)
                act.wait_ge(z_turned, n + 1)
                if g >= 2 and half == 0:
                    act.wait_ge(scattered[0][g % 2], 16 * GT * TOPK * (g // 2))
                src = bank_c.rearrange("p (t d) -> p t d", t=NT)
                for k in range(TOPK):
                    ins = nc.scalar.copy(hrow0[:, g % 2, half * NT:(half + 1) * NT, k, 0:D], src)
                ins.then_inc(z_copied, 1)

            def router_tanh(layer, n):
                act.wait_ge(d_ready[layer], n + 1)
                part = slice(0, tiles_of[layer])
                nc.scalar.activation(rt["th"][:, part, :], rt["d"][:, part, :], ACT.Tanh,
                                     scale=0.5 / (TEMP if layer == 0 else 1.0)).then_inc(th_ready[layer], 1)

            def cast_wgu(e):
                cols_e = slice(e * 2 * HID, (e + 1) * 2 * HID)
                nc.scalar.copy(wgu_hi[:, cols_e], wgu[:, cols_e]).then_inc(wgu_cast, 1)

            def copy_turned0(j, s, first):
                act.wait_ge(turned[0], j + 1)
                if not (first and s < 2):
                    act.wait_ge(up_ready[0], j - 1)
                nc.scalar.copy(state0[:, s % 2, :], turned_ps[:, s % 2, 0:P]).then_inc(state_ready[0], 1)

            def gelu(j, s, first):
                act.wait_ge(biased, j + 1)
                if not (first and s < 2):
                    act.wait_ge(act_turned[0], j - 1)
                nc.scalar.activation(act_row[:, s % 2, :], silu_row[:, s % 2, :], ACT.Gelu).then_inc(slot_act[0], 1)

            def copy_act(layer, j, s, first):
                act.wait_ge(act_turned[layer], j + 1)
                if not (first and s < 2):
                    act.wait_ge(result_ready[layer], j - 1)
                nc.scalar.copy(act_col[:, s % 2, :], act_turned_ps[:, s % 2, 0:HID]).then_inc(act_copied[layer], 1)

            def slots0(it, first=False, last=False):
                for s in range(UNROLL):
                    j = it * UNROLL + s
                    if not (last and s >= UNROLL - 2):
                        copy_turned0(j + 2, s + 2, first)
                    if not (first and s < 2):
                        copy_act(0, j - 2, s - 2, first)
                    gelu(j, s, first)

            def tanh_step(n, p, s):
                act.wait_ge(rnn_ready, STEPS * n + s + 1)
                nc.scalar.activation(hT[:, hcols(n, step_col(s), B)], rnn_ps[:, p, step_col(s):step_col(s) + B],
                                     ACT.Tanh, bias=pcol[:, ROW_CB:ROW_CB + 1]).then_inc(h_done, 1)

            def copy_x1(n):
                act.wait_ge(x1_turned, n + 1)
                nc.scalar.copy(x1T, bank_c).then_inc(x1_copied, 1)

            def keep_base(n):
                act.wait_ge(x1_ready, n + 1)
                nc.scalar.copy(base[:, bass.ds(n, 1), :].squeeze(1), x1r).then_inc(base_kept, 1)

            def copy_state(n):
                act.wait_ge(h_done, STEPS * (n + 1) + 1)
                if has(n, 1):
                    act.wait_ge(b_ready, b_use(n - 1) + 2)
                nc.scalar.copy(state_tile, hT[:, hcols(n)]).then_inc(state_copied, 1)

            def cast_state(n, p):
                act.wait_ge(h_done, STEPS * (n + 1) + 1)
                if has(n, 2):
                    act.wait_ge(pair_ready, NC * (n - 1))
                nc.scalar.copy(in_hi[:, half(p)], hT[:, hcols(n)]).then_inc(q_cast, 1)

            def copy_rows(n, p, k):
                if k == 0:
                    act.wait_ge(b_ready, b_use(n) + 1)
                    if has(n, 2):
                        act.wait_ge(scattered[1][p], 16 * NT * TOPK // 2 * (n - p))
                ins = nc.scalar.copy(hrow1[:, p, :, k, 0:D], bank_b.rearrange("p (t d) -> p t d", t=NT))
                if k == TOPK - 1:
                    ins.then_inc(b_free, 1)

            def silu(n, c):
                w = NC * n + c
                act.wait_ge(pair_ready, w + 1)
                if has(n, 1):
                    act.wait_ge(prod_done, w - 1)
                nc.scalar.activation(silu_out[:, c, :], pair_ps[:, 0, :], ACT.Silu).then_inc(silu_done, 1)

            def stream_body(i, p):
                before, ahead = i > 0, i + 1 < NB
                for s in range(STEPS):
                    tanh_step(i, p, s)
                    if before:
                        if s == STATE_AT:
                            copy_state(i - 1)
                        if s == CAST_AT:
                            cast_state(i - 1, 1 - p)
                        if s in COPY_ROWS_AT:
                            copy_rows(i - 1, 1 - p, COPY_ROWS_AT.index(s))
                        if s in SILU_AT:
                            silu(i - 1, SILU_AT.index(s))
                        if s == ROUTER_TANH_AT:
                            router_tanh(1, i - 1)
                    if ahead:
                        if s == COPY_X1_AT:
                            copy_x1(i + 1)
                        if s == KEEP_AT:
                            keep_base(i + 1)

            def last_block(n, p):
                copy_state(n)
                cast_state(n, p)
                for k in range(TOPK):
                    copy_rows(n, p, k)
                silu(n, 0)
                router_tanh(1, n)
                silu(n, 1)

            def round_turned(j, s, first):
                act.wait_ge(turned[1], j + 1)
                if not (first and s < 2):
                    act.wait_ge(up_ready[1], j - 1)
                nc.scalar.copy(state_hi[:, s % 2, :], turned_ps[:, s % 2, 0:P]).then_inc(high_ready, 1)

            def slot_silu_of(j, s, first):
                act.wait_ge(up_ready[1], j + 1)
                if not (first and s < 2):
                    act.wait_ge(slot_act[1], j - 1)
                nc.scalar.activation(silu_row[:, s % 2, :], up_ps[:, s % 2, 0:HID], ACT.Silu).then_inc(slot_silu, 1)

            def slots1(it, first=False, last=False):
                for s in range(UNROLL):
                    j = it * UNROLL + s
                    slot_silu_of(j, s, first)
                    if not (last and s >= UNROLL - 2):
                        round_turned(j + 2, s + 2, first)
                    if not (first and s == 0):
                        copy_act(1, j - 1, s - 1, first)

            act.wait_ge(params_turned, 1)
            nc.scalar.copy(pcol[:, :], param_ps[:, 0:P]).then_inc(pcol_copied, 1)
            copy_x(0)
            copy_x(1)
            copy_z(0)
            copy_z(1)
            for g in range(NG):
                nexts = range(GROUP * (g + 1), min(GROUP * (g + 2), NB))
                for n in nexts[:1]:
                    copy_x(n)
                router_tanh(0, g)
                for n in nexts[1:]:
                    copy_x(n)
                for n in nexts:
                    copy_z(n)
                if g == 1:
                    act.wait_ge(shared_in, 48)
                    nc.scalar.copy(sw_hi[:, :], sw_raw[:, 0:2 * HID]).then_inc(shared_cast, 1)
                    act.wait_ge(wgu_in, 32)
                if g >= NG // 2:
                    for e in range(E // 2 * (g - NG // 2), E // 2 * (g - NG // 2 + 1)):
                        cast_wgu(e)
            load_tables(ACT.Gelu)
            copy_turned0(0, 0, True)
            copy_turned0(1, 1, True)
            slots0(0, first=True)
            with act.Fori(1, SLOTS // UNROLL - 1) as it:
                slots0(it)
            slots0(SLOTS // UNROLL - 1, last=True)
            copy_act(0, SLOTS - 2, UNROLL - 2, False)
            copy_act(0, SLOTS - 1, UNROLL - 1, False)
            load_tables(ACT.Silu)
            copy_x1(0)
            keep_base(0)
            stream_loop(stream_body)
            last_block(NB - 1, (NB - 1) % 2)
            round_turned(0, 0, True)
            round_turned(1, 1, True)
            slots1(0, first=True)
            with act.Fori(1, SLOTS // UNROLL - 1) as it:
                slots1(it)
            slots1(SLOTS // UNROLL - 1, last=True)
            copy_act(1, SLOTS - 1, UNROLL - 1, False)
            for n in range(NB):
                act.wait_ge(summed, n + 1)
                act.dma_start(y_rows[n], base[:, n, :]).then_inc(y_out, 16)

        @block.vector
        def _(dve):
            link = Chain(dve, dve_chain)

            def per_tile(v, n):
                return v[:, 0:n].unsqueeze(2).to_broadcast([P, n, E])

            def per_expert(v, n):
                return v[:, :].unsqueeze(1).to_broadcast([P, n, E])

            def factor(n, c):
                dve.wait_ge(poly_ready, 3 * n - c)
                src = scond[:, c, n * STEPS:(n + 1) * STEPS].rearrange("p (q r) -> p r q", q=4)
                dve.tensor_tensor(
                    sfac[:, c, :].rearrange("p (r q b) -> p r q b", r=4, q=4),
                    src.unsqueeze(3).to_broadcast([96, 4, 4, B]),
                    delta[:, :].unsqueeze(1).unsqueeze(1).to_broadcast([96, 4, 4, B]),
                    ALU.mult).then_inc(sfac_ready, 1)

            def factors(n):
                for c in (2, 1, 0):
                    factor(n, c)

            def condition(n):
                xb = xT[:, n % 2, :]
                dve.wait_ge(x_copied, n + 1)
                p2, p1, p0 = (poly_ps[(3 * n + k) % len(poly_ps)] for k in range(3))
                dve.wait_ge(poly_ready, 3 * n + 1)
                dve.tensor_tensor(zt, p2, xb, ALU.mult).then_inc(poly_taken, 1)
                dve.wait_ge(poly_ready, 3 * n + 2)
                dve.wait_ge(poly_taken, 2 * n + 1)
                dve.tensor_tensor(zt, p1, zt, ALU.add).then_inc(poly_taken, 1)
                dve.wait_ge(poly_taken, 2 * n + 2)
                link(dve.tensor_tensor(zt, zt, xb, ALU.mult))
                dve.wait_ge(poly_ready, 3 * n + 3)
                if n:
                    dve.wait_ge(logits_ready, n)
                dve.tensor_tensor(z, p0, zt, ALU.add).then_inc(z_ready, 1)
                dve.wait_ge(z_ready, n + 1)

            def logits0(g):
                dve.wait_ge(logits_ready, GROUP * (g + 1))
                link(dve.tensor_tensor(rt["logit"][:, :, :], logit_ps[:, 0:GT * E].rearrange("p (t e) -> p t e", e=E),
                                       per_expert(gate_b0, GT), ALU.add))

            def variance1(n, p):
                dve.wait_ge(b_free, b_use(n) + 1)
                for t in range(NT):
                    ins = dve.bn_stats(stats[:, t, :], hrow1[:, p, t, 0, 0:D])
                link(ins)
                for t in range(NT):
                    ins = dve.bn_aggr(moments[:, t, :], stats[:, t, :])
                link(ins)
                dve.tensor_scalar(var[:, :], moments[:, :, 1:2].squeeze(2), LN_EPS, None, ALU.add).then_inc(var_ready, 1)

            def logits1(n):
                use = b_use(n) + 1
                dve.wait_ge(b_ready, use + 1)
                dve.wait_ge(rstd_ready, n + 1)
                logit = rt["logit"][:, 0:NT, :]
                dve.tensor_tensor(logit, bank_b[:, 0:NT * E].rearrange("p (t e) -> p t e", e=E),
                                  per_tile(rstd, NT), ALU.mult).then_inc(b_free, 1)
                dve.wait_ge(b_free, use + 1)
                link(dve.tensor_tensor(logit, logit, per_expert(gate_b1, NT), ALU.add))

            def choose(layer, n):
                tiles = tiles_of[layer]
                logit, score, one1, d2, two = (rt[k][:, 0:tiles, :] for k in ("logit", "score", "one1", "d2", "two"))
                d, m2 = rt["d"][:, 0:tiles, 0:E], rt["d"][:, 0:tiles, E:E + 1].squeeze(2)
                ramp = per_expert(const["ramp"], tiles)
                link(dve.tensor_reduce(rs["m1"][:, 0:tiles], logit, AX_X, ALU.max))
                link(dve.tensor_tensor(d, logit, per_tile(rs["m1"], tiles), ALU.subtract))
                link(dve.scalar_tensor_tensor(out=score, in0=d, scalar=0.0, in1=ramp, op0=ALU.is_ge, op1=ALU.mult))
                link(dve.tensor_reduce(rs["s1"][:, 0:tiles], score, AX_X, ALU.max))
                link(dve.tensor_tensor(one1, score, per_tile(rs["s1"], tiles), ALU.is_equal))
                link(dve.scalar_tensor_tensor(out=d2, in0=one1, scalar=NEG, in1=d, op0=ALU.mult, op1=ALU.add))
                dve.tensor_reduce(m2, d2, AX_X, ALU.max).then_inc(d_ready[layer], 1)
                dve.wait_ge(d_ready[layer], n + 1)
                link(dve.tensor_tensor(score, d2, rt["d"][:, 0:tiles, E:E + 1].to_broadcast([P, tiles, E]), ALU.is_equal))
                link(dve.tensor_tensor(score, score, ramp, ALU.mult))
                link(dve.tensor_reduce(rs["s2"][:, 0:tiles], score, AX_X, ALU.max))
                link(dve.tensor_tensor(two, score, per_tile(rs["s2"], tiles), ALU.is_equal))
                dve.tensor_tensor(rt["mask"][:, 0:tiles, :], one1, two, ALU.add).then_inc(chosen_ready[layer], 1)

            def gates(layer, n, q):
                tiles = tiles_of[layer]
                th, num, den, e = (rt[k][:, 0:tiles, :] for k in ("th", "num", "den", "e"))
                e2, hrow = rt["e"][:, 0:tiles, E:E + 1].squeeze(2), hrows[layer][:, q, :, :, :]
                dve.wait_ge(th_ready[layer], n + 1)
                link(dve.tensor_scalar(den, th, -1.0, 1.0, ALU.mult, ALU.add))
                dve.reciprocal(den, den)
                link(dve.tensor_scalar(num, th, 1.0, None, ALU.add))
                link(dve.tensor_tensor(e, num, den, ALU.mult))
                dve.tensor_scalar(rs["top"][:, 0:tiles], e2, 1.0, None, ALU.add)
                link(dve.tensor_reduce(rs["sum"][:, 0:tiles], rt["e"][:, 0:tiles, 0:E], AX_X, ALU.add))
                link(dve.scalar_tensor_tensor(out=rs["den"][:, 0:tiles], in0=rs["sum"][:, 0:tiles], scalar=(EPS0, EPS1)[layer],
                                              in1=rs["top"][:, 0:tiles], op0=ALU.mult, op1=ALU.add))
                link(dve.reciprocal(rs["inv"][:, 0:tiles], rs["den"][:, 0:tiles]))
                if has(n, 2):
                    dve.wait_ge(scattered[layer][q], 16 * tiles * TOPK // 2 * (n - q))
                dve.tensor_copy(hrow[:, :, 0, D:D + 1].squeeze(2), rs["inv"][:, 0:tiles])
                dve.tensor_tensor(hrow[:, :, 1, D:D + 1].squeeze(2), e2, rs["inv"][:, 0:tiles], ALU.mult)
                link(dve.tensor_copy(hrow[:, :, :, D + 1:D + 2].squeeze(3), ids[layer][:, :, :]))
                dve.tensor_scalar(ids[layer][:, :, :], ids[layer][:, :, :], float(tiles * P), None, ALU.add).then_inc(gates_ready[layer], 1)
                dve.wait_ge(gates_ready[layer], n + 1)

            def positions(layer, n, q, between=lambda: None):
                tiles = tiles_of[layer]
                rank = rt["rank"][:, 0:tiles, :]
                dve.wait_ge(rank_ready[layer], n + 1)
                dve.tensor_tensor(rank, rank_ps[layer][:, 0:tiles * E].rearrange("p (t e) -> p t e", e=E),
                                  per_expert(const["region"], tiles), ALU.add).then_inc(rank_taken[layer], 1)
                between()
                link(dve.tensor_reduce(new_choices[:, :], rt["mask"][:, 0:tiles, :].rearrange("p t e -> p e t"), AX_X, ALU.add))
                dve.wait_ge(rank_taken[layer], n + 1)
                for k, chosen in enumerate(("one1", "two")):
                    ins = dve.tensor_tensor(picks[k][:, 0:tiles, :], rank, rt[chosen][:, 0:tiles, :], ALU.mult)
                link(ins)
                if not (isinstance(n, int) and n == (NG, NB)[layer] - 1):
                    dve.tensor_tensor(choices[layer][:, :], choices[layer][:, :], new_choices[:, :], ALU.add)
                for k in range(TOPK):
                    ins = dve.tensor_reduce(pos_f[:, 0:tiles, k:k + 1].squeeze(2), picks[k][:, 0:tiles, :], AX_X, ALU.add)
                link(ins)
                dve.tensor_copy(poss[layer][q][:, :, :], pos_f[:, 0:tiles, :]).then_inc(pos_ready[layer], 1)

            def find_ends(layer):
                dve.wait_ge(counted[layer], 1)
                link(dve.tensor_copy(counts[:, :], count_ps[layer]))
                link(dve.tensor_tensor(ends[:, :], counts[:, :], const["region"], ALU.add))
                dve.tensor_copy(tables[layer][:, PADS_AT_COL:], ends[:, :]).then_inc(ends_ready[layer], 1)
                dve.wait_ge(ends_ready[layer], 1)

            def make_table(layer, middle=lambda: None):
                by_full, by_slot = [P, E, TOK // P], [P, SLOTS, E]
                table = tables[layer]
                link(dve.tensor_tensor(filled[:, :, :], counts[:, :].unsqueeze(2).to_broadcast(by_full),
                                       const["full"].unsqueeze(1).to_broadcast(by_full), ALU.is_gt))
                link(dve.tensor_reduce(blocks[:, :], filled[:, :, :], AX_X, ALU.add))
                link(dve.tensor_tensor(upto_v[:, :, :], blocks[:, :].unsqueeze(1).to_broadcast([P, E, E]),
                                       const["upto"].rearrange("p (a b) -> p a b", a=E), ALU.mult))
                link(dve.tensor_reduce(ends[:, :], upto_v[:, :, :], AX_X, ALU.add))
                middle()
                link(dve.tensor_tensor(passed[:, :, :], const["slot"].unsqueeze(2).to_broadcast(by_slot),
                                       ends[:, :].unsqueeze(1).to_broadcast(by_slot), ALU.is_ge))
                link(dve.tensor_reduce(slot_e[:, :], passed[:, :, :], AX_X, ALU.add))
                link(dve.tensor_tensor(passed[:, :, :], passed[:, :, :], blocks[:, :].unsqueeze(1).to_broadcast(by_slot), ALU.mult))
                link(dve.tensor_reduce(starts[:, :], passed[:, :, :], AX_X, ALU.add))
                link(dve.tensor_tensor(starts[:, :], const["slot"], starts[:, :], ALU.subtract))
                link(dve.tensor_scalar(slot_row[:, :], slot_e[:, :], float(REGION), None, ALU.mult))
                link(dve.scalar_tensor_tensor(out=slot_row[:, :], in0=starts[:, :], scalar=float(P), in1=slot_row[:, :],
                                              op0=ALU.mult, op1=ALU.add))
                link(dve.tensor_scalar(slot_row[:, :], slot_row[:, :], float(PAD_ROWS), None, ALU.min))
                link(dve.tensor_scalar(slot_e[:, :], slot_e[:, :], float(E - 1), None, ALU.min))
                dve.tensor_copy(table[:, TABLE_LEAD:ROWS_AT_COL], slot_e)
                dve.tensor_copy(table[:, ROWS_AT_COL:PADS_AT_COL], slot_row).then_inc(table_ready[layer], 1)

            def add_bias(j, s, e, first):
                dve.wait_ge(up_ready[0], j + 1)
                if not (first and s < 2):
                    dve.wait_ge(slot_act[0], j - 1)
                dve.tensor_tensor(silu_row[:, s % 2, :], up_ps[:, s % 2, 0:HID], b1[:, bass.ds(e * HID, HID)], ALU.add).then_inc(biased, 1)

            def gate_result(layer, it, s, e=None):
                j = it * UNROLL + s
                out_slot = s % OUT_RING
                dve.wait_ge(result_ready[layer], j + 1)
                if has(it, 1) or s >= OUT_RING:
                    dve.wait_ge(results_out[layer][out_slot], 16 * (it * (UNROLL // OUT_RING) + s // OUT_RING))
                row, y, gate = rows[:, s % ROWS_RING, :], y_row[:, out_slot, :], rows[:, s % ROWS_RING, D:D + 1]
                result = result_ps[:, s % 2, 0:D]
                if layer == 0:
                    link(dve.tensor_tensor(y, result, b2[:, bass.ds(e * D, D)], ALU.add))
                    result = y
                dve.tensor_tensor(y_dest[:, out_slot:out_slot + 1], row[:, D + 1:D + 2], const["dest"][:, bass.ds(j, 1)], ALU.min)
                dve.tensor_scalar(y, result, gate, None, ALU.mult).then_inc(y_ready[layer], 1)

            def slots0(it, first=False, last=False):
                experts = table_values(dve, 0, it * UNROLL, UNROLL + DOWN_LAG[0], E - 1)
                for s in range(UNROLL):
                    add_bias(it * UNROLL + s, s, experts[s + DOWN_LAG[0]], first)
                    if s >= DOWN_LAG[0]:
                        gate_result(0, it, s - DOWN_LAG[0], experts[s])
                    elif not first:
                        gate_result(0, it - 1, UNROLL - DOWN_LAG[0] + s, experts[s])
                return experts

            def sum_x1(n):
                if n == 0:
                    dve.wait_ge(base_in, 4 * 16)
                    dve.wait_ge(parts0_in, 16)
                    link(dve.tensor_tensor(parts[:, 0, 0, :], base[:, 0, :], parts[:, 0, 0, :], ALU.add))
                else:
                    dve.wait_ge(one_added, n)
                if has(n, 1):
                    dve.wait_ge(x1_turned, n)
                    dve.wait_ge(base_kept, n)
                at = bass.ds(n, 1)
                dve.tensor_tensor(x1r, parts[:, at, 0:1, :].squeeze(2).squeeze(1), parts[:, at, 1:2, :].squeeze(2).squeeze(1), ALU.add).then_inc(x1_ready, 1)

            def split_state(n, p):
                dve.wait_ge(q_cast, n + 1)
                dve.tensor_tensor(in_lo[:, half(p)], hT[:, hcols(n)], in_hi[:, half(p)].bitcast(F32), ALU.subtract).then_inc(q_split, 1)

            def multiply(n, c):
                w = NC * n + c
                dve.wait_ge(silu_done, w + 1)
                if has(n, 1):
                    dve.wait_ge(down1_done, w - 1)
                dve.tensor_tensor(gated[:, c, :], silu_out[:, c, :], pair_ps[:, 1, :], ALU.mult).then_inc(prod_done, 1)

            def add_shared(n, p):
                dve.wait_ge(down1_done, NC * (n + 1))
                dve.wait_ge(base_kept, n + 1)
                block_rows = base[:, bass.ds(n, 1), :].squeeze(1)
                dve.tensor_tensor(block_rows, acc[:, p, :], block_rows, ALU.add).then_inc(base_done, 1)

            def stream_body(i, p):
                before, ahead = i > 0, i + 1 < NB
                if i >= 2:
                    add_shared(i - 2, p)
                if ahead:
                    sum_x1(i + 1)
                if i >= 2:
                    positions(1, i - 2, p, lambda: split_state(i - 1, 1 - p))
                elif before:
                    split_state(i - 1, 1 - p)
                if before:
                    variance1(i - 1, 1 - p)
                    multiply(i - 1, 0)
                    logits1(i - 1)
                    choose(1, i - 1)
                    multiply(i - 1, 1)
                    gates(1, i - 1, 1 - p)
                if not ahead:
                    positions(1, i - 1, 1 - p)
                    split_state(i, p)

            def last_block(n, p):
                variance1(n, p)
                logits1(n)
                choose(1, n)
                gates(1, n, p)
                positions(1, n, p)
                multiply(n, 0)
                find_ends(1)
                add_shared(n - 1, 1 - p)
                make_table(1, lambda: multiply(n, 1))
                add_shared(n, p)

            def split_turned(j, s, first):
                dve.wait_ge(high_ready, j + 1)
                if not (first and s < 2):
                    dve.wait_ge(up_ready[1], j - 1)
                dve.tensor_tensor(state_lo[:, s % 2, :], turned_ps[:, s % 2, 0:P], state_hi[:, s % 2, :].bitcast(F32),
                                  ALU.subtract).then_inc(state_ready[1], 1)

            def multiply_slot(j, s, first):
                dve.wait_ge(slot_silu, j + 1)
                if not (first and s < 2):
                    dve.wait_ge(act_turned[1], j - 1)
                dve.tensor_tensor(act_row[:, s % 2, :], silu_row[:, s % 2, :], up_ps[:, s % 2, HID:2 * HID],
                                  ALU.mult).then_inc(slot_act[1], 1)

            def slots1(it, first=False, last=False):
                for s in range(UNROLL):
                    j = it * UNROLL + s
                    multiply_slot(j, s, first)
                    if not (last and s >= UNROLL - 2):
                        split_turned(j + 2, s + 2, first)
                    if s >= DOWN_LAG[1]:
                        gate_result(1, it, s - DOWN_LAG[1])
                    elif not first:
                        gate_result(1, it - 1, UNROLL - DOWN_LAG[1] + s)

            def add_parts(n):
                dve.wait_ge(parts1_in[n], 16)
                link(dve.tensor_tensor(base[:, n, :], base[:, n, :], parts[:, n, 0, :], ALU.add))
                dve.tensor_tensor(base[:, n, :], base[:, n, :], parts[:, n, 1, :], ALU.add).then_inc(summed, 1)

            dve.memset(xpow[0:32, :], 1.0)
            for layer in range(2):
                dve.memset(choices[layer][:, :], 0.0)
                dve.memset(tables[layer][:, 0:TABLE_LEAD], 0)
            dve.wait_ge(cond_in, 3 * 16)
            link(dve.tensor_tensor(ypow[:, 1, :], ypow[:, 0, :], ypow[:, 0, :], ALU.mult))
            dve.tensor_tensor(xpow[64:96, :], xpow[64:96, :], xpow[64:96, :], ALU.mult)
            for c in range(3):
                link(dve.tensor_scalar(scond[:, c, :], ypow[:, 0, :], coef[:, 3 + c:4 + c], coef[:, c:c + 1], ALU.mult, ALU.add))
            for c in range(3):
                link(dve.scalar_tensor_tensor(out=scond[:, c, :], in0=ypow[:, 1, :], scalar=coef[:, 6 + c:7 + c],
                                              in1=scond[:, c, :], op0=ALU.mult, op1=ALU.add))
            dve.wait_ge(consts_in, 16)
            for g in range(3):
                ins = dve.tensor_copy(delta[32 * g:32 * g + 32, :], const_sb[32 * g:32 * g + 32, 32 * g:32 * g + 32])
            ins.then_inc(scond_ready, 1)
            for layer in range(2):
                size = tiles_of[layer] * TOPK
                dve.tensor_copy(ids[layer][:, :, :].rearrange("p t k -> p (t k)"), const["ids"][:, 0:size])
            dve.wait_ge(pcol_copied, 1)
            dve.tensor_copy(hT[:, step_col(STEPS - 1):step_col(STEPS - 1) + B], pcol[:, ROW_H0:ROW_H0 + B]).then_inc(h_done, 1)
            dve.tensor_scalar(wgate1[:, :], pcol[:, ROW_GATE:ROW_GATE + E], pcol[:, ROW_LNS:ROW_LNS + 1], None, ALU.mult)
            dve.tensor_scalar(lnb_tile[:, :], const["ones"], pcol[:, ROW_LNB:ROW_LNB + 1], None, ALU.mult).then_inc(pcol_ready, 1)
            for n in range(GROUP):
                condition(n)
            dve.wait_ge(small_in, 2 * 16)
            for g in range(NG):
                nexts = range(GROUP * (g + 1), min(GROUP * (g + 2), NB))
                for n in nexts[:1]:
                    factors(n)
                logits0(g)
                choose(0, g)
                for n in nexts[1:]:
                    factors(n)
                gates(0, g, g % 2)
                positions(0, g, g % 2)
                for n in nexts:
                    condition(n)
            find_ends(0)
            make_table(0)
            dve.wait_ge(gate1_ready, 1)
            dve.tensor_copy(gate_b1[:, :], gate1_ps[:, 0:E])
            dve.tensor_copy(wgate1c[:, :], gate1_ps[:, E:2 * E]).then_inc(gate1_taken, 1)
            dve.wait_ge(shared_cast, 1)
            dve.tensor_tensor(sw_lo[:, :], sw_raw[:, 0:2 * HID], sw_hi[:, :].bitcast(F32), ALU.subtract).then_inc(shared_split, 1)
            for e in range(E):
                dve.wait_ge(wgu_cast, e + 1)
                cols_e = slice(e * 2 * HID, (e + 1) * 2 * HID)
                dve.tensor_tensor(wgu_lo[:, cols_e], wgu[:, cols_e], wgu_hi[:, cols_e].bitcast(F32), ALU.subtract).then_inc(wgu_split, 1)
            dve.wait_ge(bias_in, 32)
            link.at(link.base + link.n)
            start, per = link.base, UNROLL
            dve.wait_ge(table_ready[0], 1)
            slots0(0, first=True)
            with dve.Fori(1, SLOTS // UNROLL - 1) as it:
                link.at(start + per * it - DOWN_LAG[0])
                slots0(it)
                assert link.n == per, link.n
            link.at(start + per * (SLOTS // UNROLL - 1) - DOWN_LAG[0])
            experts = slots0(SLOTS // UNROLL - 1, last=True)
            for s in range(UNROLL - DOWN_LAG[0], UNROLL):
                gate_result(0, SLOTS // UNROLL - 1, s, experts[s + DOWN_LAG[0]])
            sum_x1(0)
            stream_loop(stream_body)
            last_block(NB - 1, (NB - 1) % 2)
            split_turned(0, 0, True)
            split_turned(1, 1, True)
            slots1(0, first=True)
            with dve.Fori(1, SLOTS // UNROLL - 1) as it:
                slots1(it)
            slots1(SLOTS // UNROLL - 1, last=True)
            for s in range(UNROLL - DOWN_LAG[1], UNROLL):
                gate_result(1, SLOTS // UNROLL - 1, s)
            for n in range(NB):
                add_parts(n)

        @block.tensor
        def _(pe):
            def mm(dst, w, v, start=True, stop=True, **kw):
                return nc.tensor.matmul(dst, w, v, start=start, stop=stop, **kw)

            def turn(bank, tiles, ready):
                for t, tile in enumerate(tiles):
                    ins = nc.tensor.transpose(bank[:, t * P:(t + 1) * P], tile, ident)
                ins.then_inc(ready, 1)

            def turn_x(n):
                pe.wait_ge(x_in[n % 2], 16 * (n // 2 + 1))
                if n:
                    pe.wait_ge(x_copied, n)
                turn(turn_x_ps, [xin[:, n % 2, t * P:(t + 1) * P] for t in range(NT)], x_turned)

            def polynomial(n):
                for c in (2, 1, 0):
                    pe.wait_ge(sfac_ready, 3 * n + 3 - c)
                    k = 3 * n + 2 - c
                    if k >= len(poly_ps):
                        last, power = divmod(k - len(poly_ps), 3)
                        pe.wait_ge(*((z_ready, last + 1) if power == 2 else (poly_taken, 2 * last + power + 1)))
                    mm(poly_ps[k % len(poly_ps)], xpow[:, :], sfac[:, c, :]).then_inc(poly_ready, 1)

            def rows_and_logits(n):
                pe.wait_ge(z_ready, n + 1)
                if n:
                    pe.wait_ge(z_copied, n)
                turn(bank_c, [z[:, t * P:(t + 1) * P] for t in range(NT)], z_turned)
                if n and n % GROUP == 0:
                    pe.wait_ge(d_ready[0], n // GROUP)
                for t in range(NT):
                    at = (n % GROUP * NT + t) * E
                    ins = mm(logit_ps[:, at:at + E], z[:, t * P:(t + 1) * P], wgate0[:, :])
                ins.then_inc(logits_ready, 1)

            def ranks(layer, n, parts_of=(0, 1)):
                tiles = tiles_of[layer]
                dst = rank_ps[layer][:, 0:tiles * E]
                mask = rt["mask"][:, 0:tiles, :].rearrange("p t e -> p (t e)")
                if 0 in parts_of:
                    pe.wait_ge(chosen_ready[layer], n + 1)
                    if has(n, 1):
                        pe.wait_ge(rank_taken[layer], n)
                    if layer:
                        pe.wait_ge(x1_copied, min(n + 3, NB) if isinstance(n, int) else n + 3)
                    mm(dst, const["tri"], mask, stop=False, skip_group_check=True)
                    mm(dst.rearrange("p (t e) -> p t e", e=E), const["ones"], choices[layer][:, :].unsqueeze(1).to_broadcast([P, tiles, E]),
                       start=False, stop=False, skip_group_check=True)
                if 1 in parts_of:
                    for t in range(1, tiles):
                        ins = mm(dst[:, t * E:], const["ones"], mask[:, 0:(tiles - t) * E], start=False, stop=(t == tiles - 1), skip_group_check=True)
                    ins.then_inc(rank_ready[layer], 1)

            def count(layer):
                tiles = tiles_of[layer]
                for t in range(tiles):
                    mm(count_ps[layer], const["ones"], rt["mask"][:, t, :], start=(t == 0), stop=False, skip_group_check=True)
                mm(count_ps[layer], const["ones"], choices[layer][:, :], start=False, skip_group_check=True).then_inc(counted[layer], 1)

            def turn_rows(layer, it, s):
                it, s = (it, s) if s < UNROLL else (it + 1, s - UNROLL)
                j = it * UNROLL + s
                pe.wait_ge(rows_in[s], 16 * (layer * (SLOTS // UNROLL) + it + 1))
                if has(it, 1) or s >= 2:
                    pe.wait_ge(state_ready[layer], j - 1)
                nc.tensor.transpose(turned_ps[:, s % 2, 0:P], rows[:, s, 0:D], ident).then_inc(turned[layer], 1)

            def hidden_slot(j, s, e, first):
                pe.wait_ge(state_ready[0], j + 1)
                if not (first and s < 2):
                    pe.wait_ge(biased, j - 1)
                mm(up_ps[:, s % 2, 0:HID], state0[:, s % 2, :], w1[:, bass.ds(e * HID, HID)]).then_inc(up_ready[0], 1)

            def gate_and_up(j, s, e, first):
                pe.wait_ge(state_ready[1], j + 1)
                if not (first and s < 2):
                    pe.wait_ge(slot_act[1], j - 1)
                expert = bass.ds(e * 2 * HID, 2 * HID)
                mm(up_ps[:, s % 2, :], state_hi[:, s % 2, :], wgu_hi[:, expert], stop=False)
                mm(up_ps[:, s % 2, :], state_hi[:, s % 2, :], wgu_lo[:, expert], start=False, stop=False)
                mm(up_ps[:, s % 2, :], state_lo[:, s % 2, :], wgu_hi[:, expert], start=False).then_inc(up_ready[1], 1)

            def turn_act(layer, j, s, first):
                pe.wait_ge(slot_act[layer], j + 1)
                if not (first and s < 2):
                    pe.wait_ge(act_copied[layer], j - 1)
                turn(act_turned_ps[:, s % 2, :], [act_row[:, s % 2, c * P:(c + 1) * P] for c in range(NC)], act_turned[layer])

            def slot_down(layer, j, s, e, first):
                pe.wait_ge(act_copied[layer], j + 1)
                if not (first and s < 2):
                    pe.wait_ge(y_ready[layer], j - 1)
                w = (w2, wd)[layer]
                for c in range(NC):
                    ins = mm(result_ps[:, s % 2, 0:D], act_col[:, s % 2, c * P:(c + 1) * P],
                             w[:, bass.ds(e * HID + c * P, P)], start=(c == 0), stop=(c == NC - 1))
                ins.then_inc(result_ready[layer], 1)

            def slots(layer, it, first=False, last=False):
                lag = DOWN_LAG[layer]
                experts = table_values(pe, layer, it * UNROLL + TABLE_LEAD - lag, UNROLL + lag, E - 1)
                for s in range(UNROLL):
                    j = it * UNROLL + s
                    if not (last and s >= UNROLL - 2):
                        turn_rows(layer, it, s + 2)
                    (gate_and_up if layer else hidden_slot)(j, s, experts[s + lag], first)
                    if not (first and s < lag - 1):
                        turn_act(layer, j - lag + 1, (s - lag + 1) % UNROLL, first)
                    if not (first and s < lag):
                        slot_down(layer, j - lag, (s - lag) % UNROLL, experts[s], first)
                return experts

            def all_slots(layer):
                turn_rows(layer, 0, 0)
                turn_rows(layer, 0, 1)
                slots(layer, 0, first=True)
                with pe.Fori(1, SLOTS // UNROLL - 1) as it:
                    slots(layer, it)
                experts = slots(layer, SLOTS // UNROLL - 1, last=True)
                lag = DOWN_LAG[layer]
                for s in range(UNROLL - lag, UNROLL):
                    if s > UNROLL - lag:
                        turn_act(layer, SLOTS - UNROLL + s, s, False)
                    slot_down(layer, SLOTS - UNROLL + s, s, experts[s + lag], False)

            def turn_back(n):
                pe.wait_ge(x1_ready, n + 1)
                if has(n, 1):
                    pe.wait_ge(x1_copied, n)
                if has(n, 3):
                    pe.wait_ge(rank_taken[1], n - 2)
                turn(bank_c, [x1r[:, t * P:(t + 1) * P] for t in range(NT)], x1_turned)

            def rnn_input(n, p, k):
                if k == 0:
                    pe.wait_ge(x1_copied, n + 1)
                    if has(n, 2):
                        pe.wait_ge(h_done, STEPS * (n - 1) + 1)
                cols = slice(k * BLK // 2, (k + 1) * BLK // 2)
                mm(rnn_ps[:, p, cols], wx[:, :], x1T[:, cols], start=(k == 0), stop=False, skip_group_check=True)

            def rnn_step(n, p, s):
                pe.wait_ge(h_done, STEPS * n + s + 1)
                prev = hT[:, hcols(n, step_col(s - 1), B)] if s else hT[:, hcols(n - 1, step_col(STEPS - 1), B)]
                mm(rnn_ps[:, p, step_col(s):step_col(s) + B], wh[:, :], prev, start=False, stop=True,
                   skip_group_check=True).then_inc(rnn_ready, 1)

            def state_rows(n):
                pe.wait_ge(state_copied, n + 1)
                if has(n, 1):
                    pe.wait_ge(b_free, b_use(n))
                turn(bank_b, [state_tile[:, t * P:(t + 1) * P] for t in range(NT)], b_ready)

            def logits1(n, tiles):
                if tiles[0] == 0:
                    pe.wait_ge(b_free, b_use(n) + 1)
                for t in tiles:
                    ins = mm(bank_b[:, t * E:(t + 1) * E], state_tile[:, t * P:(t + 1) * P], wgate1c[:, :])
                if tiles[-1] == NT - 1:
                    ins.then_inc(b_ready, 1)

            def pair(n, p, c, part):
                w = NC * n + c
                pe.wait_ge(q_split, n + 1)
                if has(n, 1) or c:
                    pe.wait_ge((silu_done, prod_done)[part], w)
                dst = pair_ps[:, part, :]
                mm(dst, shared(sw_hi, part, c), in_hi[:, half(p)], stop=False)
                mm(dst, shared(sw_hi, part, c), in_lo[:, half(p)], start=False, stop=False)
                ins = mm(dst, shared(sw_lo, part, c), in_hi[:, half(p)], start=False)
                if part:
                    ins.then_inc(pair_ready, 1)

            def down1(n, p, c, tiles):
                w = NC * n + c
                if c == 0 and tiles[0] == 0 and has(n, 2):
                    pe.wait_ge(base_done, n - 1)
                pe.wait_ge(prod_done, w + 1)
                for t in tiles:
                    tile = slice(t * P, (t + 1) * P)
                    ins = mm(acc[:, p, tile], gated[:, c, tile], shared(sw_raw, 2, c), start=(c == 0 and t == 0),
                             stop=(c == NC - 1), skip_group_check=True)
                if tiles[-1] == NT - 1:
                    ins.then_inc(down1_done, 1)

            def keep_warm(units=0):
                if units > 0:
                    pe.wait_ge(silu_done, units)
                mm(pair_ps[:, 0, :], sw_hi[:, 0:P], sw_hi[:, :])

            def stream_body(i, p):
                before, ahead = i > 0, i + 1 < NB
                for s in range(STEPS):
                    rnn_step(i, p, s)
                    for _ in range(FILL[i].get(s, 0)):
                        keep_warm(NC * (i - 1) + sum(s > at for at in SILU_AT))
                    if i >= 2 and s in RANKS_AT:
                        ranks(1, i - 2, (RANKS_AT.index(s),))
                    if not ahead and s in LAST_RANKS_AT:
                        ranks(1, i - 1, (LAST_RANKS_AT.index(s),))
                    if before:
                        if s == ROWS_AT:
                            state_rows(i - 1)
                        if s in LOGIT1_AT:
                            k = LOGIT1_AT.index(s)
                            logits1(i - 1, (2 * k, 2 * k + 1))
                        for c in range(NC):
                            if s in PAIR_AT[c]:
                                pair(i - 1, 1 - p, c, PAIR_AT[c].index(s))
                            if s in DOWN_AT[c]:
                                k = DOWN_AT[c].index(s)
                                down1(i - 1, 1 - p, c, (2 * k, 2 * k + 1))
                    if ahead:
                        if s == TURN_X1_AT:
                            turn_back(i + 1)
                        if s in XP_AT:
                            rnn_input(i + 1, 1 - p, XP_AT.index(s))

            def last_block(n, p):
                state_rows(n)
                pair(n, p, 0, 0)
                logits1(n, range(NT))
                pair(n, p, 0, 1)
                for _ in range(ROUTER_FILL):
                    keep_warm(NC * n + 1)
                ranks(1, n)
                count(1)
                for part in range(2):
                    pair(n, p, 1, part)
                for c in range(NC):
                    down1(n, p, c, range(NT))

            pe.wait_ge(consts_in, 16)
            turn_x(0)
            pe.wait_ge(params_in, 5 * 16)
            nc.tensor.transpose(param_ps[:, 0:P], prow[:, :], ident).then_inc(params_turned, 1)
            turn_x(1)
            polynomial(0)
            polynomial(1)
            pe.wait_ge(pcol_copied, 1)
            pe.wait_ge(small_in, 2 * 16)
            rows_and_logits(0)
            rows_and_logits(1)
            for g in range(NG):
                nexts = range(GROUP * (g + 1), min(GROUP * (g + 2), NB))
                for n in nexts[:1]:
                    turn_x(n)
                    polynomial(n)
                ranks(0, g)
                for n in nexts[1:]:
                    turn_x(n)
                    polynomial(n)
                for n in nexts:
                    rows_and_logits(n)
            count(0)
            pe.wait_ge(pcol_ready, 1)
            mm(gate1_ps[:, 0:E], lnb_tile[:, :], pcol[:, ROW_GATE:ROW_GATE + E])
            mm(gate1_ps[:, E:2 * E], const["center"], wgate1[:, :]).then_inc(gate1_ready, 1)
            pe.wait_ge(rank_taken[0], NG)
            pe.wait_ge(table_ready[0], 1)
            pe.wait_ge(w1_in, 16)
            pe.wait_ge(w2_in, 32)
            pe.wait_ge(shared_split, 1)
            pe.wait_ge(nearly_sent[0], 1)
            for _ in range(GAP_FILL[0]):
                keep_warm()
            all_slots(0)
            pe.wait_ge(y_ready[0], SLOTS)
            pe.wait_ge(rnn_w_in, 32)
            pe.wait_ge(shared_in, 48)
            pe.wait_ge(shared_split, 1)
            pe.wait_ge(gate1_taken, 1)
            for landed in results_out[0]:
                pe.wait_ge(landed, 16 * SLOTS // OUT_RING)
            for _ in range(GAP_FILL[1]):
                keep_warm()
            turn_back(0)
            for k in range(2):
                rnn_input(0, 0, k)
            stream_loop(stream_body)
            last_block(NB - 1, (NB - 1) % 2)
            pe.wait_ge(b_free, b_use(NB))
            pe.wait_ge(rank_taken[1], NB)
            pe.wait_ge(base_done, NB)
            pe.wait_ge(table_ready[1], 1)
            pe.wait_ge(wgu_split, E)
            pe.wait_ge(wd_in, 32)
            pe.wait_ge(nearly_sent[1], 1)
            for _ in range(GAP_FILL[2]):
                keep_warm()
            all_slots(1)


INPUTS = ("x", "fside_BxS_0", "cond_1024", "L0_cond_coeffs", "L0_ffn_Wg", "L0_ffn_bg", "L0_ffn_W1", "L0_ffn_b1",
          "L0_ffn_W2", "L0_ffn_b2", "L1_cond_Wx", "L1_cond_Wh", "L1_cond_b", "L1_ffn_ln_scale", "L1_ffn_ln_bias",
          "L1_ffn_gate_w", "L1_ffn_Wg", "L1_ffn_Wu", "L1_ffn_Wd", "L1_ffn_sWg", "L1_ffn_sWu", "L1_ffn_sWd")


def kernel(**inputs):
    import numpy as np
    import concourse.bacc as bacc
    from concourse.bass_utils import run_bass_kernel_spmd

    nc = bacc.Bacc("TRN2", target_bir_lowering=False, num_devices=1)
    arrays, args = {}, []
    for name, a in [("consts", constant_tables())] + [(n, np.ascontiguousarray(inputs[n])) for n in INPUTS]:
        arrays[f"in_{name}"] = a
        args.append(nc.dram_tensor(f"in_{name}", a.shape, mybir.dt.from_np(a.dtype), kind="ExternalInput").ap())
    out = nc.dram_tensor("out", (B, T, D), F32, kind="ExternalOutput").ap()
    build(nc, *args, out)
    result = run_bass_kernel_spmd(nc, [arrays], core_ids=[0])
    return result.results[0]["out"]
```
